# Optimizing a Trainium2 kernel written in Bass

```python
import numpy as np
import jax
import jax.numpy as jnp

def _softmax(x, axis=-1):
    return jax.nn.softmax(x, axis=axis)

def _gelu(x):
    return jax.nn.gelu(x, approximate=True)

def _silu(x):
    return jax.nn.silu(x)

def _sigmoid(x):
    return jax.nn.sigmoid(x)

def _layernorm(x, axis=-1, eps=1e-05):
    m = jnp.mean(x, axis=axis, keepdims=True)
    v = jnp.var(x, axis=axis, keepdims=True)
    return (x - m) / jnp.sqrt(v + eps)

def _scatter_add(tgt, idx, src, axis=0):
    return tgt.at[idx].add(src)

def _segment_sum(src, seg, n):
    return jax.ops.segment_sum(src, seg, n)
kernel_name = 'mk_adaln_d2_jaxref_r8_f1f854'

def setup_inputs(seed: int=0):
    np.random.seed(seed)
    _w = jnp.asarray

    def _L0_attn_setup():
        import jax, jax.numpy as jnp
        import numpy as np
        HIDDEN = 512
        NUM_HEADS = 32
        HEAD_DIM = HIDDEN // NUM_HEADS

        def _fp8_roundtrip(x):
            return x.astype(jnp.float8_e4m3fn).astype(jnp.float32)
        key = jax.random.key(seed)
        ks = jax.random.split(key, 10)
        B, S = (2, 512)
        hidden_states = jax.random.normal(ks[0], (B, S, HIDDEN), dtype=jnp.float32)
        scale = 0.02

        def lin(kw, kb):
            w = jax.random.normal(kw, (HIDDEN, HIDDEN), dtype=jnp.float32) * scale
            b = jax.random.normal(kb, (HIDDEN,), dtype=jnp.float32) * scale
            return (w, b)
        wq, bq = lin(ks[1], ks[2])
        wk, bk = lin(ks[3], ks[4])
        wv, bv = lin(ks[5], ks[6])
        wl, bl = lin(ks[7], ks[8])
        wq, bq = (_fp8_roundtrip(wq), _fp8_roundtrip(bq))
        wk, bk = (_fp8_roundtrip(wk), _fp8_roundtrip(bk))
        wv, bv = (_fp8_roundtrip(wv), _fp8_roundtrip(bv))
        return {'hidden_states': hidden_states, 'wq': wq, 'bq': bq, 'wk': wk, 'bk': bk, 'wv': wv, 'bv': bv, 'wl': wl, 'bl': bl}
    _L0_attn_in = _L0_attn_setup()

    def _L0_ffn_setup():
        import jax, jax.numpy as jnp
        import numpy as np
        TOP_K = 2
        SCALING = 32.0 / 64.0
        key = jax.random.key(seed)
        ks = jax.random.split(key, 6)
        Bsz, S, Din, Dout, R, E = (4, 256, 512, 512, 64, 16)
        x = jax.random.normal(ks[0], (Bsz, S, Din), dtype=jnp.float32)
        base_w = jax.random.normal(ks[1], (Dout, Din), dtype=jnp.float32) * 0.02
        base_b = jax.random.normal(ks[2], (Dout,), dtype=jnp.float32) * 0.02
        A = jax.random.normal(ks[3], (R, Din), dtype=jnp.float32) * (1.0 / np.sqrt(Din))
        B = jax.random.normal(ks[4], (E, Dout, R), dtype=jnp.float32) * 0.02
        router_w = jax.random.normal(ks[5], (E, Din), dtype=jnp.float32) * 0.02
        return {'x': x, 'base_w': base_w, 'base_b': base_b, 'A': A, 'B': B, 'router_w': router_w}
    _L0_ffn_in = _L0_ffn_setup()
    _L0_c = _w((lambda *s: np.random.randn(*s).astype(np.float32) * 0.05)(2, 512))
    _L0_wmod = _w((lambda *s: np.random.randn(*s).astype(np.float32) * 0.05)(512, 6 * 512) * 512 ** (-0.5))

    def _L1_attn_setup():
        import jax, jax.numpy as jnp
        import numpy as np
        H = 512
        NH = 32
        QR = 192
        KVR = 64
        RD = 64
        ND = 128
        VD = 128
        QK = RD + ND
        EPS = 1e-06
        THETA = 10000.0
        B, S = (2, 128)

        def rmsnorm(x, w):
            norm = jnp.sqrt(jnp.sum(x * x, axis=-1, keepdims=True)) * x.shape[-1] ** (-0.5)
            return x / (norm + EPS) * w

        def rope_cos_sin(seq_len):
            inv_freq = 1.0 / THETA ** (jnp.arange(0, RD, 2, dtype=jnp.float32) / RD)
            t = jnp.arange(seq_len, dtype=jnp.float32)
            freqs = jnp.outer(t, inv_freq)
            emb = jnp.concatenate([freqs, freqs], -1)
            return (jnp.cos(emb), jnpp_cos_sin_dummy() if False else jnp.sin(emb))

        def rotate_half(x):
            x1, x2 = jnp.split(x, 2, axis=-1)
            return jnp.concatenate([-x2, x1], axis=-1)
        key = jax.random.key(seed)
        ks = jax.random.split(key, 8)
        sc = 0.02
        return {'hidden_states': jax.random.normal(ks[0], (B, S, H), jnp.float32), 'w_qa': jax.random.normal(ks[1], (H, QR), jnp.float32) * sc, 'g_qa': jnp.ones((QR,), jnp.float32), 'w_qb': jax.random.normal(ks[2], (QR, NH * QK), jnp.float32) * sc, 'w_kva': jax.random.normal(ks[3], (H, KVR + RD), jnp.float32) * sc, 'g_kva': jnp.ones((KVR,), jnp.float32), 'w_kvb': jax.random.normal(ks[4], (KVR, NH * (ND + VD)), jnp.float32) * sc, 'w_o': jax.random.normal(ks[5], (NH * VD, H), jnp.float32) * sc}
    _L1_attn_in = _L1_attn_setup()

    def _L1_ffn_setup():
        import jax, jax.numpy as jnp
        import numpy as np
        B, S, DIN, DOUT, R = (2, 256, 512, 512, 32)
        key = jax.random.key(seed)
        k1, k2, k3, k4, k5 = jax.random.split(key, 5)
        std = 1.0 / np.sqrt(R)
        return {'x': jax.random.normal(k1, (B, S, DIN), dtype=jnp.float32), 'W': jax.random.normal(k2, (DOUT, DIN), dtype=jnp.float32) * 0.02, 'lora_A': jax.random.normal(k3, (R, DIN), dtype=jnp.float32) * std, 'lora_B': jax.random.normal(k4, (DOUT, R), dtype=jnp.float32) * 0.01, 'magnitude': jax.random.uniform(k5, (DOUT,), dtype=jnp.float32) + 0.5}
    _L1_ffn_in = _L1_ffn_setup()
    _L1_c = _w((lambda *s: np.random.randn(*s).astype(np.float32) * 0.05)(2, 512))
    _L1_wmod = _w((lambda *s: np.random.randn(*s).astype(np.float32) * 0.05)(512, 6 * 512) * 512 ** (-0.5))
    _d = {'L0_attn_hidden_states': _L0_attn_in['hidden_states'], 'L0_attn_wq': _L0_attn_in['wq'], 'L0_attn_bq': _L0_attn_in['bq'], 'L0_attn_wk': _L0_attn_in['wk'], 'L0_attn_bk': _L0_attn_in['bk'], 'L0_attn_wv': _L0_attn_in['wv'], 'L0_attn_bv': _L0_attn_in['bv'], 'L0_attn_wl': _L0_attn_in['wl'], 'L0_attn_bl': _L0_attn_in['bl'], 'L0_ffn_base_w': _L0_ffn_in['base_w'], 'L0_ffn_base_b': _L0_ffn_in['base_b'], 'L0_ffn_A': _L0_ffn_in['A'], 'L0_ffn_B': _L0_ffn_in['B'], 'L0_ffn_router_w': _L0_ffn_in['router_w'], 'L0_c': _L0_c, 'L0_wmod': _L0_wmod, 'L1_attn_w_qa': _L1_attn_in['w_qa'], 'L1_attn_g_qa': _L1_attn_in['g_qa'], 'L1_attn_w_qb': _L1_attn_in['w_qb'], 'L1_attn_w_kva': _L1_attn_in['w_kva'], 'L1_attn_g_kva': _L1_attn_in['g_kva'], 'L1_attn_w_kvb': _L1_attn_in['w_kvb'], 'L1_attn_w_o': _L1_attn_in['w_o'], 'L1_ffn_W': _L1_ffn_in['W'], 'L1_ffn_lora_A': _L1_ffn_in['lora_A'], 'L1_ffn_lora_B': _L1_ffn_in['lora_B'], 'L1_ffn_magnitude': _L1_ffn_in['magnitude'], 'L1_c': _L1_c, 'L1_wmod': _L1_wmod}
    _x0 = _d['L0_attn_hidden_states']
    _d['L0_attn_hidden_states'] = jax.random.normal(jax.random.fold_in(jax.random.key(seed), 1), (2, 512, 512), dtype=_x0.dtype)
    del _x0
    return _d

def reference(L0_attn_hidden_states, L0_attn_wq, L0_attn_bq, L0_attn_wk, L0_attn_bk, L0_attn_wv, L0_attn_bv, L0_attn_wl, L0_attn_bl, L0_ffn_base_w, L0_ffn_base_b, L0_ffn_A, L0_ffn_B, L0_ffn_router_w, L0_c, L0_wmod, L1_attn_w_qa, L1_attn_g_qa, L1_attn_w_qb, L1_attn_w_kva, L1_attn_g_kva, L1_attn_w_kvb, L1_attn_w_o, L1_ffn_W, L1_ffn_lora_A, L1_ffn_lora_B, L1_ffn_magnitude, L1_c, L1_wmod):

    def _L0_attn_ref(hidden_states, wq, bq, wk, bk, wv, bv, wl, bl):
        import jax, jax.numpy as jnp
        import numpy as np
        HIDDEN = 512
        NUM_HEADS = 32
        HEAD_DIM = HIDDEN // NUM_HEADS

        def _fp8_roundtrip(x):
            return x.astype(jnp.float8_e4m3fn).astype(jnp.float32)
        B, S, E = hidden_states.shape
        H, D = (NUM_HEADS, HEAD_DIM)
        q = (hidden_states @ wq.T + bq).reshape(B, S, H, D)
        k = (hidden_states @ wk.T + bk).reshape(B, S, H, D)
        v = (hidden_states @ wv.T + bv).reshape(B, S, H, D)
        latent = hidden_states @ wl.T + bl
        scores = jnp.einsum('bshd,bstd->bsht', q, k) / np.sqrt(D).astype(np.float32)
        probs = jax.nn.softmax(scores, axis=-1)
        context = jnp.einsum('bsht,bstd->bshd', probs, v).reshape(B, S, E)
        return context

    def _L0_ffn_ref(x, base_w, base_b, A, B, router_w):
        import jax, jax.numpy as jnp
        import numpy as np
        TOP_K = 2
        SCALING = 32.0 / 64.0
        base_out = jnp.einsum('bsi,oi->bso', x, base_w) + base_b
        res_hidden = jnp.einsum('bsi,ri->bsr', x, A)
        logits = jnp.einsum('bsi,ei->bse', x, router_w)
        probs = jax.nn.softmax(logits, axis=-1)
        topw, topi = jax.lax.top_k(probs, TOP_K)
        topw = topw / (jnp.sum(topw, axis=-1, keepdims=True) + 1e-06)
        num_experts = B.shape[0]
        combine = jnp.sum(jax.nn.one_hot(topi, num_experts, dtype=x.dtype) * topw[..., None], axis=-2)
        delta = jnp.einsum('bse,bsr,eor->bso', combine, res_hidden, B)
        return base_out + delta * SCALING

    def _L1_attn_ref(hidden_states, w_qa, g_qa, w_qb, w_kva, g_kva, w_kvb, w_o):
        import jax, jax.numpy as jnp
        import numpy as np
        H = 512
        NH = 32
        QR = 192
        KVR = 64
        RD = 64
        ND = 128
        VD = 128
        QK = RD + ND
        EPS = 1e-06
        THETA = 10000.0
        B, S = (2, 128)

        def rmsnorm(x, w):
            norm = jnp.sqrt(jnp.sum(x * x, axis=-1, keepdims=True)) * x.shape[-1] ** (-0.5)
            return x / (norm + EPS) * w

        def rope_cos_sin(seq_len):
            inv_freq = 1.0 / THETA ** (jnp.arange(0, RD, 2, dtype=jnp.float32) / RD)
            t = jnp.arange(seq_len, dtype=jnp.float32)
            freqs = jnp.outer(t, inv_freq)
            emb = jnp.concatenate([freqs, freqs], -1)
            return (jnp.cos(emb), jnpp_cos_sin_dummy() if False else jnp.sin(emb))

        def rotate_half(x):
            x1, x2 = jnp.split(x, 2, axis=-1)
            return jnp.concatenate([-x2, x1], axis=-1)
        b, s, _ = hidden_states.shape
        q_c = rmsnorm(hidden_states @ w_qa, g_qa)
        q = (q_c @ w_qb).reshape(b, s, NH, QK).transpose(0, 2, 1, 3)
        q_nope, q_rope = (q[..., :ND], q[..., ND:])
        kv = hidden_states @ w_kva
        k_c, k_rope = (kv[..., :KVR], kv[..., KVR:])
        k_c = rmsnorm(k_c, g_kva)
        kst = (k_c @ w_kvb).reshape(b, s, NH, ND + VD).transpose(0, 2, 1, 3)
        k_nope, v = (kst[..., :ND], kst[..., ND:])
        inv_freq = 1.0 / THETA ** (jnp.arange(0, RD, 2, dtype=jnp.float32) / RD)
        freqs = jnp.outer(jnp.arange(s, dtype=jnp.float32), inv_freq)
        emb = jnp.concatenate([freqs, freqs], -1)
        cos = jnp.cos(emb)[None, None]
        sin = jnp.sin(emb)[None, None]
        k_rope = k_rope[:, None]
        q_rope = q_rope * cos + rotate_half(q_rope) * sin
        k_rope = k_rope * cos + rotate_half(k_rope) * sin
        k_rope = jnp.broadcast_to(k_rope, (b, NH, s, RD))
        query = jnp.concatenate([q_nope, q_rope], -1)
        key_s = jnp.concatenate([k_nope, k_rope], -1)
        scaling = QK ** (-0.5)
        scores = jnp.einsum('bhqd,bhkd->bhqk', query, key_s) * scaling
        attn = jax.nn.softmax(scores, axis=-1)
        out = jnp.einsum('bhqk,bhkd->bhqd', attn, v)
        out = out.transpose(0, 2, 1, 3).reshape(b, s, NH * VD)
        return out @ w_o

    def _L1_ffn_ref(x, W, lora_A, lora_B, magnitude):
        import jax, jax.numpy as jnp
        import numpy as np
        B, S, DIN, DOUT, R = (2, 256, 512, 512, 32)
        base = jnp.einsum('bsi,oi->bso', x, W)
        lora = jnp.einsum('bsr,or->bso', jnp.einsum('bsi,ri->bsr', x, lora_A), lora_B)
        eff_W = W + lora_B @ lora_A
        column_norm = jax.lax.stop_gradient(jnp.sqrt(jnp.sum(eff_W * eff_W, axis=1)))
        result = (base + lora) / column_norm[None, None, :]
        return result * magnitude[None, None, :]
    x = L0_attn_hidden_states
    mod = (_silu(L0_c) @ L0_wmod).reshape(L0_c.shape[0], 6, 1, -1)
    sa, ca, ga, sb, cb, gb = (mod[:, 0], mod[:, 1], mod[:, 2], mod[:, 3], mod[:, 4], mod[:, 5])
    ga = (2 * (ga >= 0) - 1) * jnp.maximum(jnp.abs(ga), 0.25)
    gb = (2 * (gb >= 0) - 1) * jnp.maximum(jnp.abs(gb), 0.25)
    h = _layernorm(x, axis=-1) * (1 + ca) + sa
    x = x + ga * _L0_attn_ref(h, L0_attn_wq, L0_attn_bq, L0_attn_wk, L0_attn_bk, L0_attn_wv, L0_attn_bv, L0_attn_wl, L0_attn_bl)
    h = _layernorm(x, axis=-1) * (1 + cb) + sb
    x = x + gb * _L0_ffn_ref(h, L0_ffn_base_w, L0_ffn_base_b, L0_ffn_A, L0_ffn_B, L0_ffn_router_w)
    mod = (_silu(L1_c) @ L1_wmod).reshape(L1_c.shape[0], 6, 1, -1)
    sa, ca, ga, sb, cb, gb = (mod[:, 0], mod[:, 1], mod[:, 2], mod[:, 3], mod[:, 4], mod[:, 5])
    ga = (2 * (ga >= 0) - 1) * jnp.maximum(jnp.abs(ga), 0.25)
    gb = (2 * (gb >= 0) - 1) * jnp.maximum(jnp.abs(gb), 0.25)
    h = _layernorm(x, axis=-1) * (1 + ca) + sa
    x = x + ga * _L1_attn_ref(h, L1_attn_w_qa, L1_attn_g_qa, L1_attn_w_qb, L1_attn_w_kva, L1_attn_g_kva, L1_attn_w_kvb, L1_attn_w_o)
    h = _layernorm(x, axis=-1) * (1 + cb) + sb
    x = x + gb * _L1_ffn_ref(h, L1_ffn_W, L1_ffn_lora_A, L1_ffn_lora_B, L1_ffn_magnitude)
    return x

_drawn_inputs = setup_inputs


def setup_inputs(seed=0):
    import zlib

    import numpy as np

    out = dict(_drawn_inputs(seed))
    spreads = {'L1_attn_g_qa': (1.0, 0.6), 'L1_attn_g_kva': (1.0, 0.6)}
    factors = {'L0_attn_wq': 8.0,
     'L0_attn_bq': 8.0,
     'L0_attn_wk': 8.0,
     'L0_attn_bk': 8.0,
     'L0_attn_wv': 2.757,
     'L0_attn_bv': 8.0,
     'L0_ffn_base_b': 8.0,
     'L0_ffn_A': 4.048,
     'L0_ffn_B': 4.065,
     'L0_ffn_router_w': 4.3,
     'L1_attn_w_qa': 8.0,
     'L1_attn_w_qb': 8.0,
     'L1_attn_w_kva': 8.0,
     'L1_attn_w_kvb': 8.0,
     'L1_attn_w_o': 8.0,
     'L1_ffn_magnitude': 2.751}
    for name, (base, spread) in spreads.items():
        noise = np.random.default_rng([zlib.crc32(name.encode()), seed]).standard_normal(out[name].shape)
        drawn = base * np.exp(spread * noise) if base else spread * noise
        out[name] = jnp.asarray(drawn.astype(out[name].dtype))
    for name, factor in factors.items():
        out[name] = (out[name] * factor).astype(out[name].dtype)
    return out
```

```python
from contextlib import ExitStack

import concourse.bass as bass
from concourse import mybir

P = 128
F32 = mybir.dt.float32
F32R = mybir.dt.float32r
U32 = mybir.dt.uint32
ALU = mybir.AluOpType
ACT = mybir.ActivationFunctionType
AX = mybir.AxisListType

B, S, D = 2, 512, 512
TOK = B * S
TILES = TOK // P
TPB = S // P
KC = D // P
QD = P // 32

H0, HD0 = 32, 16
PAD0 = 32
VW = HD0 + 1

R0, E0 = 64, 16
PROJ0 = D + R0 + E0
EC = E0 * R0 // P
LORA_SCALE = 32.0 / 64.0

NH, QR, KVR, RD, ND, VD = 32, 192, 64, 64, 128, 128
QREST = QR - P
CQ = QR + KVR + RD
HP = NH // 2
SCALE1 = float(ND + RD) ** -0.5
CW = KVR + 1

R1 = 32
LN_EPS = 1e-5
RMS_EPS = 1e-6
SIX = 6 * KC
SA, CA, GA, SB, CB, GB = (j * KC for j in range(6))


def bc(ap, shape):
    return ap.to_broadcast(shape)


class Chain:

    def __init__(self, eng, sem):
        self.eng, self.sem, self.n = eng, sem, 0

    def __call__(self, ins):
        self.n += 1
        ins.then_inc(self.sem, 1)
        self.eng.wait_ge(self.sem, self.n)


def split_matmuls(pe, out, pairs, first=True, last=True):
    n = len(pairs)
    for i, ((xh, xl), (wh, wl)) in enumerate(pairs):
        pe.matmul(out, xh, wh, start=first and i == 0, stop=False)
        pe.matmul(out, xh, wl, start=False, stop=False)
        mm = pe.matmul(out, xl, wh, start=False, stop=last and i == n - 1)
    return mm


def megakernel(nc, a, out, stop_after=9):
    x_dram = a["x"].rearrange("(t p) d -> p t d", p=P)
    out_dram = out.rearrange("(t p) d -> p t d", p=P)

    with ExitStack() as whole:
        def sb(name, shape, dt=F32, ctx=whole):
            return ctx.enter_context(nc.sbuf_tensor(name, shape, dt))

        def sem(name):
            return whole.enter_context(nc.semaphore(name))

        bank = [whole.enter_context(nc.psum_tensor(f"bank{i}", [P, 512], F32)) for i in range(8)]

        x = sb("x_res", [P, TILES, D])
        ident = sb("ident", [P, P])
        ones = sb("ones", [P, P])
        eps = sb("eps", [P, 1])
        cs = sb("cs", [P, 2 * KC * B])
        cs_e = sb("cs_e", [P, 2 * KC * B])
        cs_s = sb("cs_s", [P, 2 * KC * B])
        mod = sb("mod", [P, SIX * B])
        gabs = sb("gabs", [P, 4 * KC * B])
        gate = sb("gate", [P, 2, B, D])
        stats = sb("stats", [P, TILES, 6])
        mv = sb("mv", [P, TILES, 2])
        rstd = sb("rstd", [P, TILES])
        mod3 = mod[:, :].rearrange("p (m b) -> p m b", b=B)
        cs4 = cs_s[:, :].rearrange("p (l k b) -> p l k b", l=2, b=B)

        x_in = sem("x_in")
        const_in = sem("const_in")
        wmod_in = [sem(f"wmod_in{j}") for j in range(6)]
        raw_in = [sem("raw_in0"), sem("raw_in1")]
        raw_free = sem("raw_free")
        stored = sem("stored")

        def load_chunks(sp, stage, chunks, base):
            for i, src in enumerate(chunks):
                n = base + i
                if n >= 2:
                    sp.wait_ge(raw_free, n - 1)
                w = 1
                for s in src.shape[1:]:
                    w *= s
                dst = stage[:, n % 2, 0:w]
                if len(src.shape) == 3:
                    dst = dst.rearrange("p (a b) -> p a b", a=src.shape[1])
                sp.dma_start(dst, src).then_inc(raw_in[n % 2], 16)

        split_hi = sem("split_hi")

        def split_act(act, stage, chunks, base):
            for i, (hi, lo) in enumerate(chunks):
                n = base + i
                w = hi.shape[-1]
                act.wait_ge(raw_in[n % 2], 16 * (n // 2 + 1))
                act.activation(hi, stage[:, n % 2, 0:w], ACT.Copy).then_inc(split_hi, 1)

        def split_dve(dve, stage, chunks, base):
            for i, (hi, lo) in enumerate(chunks):
                n = base + i
                w = hi.shape[-1]
                dve.wait_ge(split_hi, n + 1)
                dve.tensor_tensor(lo, stage[:, n % 2, 0:w], hi.bitcast(F32), ALU.subtract).then_inc(raw_free, 1)

        class Norm:

            def __init__(self, tag, shift, scale, used, ctx):
                self.x = sb(f"{tag}_x", [P, 2, D], F32, ctx)
                self.f = sb(f"{tag}_f", [P, KC, P], F32, ctx)
                self.h_hi = sb(f"{tag}_h_hi", [P, 2, KC, P], F32R, ctx)
                self.h_lo = sb(f"{tag}_h_lo", [P, 2, KC, P], F32R, ctx)
                self.shift, self.scale = shift, scale
                self.chain = sem(f"{tag}_chain")
                self.var = sem(f"{tag}_var")
                self.std = sem(f"{tag}_std")
                self.rstd = sem(f"{tag}_rstd")
                self.xn = sem(f"{tag}_xn")
                self.xT = sem(f"{tag}_xT")
                self.hf = sem(f"{tag}_hf")
                self.hi = sem(f"{tag}_hi")
                self.lo = sem(f"{tag}_lo")
                self.used = used

            def dve_stats(self, dve):
                for t in range(TILES):
                    dve.bn_stats(stats[:, t, :], x[:, t, :]).then_inc(self.chain, 1)
                for t in range(TILES):
                    dve.wait_ge(self.chain, t + 1)
                    dve.bn_aggr(mv[:, t, :], stats[:, t, :]).then_inc(self.var, 1)
                dve.wait_ge(self.std, 1)
                dve.reciprocal(rstd[:, :], rstd[:, :]).then_inc(self.rstd, 1)

            def act_std(self, act):
                act.wait_ge(self.var, TILES)
                act.activation(rstd[:, :], mv[:, :, 1], ACT.Sqrt, bias=eps[:, 0:1]).then_inc(self.std, 1)

            def dve_xn(self, dve, t):
                if t == 0:
                    dve.wait_ge(self.rstd, 1)
                if t >= 2:
                    dve.wait_ge(self.xT, t - 1)
                dve.tensor_scalar(self.x[:, t % 2, :], x[:, t, :], mv[:, t, 0:1], rstd[:, t:t + 1],
                                  ALU.subtract, ALU.mult).then_inc(self.xn, 1)

            def pe_xT(self, pe, t, pT):
                pe.wait_ge(self.xn, t + 1)
                if t >= 1:
                    pe.wait_ge(self.hf, t)
                for c in range(KC):
                    mm = pe.transpose(pT[:, c * P:(c + 1) * P], self.x[:, t % 2, c * P:(c + 1) * P], ident[:, :])
                mm.then_inc(self.xT, 1)

            def act_h(self, act, t, pT):
                b = t // TPB
                act.wait_ge(self.xT, t + 1)
                if t >= 1:
                    act.wait_ge(self.lo, t)
                for c in range(KC):
                    a_ = act.activation(self.f[:, c, :], pT[:, c * P:(c + 1) * P], ACT.Identity,
                                        bias=mod3[:, self.shift + c, b:b + 1], scale=mod3[:, self.scale + c, b:b + 1])
                a_.then_inc(self.hf, 1)
                if t >= 2:
                    act.wait_ge(self.used, t - 1)
                act.wait_ge(self.hf, t + 1)
                act.activation(self.h_hi[:, t % 2, :, :], self.f[:, :, :], ACT.Copy).then_inc(self.hi, 1)

            def dve_lo(self, dve, t):
                dve.wait_ge(self.hi, t + 1)
                dve.tensor_tensor(self.h_lo[:, t % 2, :, :], self.f[:, :, :], self.h_hi[:, t % 2, :, :].bitcast(F32),
                                  ALU.subtract).then_inc(self.lo, 1)

            def h(self, t, c):
                return (self.h_hi[:, t % 2, c, :], self.h_lo[:, t % 2, c, :])

        def modulation(layer, wmod, extra_act=None, extra_dve=None, extra_sp=None):
            mod_ps = sem(f"mod_ps{layer}")
            mod_done = sem(f"mod_done{layer}")
            silu = sem(f"silu{layer}")
            chain = sem(f"mod_chain{layer}")
            gate_ps = sem(f"gate_ps{layer}")
            exp_c = sem(f"exp_c{layer}")
            gate_done = sem(f"gate_done{layer}")
            const_set = sem(f"const_set{layer}")
            src = a[f"wmod{layer}"].rearrange("(k p) n -> p k n", p=P)
            with nc.Block() as block:
                @block.sync
                def _(sp):
                    if layer == 0:
                        sp.dma_start(cs[:, :].rearrange("p (l k b) -> p l k b", l=2, b=B)[:, 0],
                                     a["c0"].rearrange("(k p) b -> p k b", p=P)).then_inc(const_in, 16)
                        sp.dma_start(cs[:, :].rearrange("p (l k b) -> p l k b", l=2, b=B)[:, 1],
                                     a["c1"].rearrange("(k p) b -> p k b", p=P)).then_inc(const_in, 16)
                        sp.dma_start(ident[:, :], a["ident"]).then_inc(const_in, 16)
                    for j in range(6):
                        sp.dma_start(wmod[:, :, j * D:(j + 1) * D], src[:, :, j * D:(j + 1) * D]).then_inc(wmod_in[j], 16)
                    if layer == 0:
                        for t in range(TILES):
                            sp.dma_start(x[:, t, :], x_dram[:, t, :]).then_inc(x_in, 16)
                    if extra_sp:
                        extra_sp(sp)

                @block.scalar
                def _(act):
                    if layer == 0:
                        act.wait_ge(const_in, 48)
                        act.activation(cs_e[:, :], cs[:, :], ACT.Exp, scale=-1.0).then_inc(exp_c, 1)
                    if extra_act:
                        extra_act(act)

                @block.vector
                def _(dve):
                    link = Chain(dve, chain)
                    if layer == 0:
                        dve.memset(ones[:, :], 1.0).then_inc(const_set, 1)
                        dve.memset(eps[:, :], LN_EPS).then_inc(const_set, 1)
                        dve.wait_ge(exp_c, 1)
                        link(dve.tensor_scalar_add(cs_e[:, :], cs_e[:, :], 1.0))
                        link(dve.reciprocal(cs_e[:, :], cs_e[:, :]))
                        dve.tensor_tensor(cs_s[:, :], cs[:, :], cs_e[:, :], ALU.mult).then_inc(silu, 1)
                    if extra_dve:
                        extra_dve(dve)
                    dve.wait_ge(mod_ps, 1)
                    link(dve.tensor_copy(mod[:, :], bank[0][:, 0:SIX * B]))
                    link(dve.tensor_scalar_add(mod3[:, CA:CA + KC, :], mod3[:, CA:CA + KC, :], 1.0))
                    link(dve.tensor_scalar_add(mod3[:, CB:CB + KC, :], mod3[:, CB:CB + KC, :], 1.0))
                    w = KC * B
                    for n, g in enumerate((GA, GB)):
                        gg = mod3[:, g:g + KC, :].rearrange("p m b -> p (m b)")
                        t0, t1 = gabs[:, 2 * n * w:(2 * n + 1) * w], gabs[:, (2 * n + 1) * w:(2 * n + 2) * w]
                        link(dve.tensor_scalar(t0, gg, -1.0, None, ALU.mult))
                        link(dve.tensor_tensor(t0, t0, gg, ALU.max))
                        link(dve.tensor_scalar(t0, t0, 0.25, None, ALU.max))
                        link(dve.tensor_scalar(t1, gg, 0.0, 2.0, ALU.is_ge, ALU.mult))
                        link(dve.tensor_scalar(t1, t1, -1.0, None, ALU.add))
                        link(dve.tensor_tensor(gg, t0, t1, ALU.mult))
                    dve.tensor_scalar_add(gabs[:, 0:1], gabs[:, 0:1], 0.0).then_inc(mod_done, 1)
                    for n in range(4):
                        dve.wait_ge(gate_ps, n + 1)
                        dve.tensor_copy(gate[:, n // 2, n % 2, :], bank[1 + n][:, :]).then_inc(gate_done, 1)

                @block.tensor
                def _(pe):
                    if layer == 0:
                        pe.wait_ge(silu, 1)
                    for j in range(6):
                        pe.wait_ge(wmod_in[j], 16 * (layer + 1))
                        for m in range(j * KC, (j + 1) * KC):
                            for k in range(KC):
                                mm = pe.matmul(bank[0][:, m * B:(m + 1) * B], wmod[:, k, m * P:(m + 1) * P],
                                               cs4[:, layer, k, :], start=(k == 0), stop=(k == KC - 1))
                    mm.then_inc(mod_ps, 1)
                    pe.wait_ge(mod_done, 1)
                    for n, (g, b) in enumerate(((GA, 0), (GA, 1), (GB, 0), (GB, 1))):
                        for c in range(KC):
                            mm = pe.matmul(bank[1 + n][:, c * P:(c + 1) * P],
                                           bc(mod3[:, g + c, b:b + 1], [P, P]), ident[:, :], start=True, stop=True)
                        mm.then_inc(gate_ps, 1)

        raw_n = [0]

        with ExitStack() as ph:
            stage = sb("stage_a", [P, 2, 3 * D], F32, ph)
            wq_hi = sb("wqkv_hi", [P, KC, 3 * D], F32R, ph)
            wq_lo = sb("wqkv_lo", [P, KC, 3 * D], F32R, ph)
            wsrc = a["wqkv0"].rearrange("(k p) n -> p k n", p=P)
            chunks = [wsrc[:, k, :] for k in range(KC)]
            parts = [(wq_hi[:, k, :], wq_lo[:, k, :]) for k in range(KC)]
            base = raw_n[0]
            with ExitStack() as ms:
                wmod0 = sb("wmod0", [P, KC, 6 * D], F32, ms)
                modulation(0, wmod0,
                           extra_sp=lambda sp: load_chunks(sp, stage, chunks, base),
                           extra_act=lambda act: split_act(act, stage, parts, base),
                           extra_dve=lambda dve: split_dve(dve, stage, parts, base))
            raw_n[0] += len(chunks)

            bias0 = sb("bias0", [P, 3 * D], F32, ph)
            qk = sb("qk", [P, 2, H0, PAD0], F32, ph)
            v_tok = sb("v_tok", [P, D], F32, ph)
            qT = sb("qT", [P, 32, H0], F32, ph)
            kT = sb("kT", [P, 2, 32, H0], F32, ph)
            q_bd = sb("q_bd", [P, 32, P], F32, ph)
            e_bd = sb("e_bd", [P, 32, P], F32, ph)
            vT = sb("vT", [P, 3, 32, VW], F32, ph)
            s_max = sb("s_max", [P, 32], F32, ph)
            s_sub = sb("s_sub", [P, 32, H0], F32, ph)
            e_s = sb("e_s", [P, 32, H0], F32, ph)
            eT = sb("eT", [P, 32, H0], F32, ph)
            o_rec = sb("o_rec", [P, 32], F32, ph)
            o_n = sb("o_n", [P, HD0, 32], F32, ph)
            o_tok = sb("o_tok", [P, D], F32, ph)
            o_g = sb("o_g", [P, D], F32, ph)
            bias_in = sem("bias_in")
            pad_set = sem("pad_set")
            qkv_ps = sem("qkv_ps")
            nrm = Norm("n0", SA, CA, used=qkv_ps, ctx=ph)
            qkv_ev = sem("qkv_ev")
            qT_done = sem("qT_done")
            qbd_done = sem("qbd_done")
            s_ps = sem("s_ps")
            max_done = sem("max_done")
            sub_done = sem("sub_done")
            exp_done = sem("exp_done")
            eT_done = sem("eT_done")
            ebd_done = sem("ebd_done")
            o_ps = sem("o_ps")
            rec_done = sem("rec_done")
            on_done = sem("on_done")
            otok_done = sem("otok_done")
            og_done = sem("og_done")
            x1_done = sem("x1_done")
            pT, q_ps, k_ps, v_ps = bank[0], bank[1], bank[2], bank[3]
            s_bank, o_bank = bank[4:6], bank[6:8]
            HB = 16
            OW = HB * VW

            def s_view(j):
                return s_bank[j][:, :].rearrange("p (n h) -> p n h", h=H0)

            def o_view(j):
                return o_bank[j][:, 0:OW].rearrange("p (n d) -> p n d", d=VW)

            with nc.Block() as block:
                @block.sync
                def _(sp):
                    sp.dma_start(bias0[:, :], bc(a["bqkv0"], [P, 3 * D])).then_inc(bias_in, 16)

                @block.gpsimd
                def _(pool):
                    pool.memset(qk[:, :, :, :], 0.0).then_inc(pad_set, 1)
                    pool.memset(q_bd[:, :, :], 0.0).then_inc(pad_set, 1)
                    pool.memset(e_bd[:, :, :], 0.0).then_inc(pad_set, 1)
                    pool.memset(vT[:, :, :, :], 1.0).then_inc(pad_set, 1)
                    for t in range(TILES):
                        pool.wait_ge(otok_done, t + 1)
                        if t >= 1:
                            pool.wait_ge(x1_done, t)
                        pool.tensor_tensor(o_g[:, :], o_tok[:, :], gate[:, 0, t // TPB, :], ALU.mult).then_inc(og_done, 1)
                        pool.wait_ge(og_done, t + 1)
                        pool.tensor_tensor(x[:, t, :], x[:, t, :], o_g[:, :], ALU.add).then_inc(x1_done, 1)

                @block.scalar
                def _(act):
                    nrm.act_std(act)

                    def q_blocks(t):
                        act.wait_ge(qT_done, 3 * t + 3)
                        if t >= 1:
                            act.wait_ge(s_ps, t)
                        else:
                            act.wait_ge(pad_set, 4)
                        for g in range(QD):
                            r = slice(32 * g, 32 * g + 32)
                            a_ = act.activation(q_bd[r, :, r], qT[r, :, :], ACT.Copy)
                        a_.then_inc(qbd_done, 1)

                    def exps(t):
                        act.wait_ge(sub_done, 2 * t + 2)
                        if t >= 1:
                            act.wait_ge(eT_done, t)
                        act.activation(e_s[:, :, :], s_sub[:, :, :], ACT.Exp, scale=float(HD0) ** -0.5).then_inc(exp_done, 1)
                        act.wait_ge(eT_done, t + 1)
                        if t >= 1:
                            act.wait_ge(o_ps, t)
                        for g in range(QD):
                            r = slice(32 * g, 32 * g + 32)
                            a_ = act.activation(e_bd[r, :, r], eT[r, :, :], ACT.Copy)
                        a_.then_inc(ebd_done, 1)

                    nrm.act_h(act, 0, pT)
                    for t in range(TILES + 1):
                        if t + 1 < TILES:
                            nrm.act_h(act, t + 1, pT)
                        if t < TILES:
                            q_blocks(t)
                        if t >= 1:
                            exps(t - 1)

                @block.vector
                def _(dve):
                    dve.wait_ge(x_in, 16 * TILES)
                    nrm.dve_stats(dve)
                    nrm.dve_xn(dve, 0)
                    nrm.dve_lo(dve, 0)
                    dve.wait_ge(bias_in, 16)
                    dve.wait_ge(pad_set, 4)

                    def evac(t):
                        dve.wait_ge(qkv_ps, t + 1)
                        if t >= 1:
                            dve.wait_ge(qT_done, 3 * t)
                        for j, ps in enumerate((q_ps, k_ps)):
                            dve.tensor_tensor(qk[:, j, :, 0:HD0], ps[:, :].rearrange("p (h d) -> p h d", d=HD0),
                                              bias0[:, j * D:(j + 1) * D].rearrange("p (h d) -> p h d", d=HD0),
                                              ALU.add).then_inc(qkv_ev, 1)
                        dve.tensor_tensor(v_tok[:, :], v_ps[:, :], bias0[:, 2 * D:3 * D], ALU.add).then_inc(qkv_ev, 1)
                        dve.wait_ge(qkv_ev, 3 * t + 1)
                        if t >= 1:
                            dve.wait_ge(qbd_done, t)
                        dve.transpose(qT[:, :, :].rearrange("p n h -> p h n"), qk[:, 0, :, :]).then_inc(qT_done, 1)
                        dve.wait_ge(qkv_ev, 3 * t + 2)
                        if t >= 2:
                            dve.wait_ge(s_ps, t - 1)
                        dve.transpose(kT[:, t % 2, :, :].rearrange("p n h -> p h n"), qk[:, 1, :, :]).then_inc(qT_done, 1)
                        dve.wait_ge(qkv_ev, 3 * t + 3)
                        if t >= 3:
                            dve.wait_ge(o_ps, t - 2)
                        dve.transpose(vT[:, t % 3, :, 0:HD0].rearrange("p n d -> p d n"),
                                      v_tok[:, :].rearrange("p (h d) -> p d h", d=HD0)).then_inc(qT_done, 1)

                    def softmax(t):
                        dve.wait_ge(s_ps, t + 1)
                        if t >= 1:
                            dve.wait_ge(sub_done, 2 * t)
                        for j in range(2):
                            dve.tensor_reduce(s_max[:, HB * j:HB * (j + 1)], s_view(j), AX.X, ALU.max).then_inc(max_done, 1)
                        if t >= 1:
                            dve.wait_ge(exp_done, t)
                        for j in range(2):
                            dve.wait_ge(max_done, 2 * t + j + 1)
                            dve.tensor_tensor(s_sub[:, HB * j:HB * (j + 1), :], s_view(j),
                                              bc(s_max[:, HB * j:HB * (j + 1)].unsqueeze(2), [P, HB, H0]),
                                              ALU.subtract).then_inc(sub_done, 1)

                    def turn(t):
                        dve.wait_ge(exp_done, t + 1)
                        if t >= 1:
                            dve.wait_ge(ebd_done, t)
                        dve.transpose(eT[:, :, :].rearrange("p n h -> p (n h)"),
                                      e_s[:, :, :].rearrange("p n h -> p (n h)")).then_inc(eT_done, 1)

                    def finish(t):
                        dve.wait_ge(o_ps, t + 1)
                        if t >= 1:
                            dve.wait_ge(on_done, 2 * t)
                        for j in range(2):
                            dve.reciprocal(o_rec[:, HB * j:HB * (j + 1)], o_view(j)[:, :, HD0]).then_inc(rec_done, 1)
                        if t >= 1:
                            dve.wait_ge(otok_done, t)
                        for j in range(2):
                            dve.wait_ge(rec_done, 2 * t + j + 1)
                            dve.tensor_tensor(o_n[:, :, HB * j:HB * (j + 1)].rearrange("p d n -> p n d"),
                                              o_view(j)[:, :, 0:HD0],
                                              bc(o_rec[:, HB * j:HB * (j + 1)].unsqueeze(2), [P, HB, HD0]),
                                              ALU.mult).then_inc(on_done, 1)
                        dve.wait_ge(on_done, 2 * t + 2)
                        if t >= 1:
                            dve.wait_ge(og_done, t)
                        dve.transpose(o_tok[:, :].rearrange("p (h d) -> p d h", d=HD0), o_n[:, :, :]).then_inc(otok_done, 1)

                    for t in range(TILES + 2):
                        if t + 1 < TILES:
                            nrm.dve_xn(dve, t + 1)
                            nrm.dve_lo(dve, t + 1)
                        if 1 <= t <= TILES:
                            softmax(t - 1)
                        if t < TILES:
                            evac(t)
                        if 1 <= t <= TILES:
                            turn(t - 1)
                        if t >= 2:
                            finish(t - 2)

                @block.tensor
                def _(pe):
                    def project(t):
                        pe.wait_ge(nrm.lo, t + 1)
                        if t >= 1:
                            pe.wait_ge(qkv_ev, 3 * t)
                        for j, ps in enumerate((q_ps, k_ps, v_ps)):
                            mm = split_matmuls(pe, ps[:, :], [
                                (nrm.h(t, c), (wq_hi[:, c, j * D:(j + 1) * D], wq_lo[:, c, j * D:(j + 1) * D]))
                                for c in range(KC)])
                        mm.then_inc(qkv_ps, 1)

                    def scores(t):
                        pe.wait_ge(qbd_done, t + 1)
                        if t >= 1:
                            pe.wait_ge(sub_done, 2 * t)
                        for n in range(32):
                            mm = pe.matmul(s_view(n // HB)[:, n % HB, :], q_bd[:, n, :], kT[:, t % 2, n, :],
                                           start=True, stop=True)
                        mm.then_inc(s_ps, 1)

                    def context(t):
                        pe.wait_ge(ebd_done, t + 1)
                        if t >= 1:
                            pe.wait_ge(on_done, 2 * t)
                        for n in range(32):
                            mm = pe.matmul(o_view(n // HB)[:, n % HB, :], e_bd[:, n, :], vT[:, t % 3, n, :],
                                           start=True, stop=True)
                        mm.then_inc(o_ps, 1)

                    nrm.pe_xT(pe, 0, pT)
                    for t in range(TILES + 2):
                        if t + 1 < TILES:
                            nrm.pe_xT(pe, t + 1, pT)
                        if t < TILES:
                            project(t)
                        if 1 <= t <= TILES:
                            scores(t - 1)
                        if t >= 2:
                            context(t - 2)

        if stop_after == 0:
            with nc.Block() as block:
                @block.sync
                def _(sp):
                    sp.dma_start(out_dram, x[:, :, :]).then_inc(stored, 16)
                    sp.wait_ge(stored, 16)
            return

        with ExitStack() as ph:
            stage = sb("stage_b", [P, 2, PROJ0], F32, ph)
            wf_hi = sb("wf_hi", [P, KC, PROJ0], F32R, ph)
            wf_lo = sb("wf_lo", [P, KC, PROJ0], F32R, ph)
            we_hi = sb("we_hi", [P, EC, D], F32R, ph)
            we_lo = sb("we_lo", [P, EC, D], F32R, ph)
            biasf = sb("biasf", [P, D], F32, ph)
            iota = sb("iota", [P, E0], F32, ph)
            top = sb("top", [P, 8], F32, ph)
            topi = sb("topi", [P, 8], U32, ph)
            topf = sb("topf", [P, 2], F32, ph)
            rp = sb("rp", [P, E0], F32, ph)
            rm = sb("rm", [P, 1], F32, ph)
            rsum = sb("rsum", [P, 1], F32, ph)
            den = sb("den", [P, 4], F32, ph)
            c1 = sb("c1", [P, E0], F32, ph)
            comb = sb("comb", [P, E0], F32, ph)
            z = sb("z", [P, 2, E0, R0], F32, ph)
            z_hi = sb("z_hi", [P, 2, 512], F32R, ph)
            z_lo = sb("z_lo", [P, 2, 512], F32R, ph)
            f_sum = sb("f_sum", [P, D], F32, ph)
            f_g = sb("f_g", [P, D], F32, ph)
            bias_in = sem("biasf_in")
            chain = sem("router_chain")
            base_ps = sem("base_ps")
            rexp_done = sem("rexp_done")
            rmax_done = sem("rmax_done")
            z_done = sem("z_done")
            zT_ps = sem("zT_ps")
            zhi_done = sem("zhi_done")
            zlo_done = sem("zlo_done")
            f_ps = sem("f_ps")
            fsum_done = sem("fsum_done")
            fg_done = sem("fg_done")
            x2_done = sem("x2_done")
            nrm = Norm("n1", SB, CB, used=base_ps, ctx=ph)
            pT = bank[0]
            y_bank, r_bank, z_bank = bank[1:3], bank[3:5], bank[5:7]
            fsrc = a["wffn0"].rearrange("(k p) n -> p k n", p=P)
            esrc = a["wexp0"].rearrange("(k p) n -> p k n", p=P)
            chunks = [fsrc[:, k, :] for k in range(KC)] + [esrc[:, k, :] for k in range(EC)]
            parts = ([(wf_hi[:, k, :], wf_lo[:, k, :]) for k in range(KC)]
                     + [(we_hi[:, k, :], we_lo[:, k, :]) for k in range(EC)])
            base = raw_n[0]
            raw_n[0] += len(chunks)
            split_all = base + len(chunks)

            with nc.Block() as block:
                @block.sync
                def _(sp):
                    sp.dma_start(biasf[:, :], bc(a["bffn0"], [P, D])).then_inc(bias_in, 16)
                    sp.dma_start(iota[:, :], a["iota"]).then_inc(bias_in, 16)
                    load_chunks(sp, stage, chunks, base)

                @block.gpsimd
                def _(pool):
                    for t in range(TILES):
                        pool.wait_ge(fsum_done, t + 1)
                        if t >= 1:
                            pool.wait_ge(x2_done, t)
                        pool.tensor_tensor(f_g[:, :], f_sum[:, :], gate[:, 1, t // TPB, :], ALU.mult).then_inc(fg_done, 1)
                        pool.wait_ge(fg_done, t + 1)
                        pool.tensor_tensor(x[:, t, :], x[:, t, :], f_g[:, :], ALU.add).then_inc(x2_done, 1)

                @block.scalar
                def _(act):
                    nrm.act_std(act)
                    split_act(act, stage, parts, base)
                    nrm.act_h(act, 0, pT)
                    for t in range(TILES + 1):
                        if t + 1 < TILES:
                            nrm.act_h(act, t + 1, pT)
                        if t < TILES:
                            act.wait_ge(rmax_done, t + 1)
                            if t >= 1:
                                act.wait_ge(z_done, t)
                            act.activation(rp[:, :], r_bank[t % 2][:, R0:R0 + E0], ACT.Exp, bias=rm[:, 0:1],
                                           accum_out=rsum[:, 0:1]).then_inc(rexp_done, 1)
                        if t >= 1:
                            for j in range(2):
                                n = 2 * (t - 1) + j
                                act.wait_ge(zT_ps, n + 1)
                                if n >= 2:
                                    act.wait_ge(f_ps, n - 1)
                                act.activation(z_hi[:, j, :], z_bank[j][:, :], ACT.Copy).then_inc(zhi_done, 1)

                @block.vector
                def _(dve):
                    nrm.dve_stats(dve)
                    split_dve(dve, stage, parts, base)
                    nrm.dve_xn(dve, 0)
                    nrm.dve_lo(dve, 0)
                    dve.wait_ge(bias_in, 32)
                    link = Chain(dve, chain)

                    def route(t):
                        rb = r_bank[t % 2]
                        dve.wait_ge(base_ps, t + 1)
                        dve.tensor_reduce(rm[:, :], rb[:, R0:R0 + E0], AX.X, ALU.max, negate=True).then_inc(rmax_done, 1)
                        dve.wait_ge(rexp_done, t + 1)
                        link(dve.max(top[:, :], rp[:, :]))
                        link(dve.max_index(topi[:, :], top[:, :], rp[:, :]))
                        link(dve.tensor_copy(topf[:, :], topi[:, 0:2]))
                        link(dve.tensor_scalar(den[:, 0:1], rsum[:, :], 1e-6, None, ALU.mult))
                        link(dve.tensor_tensor(den[:, 1:2], top[:, 0:1], top[:, 1:2], ALU.add))
                        link(dve.tensor_tensor(den[:, 2:3], den[:, 0:1], den[:, 1:2], ALU.add))
                        link(dve.reciprocal(den[:, 3:4], den[:, 2:3]))
                        link(dve.tensor_scalar(top[:, 0:2], top[:, 0:2], den[:, 3:4], LORA_SCALE, ALU.mult, ALU.mult))
                        link(dve.tensor_scalar(c1[:, :], iota[:, :], topf[:, 0:1], top[:, 0:1], ALU.is_equal, ALU.mult))
                        link(dve.tensor_scalar(comb[:, :], iota[:, :], topf[:, 1:2], top[:, 1:2], ALU.is_equal, ALU.mult))
                        link(dve.tensor_tensor(comb[:, :], comb[:, :], c1[:, :], ALU.add))
                        if t >= 2:
                            dve.wait_ge(zT_ps, 2 * (t - 1))
                        dve.tensor_tensor(z[:, t % 2, :, :], bc(rb[:, 0:R0].unsqueeze(1), [P, E0, R0]),
                                          bc(comb[:, :].unsqueeze(2), [P, E0, R0]), ALU.mult).then_inc(z_done, 1)

                    for t in range(TILES + 1):
                        if t + 1 < TILES:
                            nrm.dve_xn(dve, t + 1)
                            nrm.dve_lo(dve, t + 1)
                        if t < TILES:
                            route(t)
                        if t >= 1:
                            for j in range(2):
                                n = 2 * (t - 1) + j
                                dve.wait_ge(zhi_done, n + 1)
                                if n >= 2:
                                    dve.wait_ge(f_ps, n - 1)
                                dve.tensor_tensor(z_lo[:, j, :], z_bank[j][:, :], z_hi[:, j, :].bitcast(F32),
                                                  ALU.subtract).then_inc(zlo_done, 1)
                            dve.wait_ge(f_ps, 2 * t)
                            if t >= 2:
                                dve.wait_ge(fg_done, t - 1)
                            dve.tensor_tensor(f_sum[:, :], y_bank[(t - 1) % 2][:, :], biasf[:, :],
                                              ALU.add).then_inc(fsum_done, 1)

                @block.tensor
                def _(pe):
                    def project(t):
                        pe.wait_ge(nrm.lo, t + 1)
                        if t >= 2:
                            pe.wait_ge(fsum_done, t - 1)
                            pe.wait_ge(z_done, t - 1)
                        split_matmuls(pe, y_bank[t % 2][:, :], [
                            (nrm.h(t, c), (wf_hi[:, c, 0:D], wf_lo[:, c, 0:D])) for c in range(KC)], last=False)
                        split_matmuls(pe, r_bank[t % 2][:, 0:R0 + E0], [
                            (nrm.h(t, c), (wf_hi[:, c, D:PROJ0], wf_lo[:, c, D:PROJ0]))
                            for c in range(KC)]).then_inc(base_ps, 1)

                    def turn(t):
                        pe.wait_ge(z_done, t + 1)
                        for j in range(2):
                            if t >= 1:
                                pe.wait_ge(zlo_done, 2 * t - 1 + j)
                            for c in range(4):
                                e = 2 * (4 * j + c)
                                mm = pe.transpose(z_bank[j][:, c * P:(c + 1) * P],
                                                  z[:, t % 2, e:e + 2, :].rearrange("p e r -> p (e r)"), ident[:, :])
                            mm.then_inc(zT_ps, 1)

                    def experts(t):
                        for j in range(2):
                            pe.wait_ge(zlo_done, 2 * t + j + 1)
                            mm = split_matmuls(pe, y_bank[t % 2][:, :], [
                                ((z_hi[:, j, c * P:(c + 1) * P], z_lo[:, j, c * P:(c + 1) * P]),
                                 (we_hi[:, 4 * j + c, :], we_lo[:, 4 * j + c, :])) for c in range(4)],
                                first=False, last=(j == 1))
                            mm.then_inc(f_ps, 1)

                    nrm.pe_xT(pe, 0, pT)
                    pe.wait_ge(raw_free, split_all)
                    for t in range(TILES + 1):
                        if t + 1 < TILES:
                            nrm.pe_xT(pe, t + 1, pT)
                        if t < TILES:
                            project(t)
                        if t >= 1:
                            turn(t - 1)
                            experts(t - 1)

        if stop_after == 1:
            with nc.Block() as block:
                @block.sync
                def _(sp):
                    sp.dma_start(out_dram, x[:, :, :]).then_inc(stored, 16)
                    sp.wait_ge(stored, 16)
            return

        with ExitStack() as ms:
            wmod1 = sb("wmod1", [P, KC, 6 * D], F32, ms)
            modulation(1, wmod1)

        with ExitStack() as ph:
            wq_all = sb("wq_all", [P, NH, 2, P], F32, ph)
            wb_all = sb("wb_all", [P, HP, D], F32, ph)
            xk_hi = sb("xk_hi", [P, 3, TOK], F32R, ph)
            xk_lo = sb("xk_lo", [P, 2, TOK], F32R, ph)
            c_hi = sb("c_hi", [P, TILES, 3 * KVR], F32R, ph)
            c_lo = sb("c_lo", [P, TILES, 3 * KVR], F32R, ph)
            cosq = sb("cosq", [P, S], F32, ph)
            sinq = sb("sinq", [P, S], F32, ph)
            rot_in = sem("rot_in")

            with ExitStack() as pr:
                HPC = 4
                stage = sb("stage_c", [P, 2, CQ], F32, pr)
                wc_hi = sb("wc_hi", [P, KC, CQ], F32R, pr)
                wc_lo = sb("wc_lo", [P, KC, CQ], F32R, pr)
                wqn = sb("wqn", [P, 2, HPC, 2 * P], F32, pr)
                wkn = sb("wkn", [P, NH, KVR], F32, pr)
                wvn = sb("wvn", [P, NH, KVR], F32, pr)
                wo = sb("wo", [P, 2, HPC, D], F32, pr)
                gq = sb("gq", [P, QR], F32, pr)
                gk = sb("gk", [P, KVR], F32, pr)
                cosk = sb("cosk", [P, TPB, RD], F32, pr)
                sink = sb("sink", [P, TPB, RD], F32, pr)
                sq = sb("sq", [P, QR], F32, pr)
                ssq = sb("ssq", [P, 2, 2], F32, pr)
                rms = sb("rms", [P, 2, 2], F32, pr)
                qn = sb("qn", [P, 2, 2 * P], F32, pr)
                kk = sb("kk", [P, 2, P], F32, pr)
                ra = sb("ra", [P, RD], F32, pr)
                rb = sb("rb", [P, RD], F32, pr)
                small_in = sem("small_in")
                wqn_in = [sem("wqn_in0"), sem("wqn_in1")]
                wo_in = [sem("wo_in0"), sem("wo_in1")]
                ab_ps = sem("ab_ps")
                ab_ev = sem("ab_ev")
                c_ps = sem("c_ps")
                sq_done = sem("sq_done")
                ssq_done = sem("ssq_done")
                rms_done = sem("rms_done")
                c_set = sem("c_set")
                chain = sem("rms_chain")
                kk_done = sem("kk_done")
                xkT_ps = sem("xkT_ps")
                xkhi_done = sem("xkhi_done")
                xklo_done = sem("xklo_done")
                nrm = Norm("n2", SA, CA, used=c_ps, ctx=pr)
                pT, c_bank, k_bank = bank[0], bank[1:3], bank[3:5]
                a_bank, b_bank = bank[5], bank[6:8]
                csrc = a["wc1"].rearrange("(k p) n -> p k n", p=P)
                chunks = [csrc[:, k, :] for k in range(KC)]
                parts = [(wc_hi[:, k, :], wc_lo[:, k, :]) for k in range(KC)]
                base = raw_n[0]
                raw_n[0] += len(chunks)
                split_c = base + len(chunks)
                GROUPS = NH // HPC
                STEPS = 1 + HPC // 2

                with nc.Block() as block:
                    @block.sync
                    def _(sp):
                        load_chunks(sp, stage, chunks, base)
                        sp.dma_start(gq[:, :], bc(a["gq1"], [P, QR])).then_inc(small_in, 16)
                        sp.dma_start(gk[:, :], bc(a["gk1"], [P, KVR])).then_inc(small_in, 16)
                        sp.dma_start(cosk[:, :, :], a["cosk"]).then_inc(small_in, 16)
                        sp.dma_start(sink[:, :, :], a["sink"]).then_inc(small_in, 16)
                        sp.dma_start(wkn[:, :, :], a["wkn1"]).then_inc(small_in, 16)
                        sp.dma_start(wvn[:, :, :], a["wvn1"]).then_inc(small_in, 16)
                        for g in range(GROUPS):
                            if g >= 2:
                                sp.wait_ge(ab_ps, STEPS * (g - 1))
                            hs = slice(g * HPC, (g + 1) * HPC)
                            sp.dma_start(wqn[:, g % 2, :, :], a["wqn1"][hs].rearrange("h n m -> n h m")).then_inc(wqn_in[g % 2], 16)
                            sp.dma_start(wo[:, g % 2, :, :],
                                         a["wo1"].rearrange("(h v) n -> v h n", v=VD)[:, hs, :]).then_inc(wo_in[g % 2], 16)
                        for c in range(2):
                            sp.dma_start(wq_all[:, :, c, KVR:P], a["wqr1"][:, c]).then_inc(rot_in, 16)
                        sp.dma_start(cosq[:, :], a["cosq"]).then_inc(rot_in, 16)
                        sp.dma_start(sinq[:, :], a["sinq"]).then_inc(rot_in, 16)
                        sp.wait_ge(rot_in, 64)

                    @block.scalar
                    def _(act):
                        nrm.act_std(act)
                        split_act(act, stage, parts, base)
                        nrm.act_h(act, 0, pT)
                        for t in range(TILES + 1):
                            if t + 1 < TILES:
                                nrm.act_h(act, t + 1, pT)
                            if t < TILES:
                                act.wait_ge(c_ps, t + 1)
                                if t >= 1:
                                    act.wait_ge(sq_done, 2 * t)
                                if t >= 2:
                                    act.wait_ge(rms_done, t - 1)
                                cb = c_bank[t % 2]
                                act.activation(sq[:, 0:QR], cb[:, 0:QR], ACT.Square,
                                               accum_out=ssq[:, t % 2, 0:1]).then_inc(sq_done, 1)
                                act.wait_ge(sq_done, 2 * t + 1)
                                act.activation(sq[:, 0:KVR], cb[:, QR:QR + KVR], ACT.Square,
                                               accum_out=ssq[:, t % 2, 1:2]).then_inc(sq_done, 1)
                                act.wait_ge(sq_done, 2 * t + 2)
                                act.activation(rms[:, t % 2, 0:1], ssq[:, t % 2, 0:1], ACT.Sqrt,
                                               scale=1.0 / QR).then_inc(ssq_done, 1)
                                act.activation(rms[:, t % 2, 1:2], ssq[:, t % 2, 1:2], ACT.Sqrt,
                                               scale=1.0 / KVR).then_inc(ssq_done, 1)
                            if t >= 1:
                                act.wait_ge(xkT_ps, t)
                                ts = slice((t - 1) * P, t * P)
                                act.activation(xk_hi[:, :, ts],
                                               k_bank[(t - 1) % 2][:, 0:3 * P].rearrange("p (c n) -> p c n", c=3),
                                               ACT.Copy).then_inc(xkhi_done, 1)
                        for g in range(GROUPS):
                            act.wait_ge(ab_ps, STEPS * g + 1)
                            act.activation(wq_all[:, g * HPC:(g + 1) * HPC, :, 0:KVR],
                                           a_bank[:, :].rearrange("p (h c n) -> p h c n", h=HPC, c=2),
                                           ACT.Copy).then_inc(ab_ev, 1)
                            for q in range(HPC // 2):
                                act.wait_ge(ab_ps, STEPS * g + q + 2)
                                act.activation(wb_all[:, g * HPC // 2 + q, :], b_bank[q % 2][:, :],
                                               ACT.Copy).then_inc(ab_ev, 1)

                    @block.vector
                    def _(dve):
                        nrm.dve_stats(dve)
                        split_dve(dve, stage, parts, base)
                        dve.memset(c_hi[:, :, :].bitcast(F32), 0.0).then_inc(c_set, 1)
                        dve.memset(c_lo[:, :, :].bitcast(F32), 0.0).then_inc(c_set, 1)
                        dve.wait_ge(c_set, 2)
                        nrm.dve_xn(dve, 0)
                        nrm.dve_lo(dve, 0)
                        dve.wait_ge(small_in, 96)
                        link = Chain(dve, chain)
                        for t in range(TILES + 1):
                            if t + 1 < TILES:
                                nrm.dve_xn(dve, t + 1)
                                nrm.dve_lo(dve, t + 1)
                            if t < TILES:
                                cb, s2 = c_bank[t % 2], t % 2
                                r0, r1 = rms[:, s2, 0:1], rms[:, s2, 1:2]
                                dve.wait_ge(ssq_done, 2 * t + 2)
                                link(dve.tensor_scalar_add(rms[:, s2, :], rms[:, s2, :], RMS_EPS))
                                link(dve.reciprocal(rms[:, s2, :], rms[:, s2, :]))
                                dve.tensor_tensor(ra[:, :], cb[:, QR + KVR:CQ], cosk[:, t % TPB, :], ALU.mult)
                                dve.tensor_tensor(rb[:, 0:32], cb[:, CQ - 32:CQ], sink[:, t % TPB, 32:RD], ALU.mult)
                                link(dve.tensor_tensor(rb[:, 32:RD], cb[:, QR + KVR:CQ - 32], sink[:, t % TPB, 0:32], ALU.mult))
                                if t >= 2:
                                    dve.wait_ge(xkT_ps, t - 1)
                                dve.scalar_tensor_tensor(qn[:, s2, 0:QR], cb[:, 0:QR], r0, gq[:, :], ALU.mult, ALU.mult)
                                dve.scalar_tensor_tensor(qn[:, s2, QR:2 * P], cb[:, P:QR], r0, gq[:, P:QR], ALU.mult, ALU.mult)
                                link(dve.scalar_tensor_tensor(kk[:, s2, 0:KVR], cb[:, QR:QR + KVR], r1, gk[:, :],
                                                              ALU.mult, ALU.mult))
                                link(dve.tensor_copy(c_hi[:, t, KVR:2 * KVR], kk[:, s2, 0:KVR]))
                                dve.tensor_tensor(c_lo[:, t, KVR:2 * KVR], kk[:, s2, 0:KVR],
                                                  c_hi[:, t, KVR:2 * KVR].bitcast(F32), ALU.subtract)
                                dve.tensor_tensor(kk[:, s2, KVR:P], ra[:, :], rb[:, :], ALU.add).then_inc(kk_done, 1)
                                dve.wait_ge(kk_done, t + 1)
                                dve.tensor_scalar_add(ssq[:, s2, :], ssq[:, s2, :], 0.0).then_inc(rms_done, 1)
                            if t >= 1:
                                kb = k_bank[(t - 1) % 2]
                                ts = slice((t - 1) * P, t * P)
                                dve.wait_ge(xkhi_done, t)
                                dve.tensor_tensor(xk_lo[:, :, ts],
                                                  kb[:, 0:3 * P].rearrange("p (c n) -> p c n", c=3)[:, 0:3:2, :],
                                                  xk_hi[:, 0:3:2, ts].bitcast(F32), ALU.subtract)
                                dve.tensor_tensor(xk_hi[QREST:P, 1, ts], kb[QREST:P, P:2 * P],
                                                  xk_hi[QREST:P, 1, ts].bitcast(F32), ALU.subtract).then_inc(xklo_done, 1)

                    @block.tensor
                    def _(pe):
                        def turn(t):
                            pe.wait_ge(kk_done, t + 1)
                            if t >= 2:
                                pe.wait_ge(xklo_done, t - 1)
                            kb = k_bank[t % 2]
                            pe.transpose(kb[:, 0:P], qn[:, t % 2, 0:P], ident[:, :])
                            pe.transpose(kb[:, P:2 * P], qn[:, t % 2, P:2 * P], ident[:, :])
                            pe.transpose(kb[:, 2 * P:3 * P], kk[:, t % 2, :], ident[:, :]).then_inc(xkT_ps, 1)

                        nrm.pe_xT(pe, 0, pT)
                        pe.wait_ge(raw_free, split_c)
                        for t in range(TILES + 1):
                            if t + 1 < TILES:
                                nrm.pe_xT(pe, t + 1, pT)
                            if t < TILES:
                                pe.wait_ge(nrm.lo, t + 1)
                                if t >= 2:
                                    pe.wait_ge(rms_done, t - 1)
                                split_matmuls(pe, c_bank[t % 2][:, 0:CQ], [
                                    (nrm.h(t, c), (wc_hi[:, c, :], wc_lo[:, c, :])) for c in range(KC)]).then_inc(c_ps, 1)
                            if t >= 1:
                                turn(t - 1)
                        pe.wait_ge(small_in, 96)
                        for g in range(GROUPS):
                            pe.wait_ge(wqn_in[g % 2], 16 * (g // 2 + 1))
                            if g >= 1:
                                pe.wait_ge(ab_ev, STEPS * (g - 1) + 1)
                            for q in range(HPC):
                                for c in range(2):
                                    mm = pe.matmul(a_bank[:, (2 * q + c) * KVR:(2 * q + c + 1) * KVR],
                                                   wqn[:, g % 2, q, c * P:(c + 1) * P], wkn[:, g * HPC + q, :],
                                                   start=True, stop=True)
                            mm.then_inc(ab_ps, 1)
                            pe.wait_ge(wo_in[g % 2], 16 * (g // 2 + 1))
                            for q in range(HPC // 2):
                                if g >= 1:
                                    pe.wait_ge(ab_ev, STEPS * (g - 1) + q + 2)
                                for e in range(2):
                                    mm = pe.matmul(b_bank[q % 2][e * KVR:(e + 1) * KVR, :], wvn[:, g * HPC + 2 * q + e, :],
                                                   wo[:, g % 2, 2 * q + e, :], start=True, stop=True)
                                mm.then_inc(ab_ps, 1)

            w_hi = sb("w_hi", [P, 2, 2, P], F32R, ph)
            w_lo = sb("w_lo", [P, 2, 2, P], F32R, ph)
            b_hi = sb("b_hi", [P, D], F32R, ph)
            b_lo = sb("b_lo", [P, D], F32R, ph)
            qf = sb("qf", [P, S], F32, ph)
            qu = sb("qu", [P, S], F32, ph)
            q_hi = sb("q_hi", [P, 2, S], F32R, ph)
            q_lo = sb("q_lo", [P, 2, S], F32R, ph)
            nmax = sb("nmax", [P, 2, TPB], F32, ph)
            rsum = sb("rsum1", [P, 2, TPB], F32, ph)
            rinv = sb("rinv", [P, 2, TPB], F32, ph)
            prob = sb("prob", [P, 2, TPB, S], F32, ph)
            pT_hi = sb("pT_hi", [P, TPB, S], F32R, ph)
            pT_lo = sb("pT_lo", [P, TPB, S], F32R, ph)
            cT_hi = sb("cT_hi", [P, S], F32R, ph)
            cT_lo = sb("cT_lo", [P, S], F32R, ph)
            o_tmp = sb("o_tmp", [P, 2, D], F32, ph)
            acc = sb("acc", [P, TILES, D], F32, ph)
            whi_done = sem("whi_done")
            wlo_done = sem("wlo_done")
            bhi_done = sem("bhi_done")
            blo_done = sem("blo_done")
            q_ps = sem("q1_ps")
            qrot = sem("qrot")
            qsum = sem("qsum")
            qhi_done = sem("qhi_done")
            qlo_done = sem("qlo_done")
            s_ps = sem("s1_ps")
            max_done = sem("max1_done")
            exp_done = sem("exp1_done")
            rinv_done = sem("rinv_done")
            norm_dve = sem("norm_dve")
            norm_pool = sem("norm_pool")
            pT_ps = sem("pT_ps")
            phi_done = sem("phi_done")
            plo_done = sem("plo_done")
            pv_ps = sem("pv_ps")
            chi_done = sem("chi_done")
            clo_done = sem("clo_done")
            o_ps = sem("o1_ps")
            o_ev = sem("o1_ev")
            acc_done = sem("acc_done")
            acc_set = sem("acc_set")
            x3_done = sem("x3_done")
            s_bank, t_bank = bank[0:2], bank[2:4]
            q_bank, ct_bank, o_bank = bank[4], bank[5:7], bank[7]
            UNITS = 4 * HP
            POOL_STEP = 2

            def ge(eng, s_, v):
                if not (isinstance(v, int) and v <= 0):
                    eng.wait_ge(s_, v)

            def pairs(eng, unit):
                for p in (0, 1):
                    for c in range(4):
                        unit(p, c, False)
                with eng.Fori(2, HP - 1) as p:
                    for c in range(4):
                        unit(p, c, True)
                for p in (HP - 1, HP):
                    for c in range(4):
                        unit(p, c, False)

            def out_step(p, c, st, steady):
                if c % 2:
                    return None
                n, m = st, p * 2 + (c // 2 - 2)
                if not steady and not 0 <= m < 2 * HP:
                    return None
                return m, n

            with nc.Block() as block:
                @block.tensor
                def _(pe):
                    def project(i, c, pair):
                        b, e = (c // 2) % 2, c % 2
                        ts = slice(b * S, (b + 1) * S)
                        if c == 0:
                            pe.wait_ge(wlo_done, pair + 1)
                        ge(pe, qrot, 3 * i)
                        pe.matmul(q_bank[:, :], w_hi[:, e, 0, :], xk_hi[:, 0, ts], start=True, stop=False)
                        pe.matmul(q_bank[:, :], w_hi[:, e, 0, :], xk_lo[:, 0, ts], start=False, stop=False)
                        pe.matmul(q_bank[:, :], w_lo[:, e, 0, :], xk_hi[:, 0, ts], start=False, stop=False)
                        pe.matmul(q_bank[:, :], w_hi[:, e, 1, :], xk_hi[:, 1, ts], start=False, stop=False)
                        pe.matmul(q_bank[:, :], w_lo[:, e, 1, :], xk_hi[:, 1, ts], start=False, stop=True).then_inc(q_ps, 1)

                    def context(g, c, tt):
                        e, b = c % 2, c // 2
                        w = slice(KVR, 3 * KVR) if e == 0 else slice(0, 2 * KVR)
                        ct = ct_bank[b][:, :]
                        ge(pe, plo_done, g + 1)
                        k = b * TPB + tt
                        first, last = e == 0 and tt == 0, e == 1 and tt == TPB - 1
                        pe.matmul(ct, c_hi[:, k, w], pT_hi[:, tt, :], start=first, stop=False)
                        pe.matmul(ct, c_hi[:, k, w], pT_lo[:, tt, :], start=False, stop=False)
                        pe.matmul(ct, c_lo[:, k, w], pT_hi[:, tt, :], start=False, stop=last).then_inc(pv_ps, 1)

                    def unit(p, c, steady):
                        i = p * 4 + c
                        b = c // 2
                        for st in range(TPB):
                            if steady or i < UNITS:
                                if st == 0:
                                    ge(pe, qlo_done, i + 1)
                                ge(pe, exp_done, i * 4 + (st - 1))
                                q = slice(st * P, (st + 1) * P)
                                sbk, ks = s_bank[st % 2][:, :], slice(b * S, (b + 1) * S)
                                pe.matmul(sbk, q_hi[:, c % 2, q], xk_hi[:, 2, ks], start=True, stop=False)
                                pe.matmul(sbk, q_hi[:, c % 2, q], xk_lo[:, 1, ks], start=False, stop=False)
                                pe.matmul(sbk, q_lo[:, c % 2, q], xk_hi[:, 2, ks], start=False, stop=True).then_inc(s_ps, 1)
                            if st == 0 and (steady or i + 2 < UNITS):
                                project(i + 2, (c + 2) % 4, p + (c + 2) // 4)
                            if steady or 1 <= i <= UNITS:
                                if st == 0:
                                    ge(pe, norm_dve, i * 3)
                                    ge(pe, norm_pool, i)
                                ge(pe, plo_done, i * 4 + (st - 5))
                                for n in range(TPB):
                                    mm = pe.transpose(t_bank[st % 2][:, n * P:(n + 1) * P],
                                                      prob[:, (c - 1) % 2, n, st * P:(st + 1) * P], ident[:, :])
                                mm.then_inc(pT_ps, 1)
                            if steady or 6 <= 4 * i + st < 4 * UNITS + 6:
                                cc = (c - 1) % 4 if st >= 2 else (c - 2) % 4
                                if cc % 2 == 0 and st == 2:
                                    ge(pe, clo_done, p * 2 + (c // 2 - 1))
                                context(i * 4 + (st - 6), cc, (st - 2) % TPB)
                            if (o := out_step(p, c, st, steady)) is not None:
                                m, n = o
                                if n == 0:
                                    ge(pe, clo_done, m + 1)
                                    if c == 0:
                                        ge(pe, blo_done, p)
                                ge(pe, o_ev, m * 4 + n)
                                ts = slice(n * P, (n + 1) * P)
                                pe.matmul(o_bank[:, :], cT_hi[:, ts], b_hi[:, :], start=True, stop=False)
                                pe.matmul(o_bank[:, :], cT_hi[:, ts], b_lo[:, :], start=False, stop=False)
                                pe.matmul(o_bank[:, :], cT_lo[:, ts], b_hi[:, :], start=False, stop=True).then_inc(o_ps, 1)

                    project(0, 0, 0)
                    project(1, 1, 0)
                    pairs(pe, unit)

                @block.vector
                def _(dve):
                    def rotate(i, part):
                        lo, hi = slice(KVR, KVR + 32), slice(KVR + 32, P)
                        if part == 0:
                            ge(dve, q_ps, i + 1)
                            ge(dve, qsum, i)
                            dve.tensor_tensor(qu[lo, :], q_bank[hi, :], sinq[hi, :], ALU.mult).then_inc(qrot, 1)
                        elif part == 1:
                            dve.tensor_tensor(qu[hi, :], q_bank[lo, :], sinq[lo, :], ALU.mult).then_inc(qrot, 1)
                        else:
                            ge(dve, qlo_done, i)
                            dve.tensor_tensor(qf[:, :], q_bank[:, :], cosq[:, :], ALU.mult).then_inc(qrot, 1)

                    def normalize(p, i, c, st):
                        ge(dve, exp_done, i * 4 + (st + 1))
                        if st == POOL_STEP:
                            ge(dve, norm_pool, i - 1)
                        r = rinv[:, c % 2, st:st + 1]
                        dve.reciprocal(r, rsum[:, c % 2, st:st + 1]).then_inc(rinv_done, 1)
                        if st != POOL_STEP:
                            ge(dve, rinv_done, i * 4 + (st + 1))
                            dve.tensor_scalar(prob[:, c % 2, st, :], prob[:, c % 2, st, :], r, None,
                                              ALU.mult).then_inc(norm_dve, 1)

                    def unit(p, c, steady):
                        i = p * 4 + c
                        for st in range(TPB):
                            g = i * 4 + st
                            if not st and (steady or 1 <= i <= UNITS):
                                normalize(p, i - 1, (c - 1) % 4, TPB - 1)
                            if steady or 5 <= g < 4 * UNITS + 5:
                                ge(dve, phi_done, i * 4 + (st - 4))
                                ge(dve, pv_ps, i * 4 + (st - 8))
                                dve.tensor_tensor(pT_lo[:, (st - 1) % TPB, :], t_bank[(st - 1) % 2][:, :],
                                                  pT_hi[:, (st - 1) % TPB, :].bitcast(F32), ALU.subtract).then_inc(plo_done, 1)
                            if (c % 2, st) == (1, 3) and (steady or 0 <= 2 * p + c // 2 - 1 < 2 * HP):
                                m = p * 2 + (c // 2 - 1)
                                ge(dve, chi_done, m + 1)
                                dve.tensor_tensor(cT_lo[:, :], ct_bank[(c // 2 - 1) % 2][:, :], cT_hi[:, :].bitcast(F32),
                                                  ALU.subtract).then_inc(clo_done, 1)
                            if steady or i < UNITS:
                                ge(dve, s_ps, i * 4 + (st + 1))
                                if st == 0:
                                    ge(dve, exp_done, (i - 1) * 4)
                                dve.tensor_reduce(nmax[:, c % 2, st:st + 1], s_bank[st % 2][:, :], AX.X, ALU.max,
                                                  negate=True).then_inc(max_done, 1)
                            if st and (steady or i < UNITS):
                                normalize(p, i, c, st - 1)
                            if st and (steady or i + 2 < UNITS):
                                rotate(i + 2, st - 1)

                    dve.wait_ge(acc_set, 1)
                    for i in (0, 1):
                        for part in range(3):
                            rotate(i, part)
                    pairs(dve, unit)

                @block.scalar
                def _(act):
                    def weights(p):
                        ge(act, q_ps, p * 4)
                        act.activation(w_hi[:, :, :, :], wq_all[:, bass.ds(p * 2, 2), :, :], ACT.Copy).then_inc(whi_done, 1)

                    def p_round(i, st, steady):
                        if steady or 1 <= i <= UNITS:
                            ge(act, pT_ps, (i - 1) * 4 + (st + 1))
                            ge(act, pv_ps, (i - 2) * 4 + (st + 1))
                            act.activation(pT_hi[:, st, :], t_bank[st % 2][:, :], ACT.Copy).then_inc(phi_done, 1)

                    def q_round(i, c):
                        ge(act, qsum, i + 1)
                        ge(act, s_ps, (i - 1) * 4)
                        act.activation(q_hi[:, c % 2, :], qf[:, :], ACT.Copy).then_inc(qhi_done, 1)

                    def unit(p, c, steady):
                        i = p * 4 + c
                        for st in range(TPB):
                            if st:
                                p_round(i, st, steady)
                            if steady or i < UNITS:
                                ge(act, max_done, i * 4 + (st + 1))
                                if st == 0:
                                    ge(act, pT_ps, (i - 1) * 4)
                                    ge(act, rinv_done, (i - 1) * 4)
                                act.activation(prob[:, c % 2, st, :], s_bank[st % 2][:, :], ACT.Exp,
                                               bias=nmax[:, c % 2, st:st + 1],
                                               accum_out=rsum[:, c % 2, st:st + 1]).then_inc(exp_done, 1)
                            if not st:
                                p_round(i, st, steady)
                            if (c % 2, st) == (1, 2) and (steady or 0 <= 2 * p + c // 2 - 1 < 2 * HP):
                                m = p * 2 + (c // 2 - 1)
                                ge(act, pv_ps, m * 8 + 8)
                                ge(act, o_ps, m * 4)
                                act.activation(cT_hi[:, :], ct_bank[(c // 2 - 1) % 2][:, :], ACT.Copy).then_inc(chi_done, 1)
                            if (o := out_step(p, c, st, steady)) is not None:
                                m, n = o
                                ge(act, o_ps, m * 4 + (n + 1))
                                ge(act, acc_done, m * 4 + (n - 1))
                                act.activation(o_tmp[:, n % 2, :], o_bank[:, :], ACT.Copy).then_inc(o_ev, 1)
                            if st == 0 and (steady or i + 1 < UNITS):
                                q_round(i + 1, c + 1)
                            if (c, st) == (1, 1) and (steady or p + 1 < HP):
                                weights(p + 1)
                            if (c, st) == (3, 0) and (steady or p < HP):
                                ge(act, o_ps, p * 8)
                                act.activation(b_hi[:, :], wb_all[:, p, :] if not steady else
                                               wb_all[:, bass.ds(p, 1), :].rearrange("p a n -> p (a n)"),
                                               ACT.Copy).then_inc(bhi_done, 1)

                    weights(0)
                    q_round(0, 0)
                    pairs(act, unit)

                @block.gpsimd
                def _(pool):
                    def weights(p):
                        ge(pool, whi_done, p + 1)
                        pool.tensor_tensor(w_lo[:, :, :, :], wq_all[:, bass.ds(p * 2, 2), :, :],
                                           w_hi[:, :, :, :].bitcast(F32), ALU.subtract).then_inc(wlo_done, 1)

                    def q_sum(i):
                        ge(pool, qrot, i * 3 + 3)
                        pool.tensor_tensor(qf[:, :], qf[:, :], qu[:, :], ALU.add).then_inc(qsum, 1)

                    def q_rest(i, c):
                        ge(pool, qhi_done, i + 1)
                        pool.tensor_tensor(q_lo[:, c % 2, :], qf[:, :], q_hi[:, c % 2, :].bitcast(F32),
                                           ALU.subtract).then_inc(qlo_done, 1)

                    def unit(p, c, steady):
                        i = p * 4 + c
                        for st in range(TPB):
                            if st == 0 and (steady or i + 1 < UNITS):
                                q_rest(i + 1, c + 1)
                            if (c, st) == (1, 1) and (steady or p + 1 < HP):
                                weights(p + 1)
                            if (c, st) == (3, 0) and (steady or p < HP):
                                ge(pool, bhi_done, p + 1)
                                pool.tensor_tensor(b_lo[:, :], wb_all[:, p, :] if not steady else
                                                   wb_all[:, bass.ds(p, 1), :].rearrange("p a n -> p (a n)"),
                                                   b_hi[:, :].bitcast(F32), ALU.subtract).then_inc(blo_done, 1)
                            if st == POOL_STEP + 1 and (steady or i < UNITS):
                                ge(pool, rinv_done, i * 4 + st)
                                pr_ = prob[:, c % 2, st - 1, :]
                                pool.tensor_tensor(pr_, pr_, bc(rinv[:, c % 2, st - 1:st], [P, S]),
                                                   ALU.mult).then_inc(norm_pool, 1)
                            if st == 3 and (steady or i + 2 < UNITS):
                                q_sum(i + 2)
                            if (o := out_step(p, c, st, steady)) is not None:
                                m, n = o
                                t = c // 2 * TPB + n
                                ge(pool, o_ev, m * 4 + (n + 1))
                                ge(pool, acc_done, m * 4 + n)
                                pool.tensor_tensor(acc[:, t, :], acc[:, t, :], o_tmp[:, n % 2, :], ALU.add).then_inc(acc_done, 1)

                    pool.memset(qu[:, :], 0.0).then_inc(acc_set, 1)
                    pool.memset(acc[:, :, :], 0.0).then_inc(acc_set, 1)
                    weights(0)
                    q_sum(0)
                    q_rest(0, 0)
                    q_sum(1)
                    pool.wait_ge(acc_set, 2)
                    pairs(pool, unit)
                    pool.wait_ge(acc_done, 4 * 2 * HP)
                    for t in range(TILES):
                        pool.tensor_tensor(acc[:, t, :], acc[:, t, :], gate[:, 0, t // TPB, :], ALU.mult).then_inc(acc_set, 1)
                        pool.wait_ge(acc_set, t + 3)
                        pool.tensor_tensor(x[:, t, :], x[:, t, :], acc[:, t, :], ALU.add).then_inc(x3_done, 1)

        if stop_after == 2:
            with nc.Block() as block:
                @block.sync
                def _(sp):
                    sp.dma_start(out_dram, x[:, :, :]).then_inc(stored, 16)
                    sp.wait_ge(stored, 16)
            return

        with ExitStack() as ph:
            stage = sb("stage_d", [P, KC, D], F32, ph)
            fa = sb("fa", [R1, D], F32, ph)
            fb = sb("fb", [R1, D], F32, ph)
            w_eff = sb("w_eff", [P, KC, D], F32, ph)
            w_sq = sb("w_sq", [P, KC, D], F32, ph)
            wh = sb("wl_hi", [P, KC, D], F32R, ph)
            wl = sb("wl_lo", [P, KC, D], F32R, ph)
            mag = sb("mag", [P, D], F32, ph)
            norm = sb("norm", [P, D], F32, ph)
            factor = sb("factor", [P, B, D], F32, ph)
            y_g = sb("y_g", [P, 2, D], F32, ph)
            w_in = sem("w_in")
            ba_ps = sem("ba_ps")
            weff_done = sem("weff_done")
            wsq_done = sem("wsq_done")
            whi2_done = sem("whi2_done")
            wlo2_done = sem("wlo2_done")
            norm_ps = sem("norm_ps")
            norm_done = sem("norm_done")
            chain = sem("factor_chain")
            y_ps = sem("y_ps")
            yg_done = sem("yg_done")
            x4_done = sem("x4_done")
            nrm = Norm("n3", SB, CB, used=y_ps, ctx=ph)
            pT, y_bank, n_bank, w_bank = bank[0], bank[1:3], bank[3], bank[4:8]

            with nc.Block() as block:
                @block.sync
                def _(sp):
                    sp.dma_start(stage[:, :, :], a["wf1"].rearrange("(k p) n -> p k n", p=P)).then_inc(w_in, 16)
                    sp.dma_start(fa[:, :], a["fa1"]).then_inc(w_in, 16)
                    sp.dma_start(fb[:, :], a["fb1"]).then_inc(w_in, 16)
                    sp.dma_start(mag[:, :], bc(a["mag1"], [P, D])).then_inc(w_in, 16)
                    for t in range(TILES):
                        sp.wait_ge(x4_done, t + 1)
                        sp.dma_start(out_dram[:, t, :], x[:, t, :]).then_inc(stored, 16)
                    sp.wait_ge(stored, 16 * TILES)

                @block.gpsimd
                def _(pool):
                    for t in range(TILES):
                        pool.wait_ge(yg_done, t + 1)
                        pool.tensor_tensor(x[:, t, :], x[:, t, :], y_g[:, t % 2, :], ALU.add).then_inc(x4_done, 1)

                @block.scalar
                def _(act):
                    nrm.act_std(act)
                    for k in range(KC):
                        act.wait_ge(weff_done, k + 1)
                        act.activation(w_sq[:, k, :], w_eff[:, k, :], ACT.Square).then_inc(wsq_done, 1)
                        act.activation(wh[:, k, :], w_eff[:, k, :], ACT.Copy).then_inc(whi2_done, 1)
                    act.wait_ge(norm_ps, 1)
                    act.activation(norm[:, :], n_bank[:, :], ACT.Sqrt).then_inc(norm_done, 1)
                    for t in range(TILES):
                        nrm.act_h(act, t, pT)

                @block.vector
                def _(dve):
                    nrm.dve_stats(dve)
                    dve.wait_ge(w_in, 64)
                    for k in range(KC):
                        dve.wait_ge(ba_ps, k + 1)
                        dve.tensor_tensor(w_eff[:, k, :], w_bank[k][:, :], stage[:, k, :], ALU.add).then_inc(weff_done, 1)
                    nrm.dve_xn(dve, 0)
                    for k in range(KC):
                        dve.wait_ge(whi2_done, k + 1)
                        dve.tensor_tensor(wl[:, k, :], w_eff[:, k, :], wh[:, k, :].bitcast(F32),
                                          ALU.subtract).then_inc(wlo2_done, 1)
                    link = Chain(dve, chain)
                    dve.wait_ge(norm_done, 1)
                    link(dve.reciprocal(norm[:, :], norm[:, :]))
                    link(dve.tensor_tensor(norm[:, :], norm[:, :], mag[:, :], ALU.mult))
                    for b in range(B):
                        link(dve.tensor_tensor(factor[:, b, :], norm[:, :], gate[:, 1, b, :], ALU.mult))
                    nrm.dve_lo(dve, 0)
                    for t in range(TILES):
                        if t + 1 < TILES:
                            nrm.dve_xn(dve, t + 1)
                            nrm.dve_lo(dve, t + 1)
                        dve.wait_ge(y_ps, t + 1)
                        if t >= 2:
                            dve.wait_ge(x4_done, t - 1)
                        dve.tensor_tensor(y_g[:, t % 2, :], y_bank[t % 2][:, :], factor[:, t // TPB, :],
                                          ALU.mult).then_inc(yg_done, 1)

                @block.tensor
                def _(pe):
                    pe.wait_ge(w_in, 64)
                    for k in range(KC):
                        pe.matmul(w_bank[k][:, :], fa[:, k * P:(k + 1) * P], fb[:, :],
                                  start=True, stop=True).then_inc(ba_ps, 1)
                    for k in range(KC):
                        pe.wait_ge(wsq_done, k + 1)
                        mm = pe.matmul(n_bank[:, :], ones[:, :], w_sq[:, k, :], start=(k == 0), stop=(k == KC - 1))
                    mm.then_inc(norm_ps, 1)
                    nrm.pe_xT(pe, 0, pT)
                    pe.wait_ge(wlo2_done, KC)
                    for t in range(TILES):
                        if t + 1 < TILES:
                            nrm.pe_xT(pe, t + 1, pT)
                        pe.wait_ge(nrm.lo, t + 1)
                        if t >= 2:
                            pe.wait_ge(yg_done, t - 1)
                        split_matmuls(pe, y_bank[t % 2][:, :], [
                            (nrm.h(t, c), (wh[:, c, :], wl[:, c, :])) for c in range(KC)]).then_inc(y_ps, 1)


def _constants():
    import numpy as np

    inv = (1.0 / 10000.0 ** (np.arange(0, RD, 2, dtype=np.float32) / np.float32(RD))).astype(np.float32)
    ang = np.outer(np.arange(S, dtype=np.float32), inv).astype(np.float32)
    cos, sin = np.cos(ang).astype(np.float32), np.sin(ang).astype(np.float32)
    cosq = np.full((P, S), SCALE1, np.float32)
    sinq = np.zeros((P, S), np.float32)
    cosq[KVR:] = np.concatenate([cos, cos], 1).T * np.float32(SCALE1)
    sinq[KVR:KVR + 32] = sin.T * np.float32(SCALE1)
    sinq[KVR + 32:] = -sin.T * np.float32(SCALE1)
    cosk = np.concatenate([cos, cos], 1).reshape(TPB, P, RD).transpose(1, 0, 2)
    sink = np.concatenate([sin, -sin], 1).reshape(TPB, P, RD).transpose(1, 0, 2)
    return {
        "ident": np.eye(P, dtype=np.float32),
        "iota": np.tile(np.arange(E0, dtype=np.float32), (P, 1)),
        "cosq": cosq, "sinq": sinq,
        "cosk": np.ascontiguousarray(cosk), "sink": np.ascontiguousarray(sink),
    }


def _layout(i):
    import numpy as np

    t = {k: np.asarray(v) for k, v in i.items()}
    wqb = t["L1_attn_w_qb"].reshape(QR, NH, ND + RD)
    wkvb = t["L1_attn_w_kvb"].reshape(KVR, NH, ND + VD)
    nope = wqb[:, :, :ND].transpose(1, 2, 0)
    rope = wqb[:, :, ND:]
    return {
        "x": t["L0_attn_hidden_states"].reshape(TOK, D),
        "c0": t["L0_c"].T, "c1": t["L1_c"].T,
        "wmod0": t["L0_wmod"], "wmod1": t["L1_wmod"],
        "wqkv0": np.concatenate([t["L0_attn_wq"].T, t["L0_attn_wk"].T, t["L0_attn_wv"].T], 1),
        "bqkv0": np.concatenate([t["L0_attn_bq"], t["L0_attn_bk"], t["L0_attn_bv"]])[None],
        "wffn0": np.concatenate([t["L0_ffn_base_w"].T, t["L0_ffn_A"].T, t["L0_ffn_router_w"].T], 1),
        "bffn0": t["L0_ffn_base_b"][None],
        "wexp0": t["L0_ffn_B"].transpose(0, 2, 1).reshape(E0 * R0, D),
        "wc1": np.concatenate([t["L1_attn_w_qa"], t["L1_attn_w_kva"]], 1),
        "gq1": t["L1_attn_g_qa"][None], "gk1": t["L1_attn_g_kva"][None],
        "wqn1": np.concatenate([nope, nope[:, :, P:]], 2),
        "wqr1": np.stack([rope[:P], np.concatenate([rope[P:], rope[P:]], 0)], 1),
        "wkn1": wkvb[:, :, :ND].transpose(2, 1, 0),
        "wvn1": wkvb[:, :, ND:].transpose(2, 1, 0),
        "wo1": t["L1_attn_w_o"],
        "wf1": t["L1_ffn_W"].T, "fa1": t["L1_ffn_lora_A"], "fb1": t["L1_ffn_lora_B"].T,
        "mag1": t["L1_ffn_magnitude"][None],
        **_constants(),
    }


def kernel(**inputs):
    import numpy as _np
    import concourse.bacc as _bacc
    from concourse import mybir as _mybir
    from concourse.bass_utils import run_bass_kernel_spmd as _run

    nc = _bacc.Bacc("TRN2", target_bir_lowering=False, num_devices=1)
    arrays, aps = {}, {}
    for name, v in _layout(inputs).items():
        v = _np.ascontiguousarray(v)
        arrays[f"in_{name}"] = v
        aps[name] = nc.dram_tensor(f"in_{name}", v.shape, _mybir.dt.from_np(v.dtype), kind="ExternalInput").ap()
    out = nc.dram_tensor("out_x", (TOK, D), F32, kind="ExternalOutput").ap()
    megakernel(nc, aps, out)
    r = _run(nc, [arrays], core_ids=[0])
    return r.results[0]["out_x"].reshape(B, S, D)
```

```python
from contextlib import ExitStack

import concourse.bass as bass
from concourse import mybir

P = 128
F32 = mybir.dt.float32
F32R = mybir.dt.float32r
U32 = mybir.dt.uint32
ALU = mybir.AluOpType
ACT = mybir.ActivationFunctionType
AX = mybir.AxisListType

B, S, D = 2, 512, 512
TOK = B * S
TILES = TOK // P
TPB = S // P
KC = D // P
QD = P // 32

H0, HD0 = 32, 16
PAD0 = 32
VW = HD0 + 1

R0, E0 = 64, 16
PROJ0 = D + R0 + E0
EC = E0 * R0 // P
LORA_SCALE = 32.0 / 64.0

NH, QR, KVR, RD, ND, VD = 32, 192, 64, 64, 128, 128
QREST = QR - P
CQ = QR + KVR + RD
HP = NH // 2
SCALE1 = float(ND + RD) ** -0.5
CW = KVR + 1

R1 = 32
LN_EPS = 1e-5
RMS_EPS = 1e-6
SIX = 6 * KC
SA, CA, GA, SB, CB, GB = (j * KC for j in range(6))


def bc(ap, shape):
    return ap.to_broadcast(shape)


class Chain:

    def __init__(self, eng, sem, n=0):
        self.eng, self.sem, self.n = eng, sem, n

    def __call__(self, ins):
        self.n += 1
        ins.then_inc(self.sem, 1)
        self.eng.wait_ge(self.sem, self.n)


def split_matmuls(pe, out, pairs, first=True, last=True):
    n = len(pairs)
    for i, ((xh, xl), (wh, wl)) in enumerate(pairs):
        pe.matmul(out, xh, wh, start=first and i == 0, stop=False)
        pe.matmul(out, xh, wl, start=False, stop=False)
        mm = pe.matmul(out, xl, wh, start=False, stop=last and i == n - 1)
    return mm


def megakernel(nc, a, out, stop_after=9):
    x_dram = a["x"].rearrange("(t p) d -> p t d", p=P)
    out_dram = out.rearrange("(t p) d -> p t d", p=P)

    with ExitStack() as whole:
        def sb(name, shape, dt=F32, ctx=whole):
            return ctx.enter_context(nc.sbuf_tensor(name, shape, dt))

        def sem(name):
            return whole.enter_context(nc.semaphore(name))

        bank = [whole.enter_context(nc.psum_tensor(f"bank{i}", [P, 512], F32)) for i in range(8)]

        x = sb("x_res", [P, TILES, D])
        ident = sb("ident", [P, P])
        ones = sb("ones", [P, P])
        eps = sb("eps", [P, 1])
        cs = sb("cs", [P, 2 * KC * B])
        cs_e = sb("cs_e", [P, 2 * KC * B])
        cs_s = sb("cs_s", [P, 2 * KC * B])
        mod = sb("mod", [P, SIX * B])
        gabs = sb("gabs", [P, 4 * KC * B])
        gate = sb("gate", [P, 2, B, D])
        stats = sb("stats", [P, TILES, 6])
        mv = sb("mv", [P, TILES, 2])
        rstd = sb("rstd", [P, TILES])
        mod3 = mod[:, :].rearrange("p (m b) -> p m b", b=B)
        cs4 = cs_s[:, :].rearrange("p (l k b) -> p l k b", l=2, b=B)

        x_in = sem("x_in")
        const_in = sem("const_in")
        wmod_in = [sem(f"wmod_in{j}") for j in range(6)]
        raw_in = [sem("raw_in0"), sem("raw_in1")]
        raw_free = sem("raw_free")
        stored = sem("stored")

        def load_chunks(sp, stage, chunks, base):
            for i, src in enumerate(chunks):
                n = base + i
                if n >= 2:
                    sp.wait_ge(raw_free, n - 1)
                w = 1
                for s in src.shape[1:]:
                    w *= s
                dst = stage[:, n % 2, 0:w]
                if len(src.shape) == 3:
                    dst = dst.rearrange("p (a b) -> p a b", a=src.shape[1])
                sp.dma_start(dst, src).then_inc(raw_in[n % 2], 16)

        split_hi = sem("split_hi")

        def split_act(act, stage, chunks, base):
            for i, (hi, lo) in enumerate(chunks):
                n = base + i
                w = hi.shape[-1]
                act.wait_ge(raw_in[n % 2], 16 * (n // 2 + 1))
                act.activation(hi, stage[:, n % 2, 0:w], ACT.Copy).then_inc(split_hi, 1)

        def split_dve(dve, stage, chunks, base):
            for i, (hi, lo) in enumerate(chunks):
                n = base + i
                w = hi.shape[-1]
                dve.wait_ge(split_hi, n + 1)
                dve.tensor_tensor(lo, stage[:, n % 2, 0:w], hi.bitcast(F32), ALU.subtract).then_inc(raw_free, 1)

        class Norm:

            def __init__(self, tag, shift, scale, used, ctx, used_per=1):
                self.x = sb(f"{tag}_x", [P, 2, D], F32, ctx)
                self.f = sb(f"{tag}_f", [P, KC, P], F32, ctx)
                self.h_hi = sb(f"{tag}_h_hi", [P, 2, KC, P], F32R, ctx)
                self.h_lo = sb(f"{tag}_h_lo", [P, 2, KC, P], F32R, ctx)
                self.shift, self.scale = shift, scale
                self.chain = sem(f"{tag}_chain")
                self.var = sem(f"{tag}_var")
                self.std = sem(f"{tag}_std")
                self.rstd = sem(f"{tag}_rstd")
                self.xn = sem(f"{tag}_xn")
                self.xT = sem(f"{tag}_xT")
                self.hf = sem(f"{tag}_hf")
                self.hi = sem(f"{tag}_hi")
                self.lo = sem(f"{tag}_lo")
                self.used = used
                self.used_per = used_per

            def dve_stats(self, dve):
                for t in range(TILES):
                    dve.bn_stats(stats[:, t, :], x[:, t, :]).then_inc(self.chain, 1)
                for t in range(TILES):
                    dve.wait_ge(self.chain, t + 1)
                    dve.bn_aggr(mv[:, t, :], stats[:, t, :]).then_inc(self.var, 1)
                dve.wait_ge(self.std, 1)
                dve.reciprocal(rstd[:, :], rstd[:, :]).then_inc(self.rstd, 1)

            def act_std(self, act):
                act.wait_ge(self.var, TILES)
                act.activation(rstd[:, :], mv[:, :, 1], ACT.Sqrt, bias=eps[:, 0:1]).then_inc(self.std, 1)

            def dve_xn(self, dve, t):
                if t == 0:
                    dve.wait_ge(self.rstd, 1)
                if t >= 2:
                    dve.wait_ge(self.xT, t - 1)
                dve.tensor_scalar(self.x[:, t % 2, :], x[:, t, :], mv[:, t, 0:1], rstd[:, t:t + 1],
                                  ALU.subtract, ALU.mult).then_inc(self.xn, 1)

            def pe_xT(self, pe, t, pT):
                pe.wait_ge(self.xn, t + 1)
                if t >= 1:
                    pe.wait_ge(self.hf, t)
                for c in range(KC):
                    mm = pe.transpose(pT[:, c * P:(c + 1) * P], self.x[:, t % 2, c * P:(c + 1) * P], ident[:, :])
                mm.then_inc(self.xT, 1)

            def act_h(self, act, t, pT):
                b = t // TPB
                act.wait_ge(self.xT, t + 1)
                if t >= 1:
                    act.wait_ge(self.lo, t)
                for c in range(KC):
                    a_ = act.activation(self.f[:, c, :], pT[:, c * P:(c + 1) * P], ACT.Identity,
                                        bias=mod3[:, self.shift + c, b:b + 1], scale=mod3[:, self.scale + c, b:b + 1])
                a_.then_inc(self.hf, 1)
                if t >= 2:
                    act.wait_ge(self.used, self.used_per * (t - 1))
                act.wait_ge(self.hf, t + 1)
                act.activation(self.h_hi[:, t % 2, :, :], self.f[:, :, :], ACT.Copy).then_inc(self.hi, 1)

            def dve_lo(self, dve, t):
                dve.wait_ge(self.hi, t + 1)
                dve.tensor_tensor(self.h_lo[:, t % 2, :, :], self.f[:, :, :], self.h_hi[:, t % 2, :, :].bitcast(F32),
                                  ALU.subtract).then_inc(self.lo, 1)

            def h(self, t, c):
                return (self.h_hi[:, t % 2, c, :], self.h_lo[:, t % 2, c, :])

        prefetch = whole.enter_context(ExitStack())
        stage = sb("stage_a", [P, 2, 3 * D], F32, prefetch)
        raw_e = sb("raw_e", [P, EC, D], F32, prefetch)
        raw_f = stage[:, :, :].rearrange("p a b -> p (a b)")[:, 0:KC * PROJ0].rearrange("p (k n) -> p k n", k=KC)
        mrow = raw_e[:, :, :].rearrange("p a b -> p (a b)")[0:B, 0:SIX * P]
        exp_c = sem("exp_c")
        silu = sem("silu")
        const_set = sem("const_set")
        row_ps = sem("row_ps")
        row_ev = sem("row_ev")
        mod_ps = sem("mod_ps")
        mod_done = sem("mod_done")
        mod_chain = sem("mod_chain")
        gate_ps = sem("gate_ps")
        gate_done = sem("gate_done")
        mod_steps = [0]

        def load_wmod(sp, layer, wmod):
            src = a[f"wmod{layer}"].rearrange("(k p) n -> p k n", p=P)
            for j in range(6):
                sp.dma_start(wmod[:, :, j * D:(j + 1) * D], src[:, :, j * D:(j + 1) * D]).then_inc(wmod_in[j], 16)

        def pe_rows(pe, layer, j, wmod, ps):
            pe.wait_ge(wmod_in[j], 16 * (layer + 1))
            for k in range(KC):
                mm = pe.matmul(ps[0:B, :], cs4[:, layer, k, :], wmod[:, k, j * D:(j + 1) * D],
                               start=(k == 0), stop=(k == KC - 1))
            mm.then_inc(row_ps, 1)

        def act_rows(act, layer, j, ps):
            act.wait_ge(row_ps, 6 * layer + j + 1)
            act.activation(mrow[:, j * D:(j + 1) * D], ps[0:B, :], ACT.Copy).then_inc(row_ev, 1)

        def modulation(layer, wmod=None, extra_act=None, extra_dve=None, extra_sp=None, extra_pool=None):
            with nc.Block() as block:
                @block.sync
                def _(sp):
                    if layer == 0:
                        cs_in = cs[:, :].rearrange("p (l k b) -> p l k b", l=2, b=B)
                        sp.dma_start(cs_in[:, 0], a["c0"].rearrange("(k p) b -> p k b", p=P)).then_inc(const_in, 16)
                        sp.dma_start(cs_in[:, 1], a["c1"].rearrange("(k p) b -> p k b", p=P)).then_inc(const_in, 16)
                        sp.dma_start(ident[:, :], a["ident"]).then_inc(const_in, 16)
                        load_wmod(sp, 0, wmod)
                    if extra_sp:
                        extra_sp(sp)

                @block.gpsimd
                def _(pool):
                    if extra_pool:
                        extra_pool(pool)

                @block.scalar
                def _(act):
                    if layer == 0:
                        act.wait_ge(const_in, 48)
                        act.activation(cs_e[:, :], cs[:, :], ACT.Exp, scale=-1.0).then_inc(exp_c, 1)
                        for j in range(6):
                            act_rows(act, 0, j, bank[2 + j])
                    if extra_act:
                        extra_act(act)

                @block.vector
                def _(dve):
                    link = Chain(dve, mod_chain, mod_steps[0])
                    if layer == 0:
                        dve.memset(ones[:, :], 1.0).then_inc(const_set, 1)
                        dve.memset(eps[:, :], LN_EPS).then_inc(const_set, 1)
                        dve.wait_ge(exp_c, 1)
                        link(dve.tensor_scalar_add(cs_e[:, :], cs_e[:, :], 1.0))
                        link(dve.reciprocal(cs_e[:, :], cs_e[:, :]))
                        dve.tensor_tensor(cs_s[:, :], cs[:, :], cs_e[:, :], ALU.mult).then_inc(silu, 1)
                    if extra_dve:
                        extra_dve(dve)
                    dve.wait_ge(mod_ps, layer + 1)
                    link(dve.tensor_copy(mod[:, :], bank[0][:, 0:SIX * B]))
                    w = KC * B
                    for n, g in enumerate((GA, GB)):
                        gg = mod3[:, g:g + KC, :].rearrange("p m b -> p (m b)")
                        t0, t1 = gabs[:, 2 * n * w:(2 * n + 1) * w], gabs[:, (2 * n + 1) * w:(2 * n + 2) * w]
                        link(dve.tensor_scalar(t0, gg, -1.0, None, ALU.mult))
                        link(dve.tensor_tensor(t0, t0, gg, ALU.max))
                        link(dve.tensor_scalar(t0, t0, 0.25, None, ALU.max))
                        link(dve.tensor_scalar(t1, gg, 0.0, 2.0, ALU.is_ge, ALU.mult))
                        link(dve.tensor_scalar(t1, t1, -1.0, None, ALU.add))
                        dve.tensor_tensor(gg, t0, t1, ALU.mult).then_inc(mod_done, 1)
                    link(dve.tensor_scalar_add(mod3[:, CA:CA + KC, :], mod3[:, CA:CA + KC, :], 1.0))
                    link(dve.tensor_scalar_add(mod3[:, CB:CB + KC, :], mod3[:, CB:CB + KC, :], 1.0))
                    mod_steps[0] = link.n
                    for n in range(4):
                        dve.wait_ge(gate_ps, 4 * layer + n + 1)
                        dve.tensor_copy(gate[:, n // 2, n % 2, :], bank[1 + n][:, :]).then_inc(gate_done, 1)

                @block.tensor
                def _(pe):
                    if layer == 0:
                        pe.wait_ge(silu, 1)
                        for j in range(6):
                            pe_rows(pe, 0, j, wmod, bank[2 + j])
                    for j in range(6):
                        pe.wait_ge(row_ev, 6 * layer + j + 1)
                        for m in range(j * KC, (j + 1) * KC):
                            mm = pe.transpose(bank[0][:, m * B:(m + 1) * B], mrow[:, m * P:(m + 1) * P], ident[0:B, 0:B])
                    mm.then_inc(mod_ps, 1)
                    for n, (g, b) in enumerate(((GA, 0), (GA, 1), (GB, 0), (GB, 1))):
                        pe.wait_ge(mod_done, 2 * layer + n // 2 + 1)
                        for c in range(KC):
                            mm = pe.matmul(bank[1 + n][:, c * P:(c + 1) * P],
                                           bc(mod3[:, g + c, b:b + 1], [P, P]), ident[:, :], start=True, stop=True)
                        mm.then_inc(gate_ps, 1)

        raw_n = [0]

        fsrc = a["wffn0"].rearrange("(k p) n -> p k n", p=P)
        esrc = a["wexp0"].rearrange("(k p) n -> p k n", p=P)
        ffn_in = sem("ffn_in")
        with ExitStack() as ph:
            wq_hi = sb("wqkv_hi", [P, KC, 3 * D], F32R, ph)
            wq_lo = sb("wqkv_lo", [P, KC, 3 * D], F32R, ph)
            wsrc = a["wqkv0"].rearrange("(k p) n -> p k n", p=P)
            chunks = [wsrc[:, k, :] for k in range(KC)]
            parts = [(wq_hi[:, k, :], wq_lo[:, k, :]) for k in range(KC)]
            base = raw_n[0]
            bias0 = sb("bias0", [P, 3 * D], F32, ph)
            qk = sb("qk", [P, 2, H0, PAD0], F32, ph)
            q_bd = sb("q_bd", [P, 32, P], F32, ph)
            bias_in = sem("bias_in")
            pad_set = sem("pad_set")
            qkv_ready = sem("qkv_ready")
            nrm = Norm("n0", SA, CA, used=qkv_ready, ctx=ph, used_per=3)

            def load_start(sp):
                for t in range(TILES):
                    sp.dma_start(x[:, t, :], x_dram[:, t, :]).then_inc(x_in, 16)
                load_chunks(sp, stage, chunks, base)
                sp.dma_start(bias0[:, :], bc(a["bqkv0"], [P, 3 * D])).then_inc(bias_in, 16)

            def act_start(act):
                nrm.act_std(act)
                split_act(act, stage, parts, base)

            def dve_start(dve):
                dve.wait_ge(x_in, 16 * TILES)
                nrm.dve_stats(dve)
                split_dve(dve, stage, parts, base)

            def pad_start(pool):
                pool.memset(qk[:, :, :, :], 0.0).then_inc(pad_set, 1)
                pool.memset(q_bd[:, :, :], 0.0).then_inc(pad_set, 1)

            with ExitStack() as ms:
                wmod0 = sb("wmod0", [P, KC, 6 * D], F32, ms)
                modulation(0, wmod0, extra_sp=load_start, extra_act=act_start, extra_dve=dve_start,
                           extra_pool=pad_start)
            raw_n[0] += len(chunks)

            v_tok = sb("v_tok", [P, D], F32, ph)
            qT = sb("qT", [P, 32, H0], F32, ph)
            kT = sb("kT", [P, 2, 32, H0], F32, ph)
            e_bd = sb("e_bd", [P, 32, P], F32, ph)
            vT = sb("vT", [P, 3, 32, VW], F32, ph)
            s_max = sb("s_max", [P, 32], F32, ph)
            s_sub = sb("s_sub", [P, 32, H0], F32, ph)
            e_s = sb("e_s", [P, 32, H0], F32, ph)
            eT = sb("eT", [P, 32, H0], F32, ph)
            o_rec = sb("o_rec", [P, 32], F32, ph)
            o_n = sb("o_n", [P, HD0, 32], F32, ph)
            o_tok = sb("o_tok", [P, D], F32, ph)
            o_g = sb("o_g", [P, D], F32, ph)
            qkv_ev = sem("qkv_ev")
            turned = sem("turned")
            qbd_done = sem("qbd_done")
            s_ps = sem("s_ps")
            max_done = sem("max_done")
            sub_done = sem("sub_done")
            exp_done = sem("exp_done")
            eT_done = sem("eT_done")
            ebd_done = sem("ebd_done")
            o_ps = sem("o_ps")
            rec_done = sem("rec_done")
            on_done = sem("on_done")
            otok_done = sem("otok_done")
            og_done = sem("og_done")
            x1_done = sem("x1_done")
            pT, q_ps, k_ps, v_ps = bank[0], bank[1], bank[2], bank[3]
            s_bank, o_bank = bank[4:6], bank[6:8]
            HB = 16
            OW = HB * VW

            def s_view(j):
                return s_bank[j][:, :].rearrange("p (n h) -> p n h", h=H0)

            def o_view(j):
                return o_bank[j][:, 0:OW].rearrange("p (n d) -> p n d", d=VW)

            with nc.Block() as block:
                @block.sync
                def _(sp):
                    sp.dma_start(raw_f, fsrc).then_inc(ffn_in, 16)
                    sp.dma_start(raw_e[:, 0:4, :], esrc[:, 0:4, :]).then_inc(ffn_in, 16)
                    sp.dma_start(raw_e[:, 4:8, :], esrc[:, 4:8, :]).then_inc(ffn_in, 16)

                @block.gpsimd
                def _(pool):
                    pool.memset(vT[:, :, :, :], 1.0).then_inc(pad_set, 1)
                    pool.memset(e_bd[:, :, :], 0.0).then_inc(pad_set, 1)
                    for t in range(TILES):
                        pool.wait_ge(otok_done, t + 1)
                        if t >= 1:
                            pool.wait_ge(x1_done, t)
                        pool.tensor_tensor(o_g[:, :], o_tok[:, :], gate[:, 0, t // TPB, :], ALU.mult).then_inc(og_done, 1)
                        pool.wait_ge(og_done, t + 1)
                        pool.tensor_tensor(x[:, t, :], x[:, t, :], o_g[:, :], ALU.add).then_inc(x1_done, 1)

                @block.scalar
                def _(act):
                    def q_blocks(t):
                        act.wait_ge(turned, 3 * t + 1)
                        if t >= 1:
                            act.wait_ge(s_ps, 2 * t)
                        for g in range(QD):
                            r = slice(32 * g, 32 * g + 32)
                            a_ = act.activation(q_bd[r, :, r], qT[r, :, :], ACT.Copy)
                        a_.then_inc(qbd_done, 1)

                    def exps(t):
                        act.wait_ge(sub_done, 2 * t + 2)
                        if t >= 1:
                            act.wait_ge(eT_done, t)
                        act.activation(e_s[:, :, :], s_sub[:, :, :], ACT.Exp, scale=float(HD0) ** -0.5).then_inc(exp_done, 1)

                    def e_blocks(t):
                        act.wait_ge(eT_done, t + 1)
                        if t >= 1:
                            act.wait_ge(o_ps, 2 * t)
                        else:
                            act.wait_ge(pad_set, 4)
                        for g in range(QD):
                            r = slice(32 * g, 32 * g + 32)
                            a_ = act.activation(e_bd[r, :, r], eT[r, :, :], ACT.Copy)
                        a_.then_inc(ebd_done, 1)

                    nrm.act_h(act, 0, pT)
                    for t in range(TILES + 1):
                        if t >= 2:
                            e_blocks(t - 2)
                        if t + 1 < TILES:
                            nrm.act_h(act, t + 1, pT)
                        if t < TILES:
                            q_blocks(t)
                        if t >= 1:
                            exps(t - 1)
                    e_blocks(TILES - 1)

                @block.vector
                def _(dve):
                    nrm.dve_xn(dve, 0)
                    nrm.dve_lo(dve, 0)
                    dve.wait_ge(bias_in, 16)

                    def q_turn(t):
                        dve.wait_ge(qkv_ready, 3 * t + 1)
                        if t >= 1:
                            dve.wait_ge(turned, 3 * t - 2)
                        dve.tensor_tensor(qk[:, 0, :, 0:HD0], q_ps[:, :].rearrange("p (h d) -> p h d", d=HD0),
                                          bias0[:, 0:D].rearrange("p (h d) -> p h d", d=HD0),
                                          ALU.add).then_inc(qkv_ev, 1)
                        dve.wait_ge(qkv_ev, 3 * t + 1)
                        if t >= 1:
                            dve.wait_ge(qbd_done, t)
                        dve.transpose(qT[:, :, :].rearrange("p n h -> p h n"), qk[:, 0, :, :]).then_inc(turned, 1)

                    def k_turn(t):
                        dve.wait_ge(qkv_ready, 3 * t + 2)
                        if t >= 1:
                            dve.wait_ge(turned, 3 * t - 1)
                        dve.tensor_tensor(qk[:, 1, :, 0:HD0], k_ps[:, :].rearrange("p (h d) -> p h d", d=HD0),
                                          bias0[:, D:2 * D].rearrange("p (h d) -> p h d", d=HD0),
                                          ALU.add).then_inc(qkv_ev, 1)
                        dve.wait_ge(qkv_ev, 3 * t + 2)
                        if t >= 2:
                            dve.wait_ge(s_ps, 2 * (t - 1))
                        dve.transpose(kT[:, t % 2, :, :].rearrange("p n h -> p h n"), qk[:, 1, :, :]).then_inc(turned, 1)

                    def v_turn(t):
                        dve.wait_ge(qkv_ready, 3 * t + 3)
                        if t >= 1:
                            dve.wait_ge(turned, 3 * t)
                        dve.tensor_tensor(v_tok[:, :], v_ps[:, :], bias0[:, 2 * D:3 * D], ALU.add).then_inc(qkv_ev, 1)
                        dve.wait_ge(qkv_ev, 3 * t + 3)
                        if t == 0:
                            dve.wait_ge(pad_set, 3)
                        if t >= 3:
                            dve.wait_ge(o_ps, 2 * (t - 2))
                        dve.transpose(vT[:, t % 3, :, 0:HD0].rearrange("p n d -> p d n"),
                                      v_tok[:, :].rearrange("p (h d) -> p d h", d=HD0)).then_inc(turned, 1)

                    def softmax(t, j):
                        dve.wait_ge(s_ps, 2 * t + j + 1)
                        if t >= 1:
                            dve.wait_ge(sub_done, 2 * t - 1 + j)
                        dve.tensor_reduce(s_max[:, HB * j:HB * (j + 1)], s_view(j), AX.X, ALU.max).then_inc(max_done, 1)
                        if t >= 1:
                            dve.wait_ge(exp_done, t)
                        dve.wait_ge(max_done, 2 * t + j + 1)
                        dve.tensor_tensor(s_sub[:, HB * j:HB * (j + 1), :], s_view(j),
                                          bc(s_max[:, HB * j:HB * (j + 1)].unsqueeze(2), [P, HB, H0]),
                                          ALU.subtract).then_inc(sub_done, 1)

                    def turn(t):
                        dve.wait_ge(exp_done, t + 1)
                        if t >= 1:
                            dve.wait_ge(ebd_done, t)
                        dve.transpose(eT[:, :, :].rearrange("p n h -> p (n h)"),
                                      e_s[:, :, :].rearrange("p n h -> p (n h)")).then_inc(eT_done, 1)

                    def finish(t):
                        for j in range(2):
                            dve.wait_ge(o_ps, 2 * t + j + 1)
                            if t >= 1:
                                dve.wait_ge(on_done, 2 * t - 1 + j)
                            dve.reciprocal(o_rec[:, HB * j:HB * (j + 1)], o_view(j)[:, :, HD0]).then_inc(rec_done, 1)
                        if t >= 1:
                            dve.wait_ge(otok_done, t)
                        for j in range(2):
                            dve.wait_ge(rec_done, 2 * t + j + 1)
                            dve.tensor_tensor(o_n[:, :, HB * j:HB * (j + 1)].rearrange("p d n -> p n d"),
                                              o_view(j)[:, :, 0:HD0],
                                              bc(o_rec[:, HB * j:HB * (j + 1)].unsqueeze(2), [P, HB, HD0]),
                                              ALU.mult).then_inc(on_done, 1)
                        dve.wait_ge(on_done, 2 * t + 2)
                        if t >= 1:
                            dve.wait_ge(og_done, t)
                        dve.transpose(o_tok[:, :].rearrange("p (h d) -> p d h", d=HD0), o_n[:, :, :]).then_inc(otok_done, 1)

                    for t in range(TILES + 3):
                        if 1 <= t <= TILES:
                            v_turn(t - 1)
                        if t >= 3:
                            finish(t - 3)
                        if t + 1 < TILES:
                            nrm.dve_xn(dve, t + 1)
                        if 1 <= t <= TILES:
                            softmax(t - 1, 0)
                        if t < TILES:
                            q_turn(t)
                        if 1 <= t <= TILES:
                            softmax(t - 1, 1)
                        if t + 1 < TILES:
                            nrm.dve_lo(dve, t + 1)
                        if t < TILES:
                            k_turn(t)
                        if 1 <= t <= TILES:
                            turn(t - 1)

                @block.tensor
                def _(pe):
                    BIG = 3 * 3 * KC

                    def project(t, i):
                        j, c, term = i // (3 * KC), i // 3 % KC, i % 3
                        ps = (q_ps, k_ps, v_ps)[j]
                        if i == 0:
                            pe.wait_ge(nrm.lo, t + 1)
                        if i % (3 * KC) == 0 and t >= 1:
                            pe.wait_ge(qkv_ev, 3 * t - 2 + j)
                        (h_hi, h_lo), cols = nrm.h(t, c), slice(j * D, (j + 1) * D)
                        x_, w_ = ((h_hi, wq_hi), (h_hi, wq_lo), (h_lo, wq_hi))[term]
                        mm = pe.matmul(ps[:, :], x_, w_[:, c, cols], start=(i % (3 * KC) == 0),
                                       stop=(i % (3 * KC) == 3 * KC - 1))
                        if i % (3 * KC) == 3 * KC - 1:
                            mm.then_inc(qkv_ready, 1)

                    def scores(t, n):
                        if n == 0:
                            pe.wait_ge(qbd_done, t + 1)
                            pe.wait_ge(turned, 3 * t + 2)
                        if n % HB == 0 and t >= 1:
                            pe.wait_ge(sub_done, 2 * t - 1 + n // HB)
                        mm = pe.matmul(s_view(n // HB)[:, n % HB, :], q_bd[:, n, :], kT[:, t % 2, n, :],
                                       start=True, stop=True)
                        if n % HB == HB - 1:
                            mm.then_inc(s_ps, 1)

                    def context(t, n):
                        if n == 0:
                            pe.wait_ge(ebd_done, t + 1)
                            pe.wait_ge(turned, 3 * t + 3)
                        if n % HB == 0 and t >= 1:
                            pe.wait_ge(on_done, 2 * t - 1 + n // HB)
                        mm = pe.matmul(o_view(n // HB)[:, n % HB, :], e_bd[:, n, :], vT[:, t % 3, n, :],
                                       start=True, stop=True)
                        if n % HB == HB - 1:
                            mm.then_inc(o_ps, 1)

                    nrm.pe_xT(pe, 0, pT)
                    for t in range(TILES + 2):
                        for part in range(2):
                            if t < TILES:
                                for i in range(part * BIG // 2, (part + 1) * BIG // 2):
                                    project(t, i)
                            if part == 0 and 1 <= t <= TILES:
                                for n in range(32):
                                    scores(t - 1, n)
                            if part == 1 and t >= 2:
                                for n in range(32):
                                    context(t - 2, n)
                            if part == 0 and t + 1 < TILES:
                                nrm.pe_xT(pe, t + 1, pT)

        if stop_after == 0:
            with nc.Block() as block:
                @block.sync
                def _(sp):
                    sp.dma_start(out_dram, x[:, :, :]).then_inc(stored, 16)
                    sp.wait_ge(stored, 16)
            return

        with ExitStack() as ph:
            wmod1 = sb("wmod1", [P, KC, 6 * D], F32, ph)
            wf_hi = sb("wf_hi", [P, KC, PROJ0], F32R, ph)
            wf_lo = sb("wf_lo", [P, KC, PROJ0], F32R, ph)
            we_hi = sb("we_hi", [P, EC, D], F32R, ph)
            we_lo = sb("we_lo", [P, EC, D], F32R, ph)
            biasf = sb("biasf", [P, D], F32, ph)
            iota = sb("iota", [P, E0], F32, ph)
            top = sb("top", [P, 8], F32, ph)
            topi = sb("topi", [P, 8], U32, ph)
            topf = sb("topf", [P, 2], F32, ph)
            rp = sb("rp", [P, E0], F32, ph)
            rm = sb("rm", [P, 1], F32, ph)
            rsum = sb("rsum", [P, 1], F32, ph)
            den = sb("den", [P, 4], F32, ph)
            c1 = sb("c1", [P, E0], F32, ph)
            comb = sb("comb", [P, E0], F32, ph)
            z = sb("z", [P, 2, E0, R0], F32, ph)
            z_hi = sb("z_hi", [P, 2, 512], F32R, ph)
            z_lo = sb("z_lo", [P, 2, 512], F32R, ph)
            f_sum = sb("f_sum", [P, D], F32, ph)
            f_g = sb("f_g", [P, D], F32, ph)
            bias_in = sem("biasf_in")
            chain = sem("router_chain")
            base_ps = sem("base_ps")
            rexp_done = sem("rexp_done")
            rmax_done = sem("rmax_done")
            z_done = sem("z_done")
            zT_ps = sem("zT_ps")
            zhi_done = sem("zhi_done")
            zlo_done = sem("zlo_done")
            f_ps = sem("f_ps")
            fsum_done = sem("fsum_done")
            fg_done = sem("fg_done")
            x2_done = sem("x2_done")
            nrm = Norm("n1", SB, CB, used=base_ps, ctx=ph, used_per=2)
            split2_hi = sem("split2_hi")
            split2_lo = sem("split2_lo")
            pT = bank[0]
            y_bank, r_bank, z_bank, m_bank = bank[1:3], bank[3:5], bank[5:7], bank[7]
            parts = ([(raw_f[:, k, :], wf_hi[:, k, :], wf_lo[:, k, :]) for k in range(KC)]
                     + [(raw_e[:, k, :], we_hi[:, k, :], we_lo[:, k, :]) for k in range(EC)])

            with nc.Block() as block:
                @block.sync
                def _(sp):
                    sp.dma_start(biasf[:, :], bc(a["bffn0"], [P, D])).then_inc(bias_in, 16)
                    sp.dma_start(iota[:, :], a["iota"]).then_inc(bias_in, 16)
                    load_wmod(sp, 1, wmod1)

                @block.gpsimd
                def _(pool):
                    for t in range(TILES):
                        pool.wait_ge(fsum_done, t + 1)
                        if t >= 1:
                            pool.wait_ge(x2_done, t)
                        pool.tensor_tensor(f_g[:, :], f_sum[:, :], gate[:, 1, t // TPB, :], ALU.mult).then_inc(fg_done, 1)
                        pool.wait_ge(fg_done, t + 1)
                        pool.tensor_tensor(x[:, t, :], x[:, t, :], f_g[:, :], ALU.add).then_inc(x2_done, 1)

                @block.scalar
                def _(act):
                    nrm.act_std(act)
                    act.wait_ge(ffn_in, 48)
                    for raw, hi, lo in parts[:KC]:
                        act.activation(hi, raw, ACT.Copy).then_inc(split2_hi, 1)
                    nrm.act_h(act, 0, pT)
                    for raw, hi, lo in parts[KC:]:
                        act.activation(hi, raw, ACT.Copy).then_inc(split2_hi, 1)
                    for t in range(TILES + 1):
                        if t >= 1:
                            for j in range(2):
                                n = 2 * (t - 1) + j
                                act.wait_ge(zT_ps, n + 1)
                                if n >= 2:
                                    act.wait_ge(f_ps, n - 1)
                                act.activation(z_hi[:, j, :], z_bank[j][:, :], ACT.Copy).then_inc(zhi_done, 1)
                        if t + 1 < TILES:
                            nrm.act_h(act, t + 1, pT)
                        if t < TILES:
                            act.wait_ge(rmax_done, t + 1)
                            if t >= 1:
                                act.wait_ge(z_done, t)
                            act.activation(rp[:, :], r_bank[t % 2][:, R0:R0 + E0], ACT.Exp, bias=rm[:, 0:1],
                                           accum_out=rsum[:, 0:1]).then_inc(rexp_done, 1)
                        if 1 <= t <= 6:
                            act.wait_ge(split2_lo, KC + EC)
                            act_rows(act, 1, t - 1, m_bank)

                @block.vector
                def _(dve):
                    nrm.dve_stats(dve)
                    nrm.dve_xn(dve, 0)
                    nrm.dve_xn(dve, 1)
                    for i, (raw, hi, lo) in enumerate(parts):
                        if i == KC:
                            nrm.dve_lo(dve, 0)
                        dve.wait_ge(split2_hi, i + 1)
                        dve.tensor_tensor(lo, raw, hi.bitcast(F32), ALU.subtract).then_inc(split2_lo, 1)
                    dve.wait_ge(bias_in, 32)
                    link = Chain(dve, chain)

                    def route(t):
                        rb = r_bank[t % 2]
                        dve.wait_ge(base_ps, 2 * t + 1)
                        dve.tensor_reduce(rm[:, :], rb[:, R0:R0 + E0], AX.X, ALU.max, negate=True).then_inc(rmax_done, 1)
                        dve.wait_ge(rexp_done, t + 1)
                        link(dve.max(top[:, :], rp[:, :]))
                        dve.tensor_scalar(den[:, 0:1], rsum[:, :], 1e-6, None, ALU.mult)
                        dve.tensor_tensor(den[:, 1:2], top[:, 0:1], top[:, 1:2], ALU.add)
                        link(dve.max_index(topi[:, :], top[:, :], rp[:, :]))
                        dve.tensor_tensor(den[:, 2:3], den[:, 0:1], den[:, 1:2], ALU.add)
                        link(dve.tensor_copy(topf[:, :], topi[:, 0:2]))
                        link(dve.reciprocal(den[:, 3:4], den[:, 2:3]))
                        link(dve.tensor_scalar(top[:, 0:2], top[:, 0:2], den[:, 3:4], LORA_SCALE, ALU.mult, ALU.mult))
                        dve.tensor_scalar(c1[:, :], iota[:, :], topf[:, 0:1], top[:, 0:1], ALU.is_equal, ALU.mult)
                        link(dve.tensor_scalar(comb[:, :], iota[:, :], topf[:, 1:2], top[:, 1:2], ALU.is_equal, ALU.mult))
                        link(dve.tensor_tensor(comb[:, :], comb[:, :], c1[:, :], ALU.add))
                        if t >= 2:
                            dve.wait_ge(zT_ps, 2 * (t - 1))
                        dve.tensor_tensor(z[:, t % 2, :, :], bc(rb[:, 0:R0].unsqueeze(1), [P, E0, R0]),
                                          bc(comb[:, :].unsqueeze(2), [P, E0, R0]), ALU.mult).then_inc(z_done, 1)

                    for t in range(TILES + 2):
                        if 1 <= t <= TILES:
                            for j in range(2):
                                n = 2 * (t - 1) + j
                                dve.wait_ge(zhi_done, n + 1)
                                if n >= 2:
                                    dve.wait_ge(f_ps, n - 1)
                                dve.tensor_tensor(z_lo[:, j, :], z_bank[j][:, :], z_hi[:, j, :].bitcast(F32),
                                                  ALU.subtract).then_inc(zlo_done, 1)
                        if t >= 2:
                            dve.wait_ge(f_ps, 2 * (t - 1))
                            if t >= 3:
                                dve.wait_ge(fg_done, t - 2)
                            dve.tensor_tensor(f_sum[:, :], y_bank[t % 2][:, :], biasf[:, :],
                                              ALU.add).then_inc(fsum_done, 1)
                        if t + 1 < TILES:
                            nrm.dve_lo(dve, t + 1)
                        if t + 2 < TILES:
                            nrm.dve_xn(dve, t + 2)
                        if t < TILES:
                            route(t)

                @block.tensor
                def _(pe):
                    def project(t):
                        pe.wait_ge(nrm.lo, t + 1)
                        if t >= 2:
                            pe.wait_ge(z_done, t - 1)
                        split_matmuls(pe, r_bank[t % 2][:, 0:R0 + E0], [
                            (nrm.h(t, c), (wf_hi[:, c, D:PROJ0], wf_lo[:, c, D:PROJ0]))
                            for c in range(KC)]).then_inc(base_ps, 1)
                        if t >= 2:
                            pe.wait_ge(fsum_done, t - 1)
                        split_matmuls(pe, y_bank[t % 2][:, :], [
                            (nrm.h(t, c), (wf_hi[:, c, 0:D], wf_lo[:, c, 0:D])) for c in range(KC)],
                            last=False).then_inc(base_ps, 1)

                    def turn(t):
                        pe.wait_ge(z_done, t + 1)
                        for j in range(2):
                            if t >= 1:
                                pe.wait_ge(zlo_done, 2 * t - 1 + j)
                            for c in range(4):
                                e = 2 * (4 * j + c)
                                mm = pe.transpose(z_bank[j][:, c * P:(c + 1) * P],
                                                  z[:, t % 2, e:e + 2, :].rearrange("p e r -> p (e r)"), ident[:, :])
                            mm.then_inc(zT_ps, 1)

                    def experts(t):
                        if t == 0:
                            pe.wait_ge(split2_lo, KC + EC)
                        for j in range(2):
                            pe.wait_ge(zlo_done, 2 * t + j + 1)
                            mm = split_matmuls(pe, y_bank[t % 2][:, :], [
                                ((z_hi[:, j, c * P:(c + 1) * P], z_lo[:, j, c * P:(c + 1) * P]),
                                 (we_hi[:, 4 * j + c, :], we_lo[:, 4 * j + c, :])) for c in range(4)],
                                first=False, last=(j == 1))
                            mm.then_inc(f_ps, 1)

                    nrm.pe_xT(pe, 0, pT)
                    pe.wait_ge(split2_lo, KC)
                    for t in range(TILES + 1):
                        if t >= 1:
                            turn(t - 1)
                        if t + 1 < TILES:
                            nrm.pe_xT(pe, t + 1, pT)
                        if t < TILES:
                            project(t)
                        if t >= 1:
                            experts(t - 1)
                        if 1 <= t <= 6:
                            if t >= 2:
                                pe.wait_ge(row_ev, 6 + t - 1)
                            pe_rows(pe, 1, t - 1, wmod1, m_bank)

        if stop_after == 1:
            with nc.Block() as block:
                @block.sync
                def _(sp):
                    sp.dma_start(out_dram, x[:, :, :]).then_inc(stored, 16)
                    sp.wait_ge(stored, 16)
            return

        modulation(1)
        prefetch.close()

        with ExitStack() as ph:
            wq_all = sb("wq_all", [P, NH, 2, P], F32, ph)
            wb_all = sb("wb_all", [P, HP, D], F32, ph)
            xk_hi = sb("xk_hi", [P, 3, TOK], F32R, ph)
            xk_lo = sb("xk_lo", [P, 2, TOK], F32R, ph)
            c_hi = sb("c_hi", [P, TILES, 3 * KVR], F32R, ph)
            c_lo = sb("c_lo", [P, TILES, 3 * KVR], F32R, ph)
            cosq = sb("cosq", [P, S], F32, ph)
            sinq = sb("sinq", [P, S], F32, ph)
            rot_in = sem("rot_in")

            with ExitStack() as pr:
                HPC = 4
                stage = sb("stage_c", [P, 2, CQ], F32, pr)
                wc_hi = sb("wc_hi", [P, KC, CQ], F32R, pr)
                wc_lo = sb("wc_lo", [P, KC, CQ], F32R, pr)
                wqn = sb("wqn", [P, 2, HPC, 2 * P], F32, pr)
                wkn = sb("wkn", [P, NH, KVR], F32, pr)
                wvn = sb("wvn", [P, NH, KVR], F32, pr)
                wo = sb("wo", [P, 2, HPC, D], F32, pr)
                gq = sb("gq", [P, QR], F32, pr)
                gk = sb("gk", [P, KVR], F32, pr)
                cosk = sb("cosk", [P, TPB, RD], F32, pr)
                sink = sb("sink", [P, TPB, RD], F32, pr)
                sq = sb("sq", [P, QR], F32, pr)
                ssq = sb("ssq", [P, 2, 2], F32, pr)
                rms = sb("rms", [P, 2, 2], F32, pr)
                qn = sb("qn", [P, 2, 2 * P], F32, pr)
                kk = sb("kk", [P, 2, P], F32, pr)
                ra = sb("ra", [P, RD], F32, pr)
                rb = sb("rb", [P, RD], F32, pr)
                small_in = sem("small_in")
                wqn_in = [sem("wqn_in0"), sem("wqn_in1")]
                wo_in = [sem("wo_in0"), sem("wo_in1")]
                ab_ps = sem("ab_ps")
                ab_ev = sem("ab_ev")
                c_ps = sem("c_ps")
                sq_done = sem("sq_done")
                ssq_done = sem("ssq_done")
                rms_done = sem("rms_done")
                c_set = sem("c_set")
                chain = sem("rms_chain")
                kk_done = sem("kk_done")
                xkT_ps = sem("xkT_ps")
                xkhi_done = sem("xkhi_done")
                xklo_done = sem("xklo_done")
                nrm = Norm("n2", SA, CA, used=c_ps, ctx=pr)
                pT, c_bank, k_bank = bank[0], bank[1:3], bank[3:5]
                a_bank, b_bank = bank[5], bank[6:8]
                csrc = a["wc1"].rearrange("(k p) n -> p k n", p=P)
                chunks = [csrc[:, k, :] for k in range(KC)]
                parts = [(wc_hi[:, k, :], wc_lo[:, k, :]) for k in range(KC)]
                base = raw_n[0]
                raw_n[0] += len(chunks)
                split_c = base + len(chunks)
                GROUPS = NH // HPC
                STEPS = 1 + HPC // 2

                with nc.Block() as block:
                    @block.sync
                    def _(sp):
                        load_chunks(sp, stage, chunks, base)
                        sp.dma_start(gq[:, :], bc(a["gq1"], [P, QR])).then_inc(small_in, 16)
                        sp.dma_start(gk[:, :], bc(a["gk1"], [P, KVR])).then_inc(small_in, 16)
                        sp.dma_start(cosk[:, :, :], a["cosk"]).then_inc(small_in, 16)
                        sp.dma_start(sink[:, :, :], a["sink"]).then_inc(small_in, 16)
                        sp.dma_start(wkn[:, :, :], a["wkn1"]).then_inc(small_in, 16)
                        sp.dma_start(wvn[:, :, :], a["wvn1"]).then_inc(small_in, 16)
                        for g in range(GROUPS):
                            if g >= 2:
                                sp.wait_ge(ab_ps, STEPS * (g - 1))
                            hs = slice(g * HPC, (g + 1) * HPC)
                            sp.dma_start(wqn[:, g % 2, :, :], a["wqn1"][hs].rearrange("h n m -> n h m")).then_inc(wqn_in[g % 2], 16)
                            sp.dma_start(wo[:, g % 2, :, :],
                                         a["wo1"].rearrange("(h v) n -> v h n", v=VD)[:, hs, :]).then_inc(wo_in[g % 2], 16)
                        for c in range(2):
                            sp.dma_start(wq_all[:, :, c, KVR:P], a["wqr1"][:, c]).then_inc(rot_in, 16)
                        sp.dma_start(cosq[:, :], a["cosq"]).then_inc(rot_in, 16)
                        sp.dma_start(sinq[:, :], a["sinq"]).then_inc(rot_in, 16)
                        sp.wait_ge(rot_in, 64)

                    @block.scalar
                    def _(act):
                        nrm.act_std(act)
                        split_act(act, stage, parts, base)
                        nrm.act_h(act, 0, pT)
                        for t in range(TILES + 1):
                            if t + 1 < TILES:
                                nrm.act_h(act, t + 1, pT)
                            if t < TILES:
                                act.wait_ge(c_ps, t + 1)
                                if t >= 1:
                                    act.wait_ge(sq_done, 2 * t)
                                if t >= 2:
                                    act.wait_ge(rms_done, t - 1)
                                cb = c_bank[t % 2]
                                act.activation(sq[:, 0:QR], cb[:, 0:QR], ACT.Square,
                                               accum_out=ssq[:, t % 2, 0:1]).then_inc(sq_done, 1)
                                act.wait_ge(sq_done, 2 * t + 1)
                                act.activation(sq[:, 0:KVR], cb[:, QR:QR + KVR], ACT.Square,
                                               accum_out=ssq[:, t % 2, 1:2]).then_inc(sq_done, 1)
                                act.wait_ge(sq_done, 2 * t + 2)
                                act.activation(rms[:, t % 2, 0:1], ssq[:, t % 2, 0:1], ACT.Sqrt,
                                               scale=1.0 / QR).then_inc(ssq_done, 1)
                                act.activation(rms[:, t % 2, 1:2], ssq[:, t % 2, 1:2], ACT.Sqrt,
                                               scale=1.0 / KVR).then_inc(ssq_done, 1)
                            if t >= 1:
                                act.wait_ge(xkT_ps, t)
                                ts = slice((t - 1) * P, t * P)
                                act.activation(xk_hi[:, :, ts],
                                               k_bank[(t - 1) % 2][:, 0:3 * P].rearrange("p (c n) -> p c n", c=3),
                                               ACT.Copy).then_inc(xkhi_done, 1)
                        for g in range(GROUPS):
                            act.wait_ge(ab_ps, STEPS * g + 1)
                            act.activation(wq_all[:, g * HPC:(g + 1) * HPC, :, 0:KVR],
                                           a_bank[:, :].rearrange("p (h c n) -> p h c n", h=HPC, c=2),
                                           ACT.Copy).then_inc(ab_ev, 1)
                            for q in range(HPC // 2):
                                act.wait_ge(ab_ps, STEPS * g + q + 2)
                                act.activation(wb_all[:, g * HPC // 2 + q, :], b_bank[q % 2][:, :],
                                               ACT.Copy).then_inc(ab_ev, 1)

                    @block.vector
                    def _(dve):
                        nrm.dve_stats(dve)
                        split_dve(dve, stage, parts, base)
                        dve.memset(c_hi[:, :, :].bitcast(F32), 0.0).then_inc(c_set, 1)
                        dve.memset(c_lo[:, :, :].bitcast(F32), 0.0).then_inc(c_set, 1)
                        dve.wait_ge(c_set, 2)
                        nrm.dve_xn(dve, 0)
                        nrm.dve_lo(dve, 0)
                        dve.wait_ge(small_in, 96)
                        link = Chain(dve, chain)
                        for t in range(TILES + 1):
                            if t + 1 < TILES:
                                nrm.dve_xn(dve, t + 1)
                                nrm.dve_lo(dve, t + 1)
                            if t < TILES:
                                cb, s2 = c_bank[t % 2], t % 2
                                r0, r1 = rms[:, s2, 0:1], rms[:, s2, 1:2]
                                dve.wait_ge(ssq_done, 2 * t + 2)
                                link(dve.tensor_scalar_add(rms[:, s2, :], rms[:, s2, :], RMS_EPS))
                                link(dve.reciprocal(rms[:, s2, :], rms[:, s2, :]))
                                dve.tensor_tensor(ra[:, :], cb[:, QR + KVR:CQ], cosk[:, t % TPB, :], ALU.mult)
                                dve.tensor_tensor(rb[:, 0:32], cb[:, CQ - 32:CQ], sink[:, t % TPB, 32:RD], ALU.mult)
                                link(dve.tensor_tensor(rb[:, 32:RD], cb[:, QR + KVR:CQ - 32], sink[:, t % TPB, 0:32], ALU.mult))
                                if t >= 2:
                                    dve.wait_ge(xkT_ps, t - 1)
                                dve.scalar_tensor_tensor(qn[:, s2, 0:QR], cb[:, 0:QR], r0, gq[:, :], ALU.mult, ALU.mult)
                                dve.scalar_tensor_tensor(qn[:, s2, QR:2 * P], cb[:, P:QR], r0, gq[:, P:QR], ALU.mult, ALU.mult)
                                link(dve.scalar_tensor_tensor(kk[:, s2, 0:KVR], cb[:, QR:QR + KVR], r1, gk[:, :],
                                                              ALU.mult, ALU.mult))
                                link(dve.tensor_copy(c_hi[:, t, KVR:2 * KVR], kk[:, s2, 0:KVR]))
                                dve.tensor_tensor(c_lo[:, t, KVR:2 * KVR], kk[:, s2, 0:KVR],
                                                  c_hi[:, t, KVR:2 * KVR].bitcast(F32), ALU.subtract)
                                dve.tensor_tensor(kk[:, s2, KVR:P], ra[:, :], rb[:, :], ALU.add).then_inc(kk_done, 1)
                                dve.wait_ge(kk_done, t + 1)
                                dve.tensor_scalar_add(ssq[:, s2, :], ssq[:, s2, :], 0.0).then_inc(rms_done, 1)
                            if t >= 1:
                                kb = k_bank[(t - 1) % 2]
                                ts = slice((t - 1) * P, t * P)
                                dve.wait_ge(xkhi_done, t)
                                dve.tensor_tensor(xk_lo[:, :, ts],
                                                  kb[:, 0:3 * P].rearrange("p (c n) -> p c n", c=3)[:, 0:3:2, :],
                                                  xk_hi[:, 0:3:2, ts].bitcast(F32), ALU.subtract)
                                dve.tensor_tensor(xk_hi[QREST:P, 1, ts], kb[QREST:P, P:2 * P],
                                                  xk_hi[QREST:P, 1, ts].bitcast(F32), ALU.subtract).then_inc(xklo_done, 1)

                    @block.tensor
                    def _(pe):
                        def turn(t):
                            pe.wait_ge(kk_done, t + 1)
                            if t >= 2:
                                pe.wait_ge(xklo_done, t - 1)
                            kb = k_bank[t % 2]
                            pe.transpose(kb[:, 0:P], qn[:, t % 2, 0:P], ident[:, :])
                            pe.transpose(kb[:, P:2 * P], qn[:, t % 2, P:2 * P], ident[:, :])
                            pe.transpose(kb[:, 2 * P:3 * P], kk[:, t % 2, :], ident[:, :]).then_inc(xkT_ps, 1)

                        nrm.pe_xT(pe, 0, pT)
                        pe.wait_ge(raw_free, split_c)
                        for t in range(TILES + 1):
                            if t + 1 < TILES:
                                nrm.pe_xT(pe, t + 1, pT)
                            if t < TILES:
                                pe.wait_ge(nrm.lo, t + 1)
                                if t >= 2:
                                    pe.wait_ge(rms_done, t - 1)
                                split_matmuls(pe, c_bank[t % 2][:, 0:CQ], [
                                    (nrm.h(t, c), (wc_hi[:, c, :], wc_lo[:, c, :])) for c in range(KC)]).then_inc(c_ps, 1)
                            if t >= 1:
                                turn(t - 1)
                        pe.wait_ge(small_in, 96)
                        for g in range(GROUPS):
                            pe.wait_ge(wqn_in[g % 2], 16 * (g // 2 + 1))
                            if g >= 1:
                                pe.wait_ge(ab_ev, STEPS * (g - 1) + 1)
                            for q in range(HPC):
                                for c in range(2):
                                    mm = pe.matmul(a_bank[:, (2 * q + c) * KVR:(2 * q + c + 1) * KVR],
                                                   wqn[:, g % 2, q, c * P:(c + 1) * P], wkn[:, g * HPC + q, :],
                                                   start=True, stop=True)
                            mm.then_inc(ab_ps, 1)
                            pe.wait_ge(wo_in[g % 2], 16 * (g // 2 + 1))
                            for q in range(HPC // 2):
                                if g >= 1:
                                    pe.wait_ge(ab_ev, STEPS * (g - 1) + q + 2)
                                for e in range(2):
                                    mm = pe.matmul(b_bank[q % 2][e * KVR:(e + 1) * KVR, :], wvn[:, g * HPC + 2 * q + e, :],
                                                   wo[:, g % 2, 2 * q + e, :], start=True, stop=True)
                                mm.then_inc(ab_ps, 1)

            w_hi = sb("w_hi", [P, 2, 2, P], F32R, ph)
            w_lo = sb("w_lo", [P, 2, 2, P], F32R, ph)
            b_hi = sb("b_hi", [P, D], F32R, ph)
            b_lo = sb("b_lo", [P, D], F32R, ph)
            qf = sb("qf", [P, S], F32, ph)
            qu = sb("qu", [P, S], F32, ph)
            q_hi = sb("q_hi", [P, 2, S], F32R, ph)
            q_lo = sb("q_lo", [P, 2, S], F32R, ph)
            nmax = sb("nmax", [P, 2, TPB], F32, ph)
            rsum = sb("rsum1", [P, 2, TPB], F32, ph)
            rinv = sb("rinv", [P, 2, TPB], F32, ph)
            prob = sb("prob", [P, 2, TPB, S], F32, ph)
            pT_hi = sb("pT_hi", [P, TPB, S], F32R, ph)
            pT_lo = sb("pT_lo", [P, TPB, S], F32R, ph)
            cT_hi = sb("cT_hi", [P, S], F32R, ph)
            cT_lo = sb("cT_lo", [P, S], F32R, ph)
            o_tmp = sb("o_tmp", [P, 2, D], F32, ph)
            acc = sb("acc", [P, TILES, D], F32, ph)
            whi_done = sem("whi_done")
            wlo_done = sem("wlo_done")
            bhi_done = sem("bhi_done")
            blo_done = sem("blo_done")
            q_ps = sem("q1_ps")
            qrot = sem("qrot")
            qsum = sem("qsum")
            qhi_done = sem("qhi_done")
            qlo_done = sem("qlo_done")
            s_ps = sem("s1_ps")
            max_done = sem("max1_done")
            exp_done = sem("exp1_done")
            rinv_done = sem("rinv_done")
            norm_dve = sem("norm_dve")
            norm_pool = sem("norm_pool")
            pT_ps = sem("pT_ps")
            phi_done = sem("phi_done")
            plo_done = sem("plo_done")
            pv_ps = sem("pv_ps")
            chi_done = sem("chi_done")
            clo_done = sem("clo_done")
            o_ps = sem("o1_ps")
            o_ev = sem("o1_ev")
            acc_done = sem("acc_done")
            acc_set = sem("acc_set")
            x3_done = sem("x3_done")
            s_bank, t_bank = bank[0:2], bank[2:4]
            q_bank, ct_bank, o_bank = bank[4], bank[5:7], bank[7]
            UNITS = 4 * HP
            POOL_STEP = 2

            def ge(eng, s_, v):
                if not (isinstance(v, int) and v <= 0):
                    eng.wait_ge(s_, v)

            def pairs(eng, unit):
                for p in (0, 1):
                    for c in range(4):
                        unit(p, c, False)
                with eng.Fori(2, HP - 1) as p:
                    for c in range(4):
                        unit(p, c, True)
                for p in (HP - 1, HP):
                    for c in range(4):
                        unit(p, c, False)

            def out_step(p, c, st, steady):
                if c % 2:
                    return None
                n, m = st, p * 2 + (c // 2 - 2)
                if not steady and not 0 <= m < 2 * HP:
                    return None
                return m, n

            with nc.Block() as block:
                @block.tensor
                def _(pe):
                    def project(i, c, pair):
                        b, e = (c // 2) % 2, c % 2
                        ts = slice(b * S, (b + 1) * S)
                        if c == 0:
                            pe.wait_ge(wlo_done, pair + 1)
                        ge(pe, qrot, 3 * i)
                        pe.matmul(q_bank[:, :], w_hi[:, e, 0, :], xk_hi[:, 0, ts], start=True, stop=False)
                        pe.matmul(q_bank[:, :], w_hi[:, e, 0, :], xk_lo[:, 0, ts], start=False, stop=False)
                        pe.matmul(q_bank[:, :], w_lo[:, e, 0, :], xk_hi[:, 0, ts], start=False, stop=False)
                        pe.matmul(q_bank[:, :], w_hi[:, e, 1, :], xk_hi[:, 1, ts], start=False, stop=False)
                        pe.matmul(q_bank[:, :], w_lo[:, e, 1, :], xk_hi[:, 1, ts], start=False, stop=True).then_inc(q_ps, 1)

                    def context(g, c, tt):
                        e, b = c % 2, c // 2
                        w = slice(KVR, 3 * KVR) if e == 0 else slice(0, 2 * KVR)
                        ct = ct_bank[b][:, :]
                        ge(pe, plo_done, g + 1)
                        k = b * TPB + tt
                        first, last = e == 0 and tt == 0, e == 1 and tt == TPB - 1
                        pe.matmul(ct, c_hi[:, k, w], pT_hi[:, tt, :], start=first, stop=False)
                        pe.matmul(ct, c_hi[:, k, w], pT_lo[:, tt, :], start=False, stop=False)
                        pe.matmul(ct, c_lo[:, k, w], pT_hi[:, tt, :], start=False, stop=last).then_inc(pv_ps, 1)

                    def unit(p, c, steady):
                        i = p * 4 + c
                        b = c // 2
                        for st in range(TPB):
                            if steady or i < UNITS:
                                if st == 0:
                                    ge(pe, qlo_done, i + 1)
                                ge(pe, exp_done, i * 4 + (st - 1))
                                q = slice(st * P, (st + 1) * P)
                                sbk, ks = s_bank[st % 2][:, :], slice(b * S, (b + 1) * S)
                                pe.matmul(sbk, q_hi[:, c % 2, q], xk_hi[:, 2, ks], start=True, stop=False)
                                pe.matmul(sbk, q_hi[:, c % 2, q], xk_lo[:, 1, ks], start=False, stop=False)
                                pe.matmul(sbk, q_lo[:, c % 2, q], xk_hi[:, 2, ks], start=False, stop=True).then_inc(s_ps, 1)
                            if st == 0 and (steady or i + 2 < UNITS):
                                project(i + 2, (c + 2) % 4, p + (c + 2) // 4)
                            if steady or 1 <= i <= UNITS:
                                if st == 0:
                                    ge(pe, norm_dve, i * 3)
                                    ge(pe, norm_pool, i)
                                ge(pe, plo_done, i * 4 + (st - 5))
                                for n in range(TPB):
                                    mm = pe.transpose(t_bank[st % 2][:, n * P:(n + 1) * P],
                                                      prob[:, (c - 1) % 2, n, st * P:(st + 1) * P], ident[:, :])
                                mm.then_inc(pT_ps, 1)
                            if steady or 6 <= 4 * i + st < 4 * UNITS + 6:
                                cc = (c - 1) % 4 if st >= 2 else (c - 2) % 4
                                if cc % 2 == 0 and st == 2:
                                    ge(pe, clo_done, p * 2 + (c // 2 - 1))
                                context(i * 4 + (st - 6), cc, (st - 2) % TPB)
                            if (o := out_step(p, c, st, steady)) is not None:
                                m, n = o
                                if n == 0:
                                    ge(pe, clo_done, m + 1)
                                    if c == 0:
                                        ge(pe, blo_done, p)
                                ge(pe, o_ev, m * 4 + n)
                                ts = slice(n * P, (n + 1) * P)
                                pe.matmul(o_bank[:, :], cT_hi[:, ts], b_hi[:, :], start=True, stop=False)
                                pe.matmul(o_bank[:, :], cT_hi[:, ts], b_lo[:, :], start=False, stop=False)
                                pe.matmul(o_bank[:, :], cT_lo[:, ts], b_hi[:, :], start=False, stop=True).then_inc(o_ps, 1)

                    project(0, 0, 0)
                    project(1, 1, 0)
                    pairs(pe, unit)

                @block.vector
                def _(dve):
                    def rotate(i, part):
                        lo, hi = slice(KVR, KVR + 32), slice(KVR + 32, P)
                        if part == 0:
                            ge(dve, q_ps, i + 1)
                            ge(dve, qsum, i)
                            dve.tensor_tensor(qu[lo, :], q_bank[hi, :], sinq[hi, :], ALU.mult).then_inc(qrot, 1)
                        elif part == 1:
                            dve.tensor_tensor(qu[hi, :], q_bank[lo, :], sinq[lo, :], ALU.mult).then_inc(qrot, 1)
                        else:
                            ge(dve, qlo_done, i)
                            dve.tensor_tensor(qf[:, :], q_bank[:, :], cosq[:, :], ALU.mult).then_inc(qrot, 1)

                    def normalize(p, i, c, st):
                        ge(dve, exp_done, i * 4 + (st + 1))
                        if st == POOL_STEP:
                            ge(dve, norm_pool, i - 1)
                        r = rinv[:, c % 2, st:st + 1]
                        dve.reciprocal(r, rsum[:, c % 2, st:st + 1]).then_inc(rinv_done, 1)
                        if st != POOL_STEP:
                            ge(dve, rinv_done, i * 4 + (st + 1))
                            dve.tensor_scalar(prob[:, c % 2, st, :], prob[:, c % 2, st, :], r, None,
                                              ALU.mult).then_inc(norm_dve, 1)

                    def unit(p, c, steady):
                        i = p * 4 + c
                        for st in range(TPB):
                            g = i * 4 + st
                            if not st and (steady or 1 <= i <= UNITS):
                                normalize(p, i - 1, (c - 1) % 4, TPB - 1)
                            if steady or 5 <= g < 4 * UNITS + 5:
                                ge(dve, phi_done, i * 4 + (st - 4))
                                ge(dve, pv_ps, i * 4 + (st - 8))
                                dve.tensor_tensor(pT_lo[:, (st - 1) % TPB, :], t_bank[(st - 1) % 2][:, :],
                                                  pT_hi[:, (st - 1) % TPB, :].bitcast(F32), ALU.subtract).then_inc(plo_done, 1)
                            if (c % 2, st) == (1, 3) and (steady or 0 <= 2 * p + c // 2 - 1 < 2 * HP):
                                m = p * 2 + (c // 2 - 1)
                                ge(dve, chi_done, m + 1)
                                dve.tensor_tensor(cT_lo[:, :], ct_bank[(c // 2 - 1) % 2][:, :], cT_hi[:, :].bitcast(F32),
                                                  ALU.subtract).then_inc(clo_done, 1)
                            if steady or i < UNITS:
                                ge(dve, s_ps, i * 4 + (st + 1))
                                if st == 0:
                                    ge(dve, exp_done, (i - 1) * 4)
                                dve.tensor_reduce(nmax[:, c % 2, st:st + 1], s_bank[st % 2][:, :], AX.X, ALU.max,
                                                  negate=True).then_inc(max_done, 1)
                            if st and (steady or i < UNITS):
                                normalize(p, i, c, st - 1)
                            if st and (steady or i + 2 < UNITS):
                                rotate(i + 2, st - 1)

                    dve.wait_ge(acc_set, 1)
                    for i in (0, 1):
                        for part in range(3):
                            rotate(i, part)
                    pairs(dve, unit)

                @block.scalar
                def _(act):
                    def weights(p):
                        ge(act, q_ps, p * 4)
                        act.activation(w_hi[:, :, :, :], wq_all[:, bass.ds(p * 2, 2), :, :], ACT.Copy).then_inc(whi_done, 1)

                    def p_round(i, st, steady):
                        if steady or 1 <= i <= UNITS:
                            ge(act, pT_ps, (i - 1) * 4 + (st + 1))
                            ge(act, pv_ps, (i - 2) * 4 + (st + 1))
                            act.activation(pT_hi[:, st, :], t_bank[st % 2][:, :], ACT.Copy).then_inc(phi_done, 1)

                    def q_round(i, c):
                        ge(act, qsum, i + 1)
                        ge(act, s_ps, (i - 1) * 4)
                        act.activation(q_hi[:, c % 2, :], qf[:, :], ACT.Copy).then_inc(qhi_done, 1)

                    def unit(p, c, steady):
                        i = p * 4 + c
                        for st in range(TPB):
                            if st:
                                p_round(i, st, steady)
                            if steady or i < UNITS:
                                ge(act, max_done, i * 4 + (st + 1))
                                if st == 0:
                                    ge(act, pT_ps, (i - 1) * 4)
                                    ge(act, rinv_done, (i - 1) * 4)
                                act.activation(prob[:, c % 2, st, :], s_bank[st % 2][:, :], ACT.Exp,
                                               bias=nmax[:, c % 2, st:st + 1],
                                               accum_out=rsum[:, c % 2, st:st + 1]).then_inc(exp_done, 1)
                            if not st:
                                p_round(i, st, steady)
                            if (c % 2, st) == (1, 2) and (steady or 0 <= 2 * p + c // 2 - 1 < 2 * HP):
                                m = p * 2 + (c // 2 - 1)
                                ge(act, pv_ps, m * 8 + 8)
                                ge(act, o_ps, m * 4)
                                act.activation(cT_hi[:, :], ct_bank[(c // 2 - 1) % 2][:, :], ACT.Copy).then_inc(chi_done, 1)
                            if (o := out_step(p, c, st, steady)) is not None:
                                m, n = o
                                ge(act, o_ps, m * 4 + (n + 1))
                                ge(act, acc_done, m * 4 + (n - 1))
                                act.activation(o_tmp[:, n % 2, :], o_bank[:, :], ACT.Copy).then_inc(o_ev, 1)
                            if st == 0 and (steady or i + 1 < UNITS):
                                q_round(i + 1, c + 1)
                            if (c, st) == (1, 1) and (steady or p + 1 < HP):
                                weights(p + 1)
                            if (c, st) == (3, 0) and (steady or p < HP):
                                ge(act, o_ps, p * 8)
                                act.activation(b_hi[:, :], wb_all[:, p, :] if not steady else
                                               wb_all[:, bass.ds(p, 1), :].rearrange("p a n -> p (a n)"),
                                               ACT.Copy).then_inc(bhi_done, 1)

                    weights(0)
                    q_round(0, 0)
                    pairs(act, unit)

                @block.gpsimd
                def _(pool):
                    def weights(p):
                        ge(pool, whi_done, p + 1)
                        pool.tensor_tensor(w_lo[:, :, :, :], wq_all[:, bass.ds(p * 2, 2), :, :],
                                           w_hi[:, :, :, :].bitcast(F32), ALU.subtract).then_inc(wlo_done, 1)

                    def q_sum(i):
                        ge(pool, qrot, i * 3 + 3)
                        pool.tensor_tensor(qf[:, :], qf[:, :], qu[:, :], ALU.add).then_inc(qsum, 1)

                    def q_rest(i, c):
                        ge(pool, qhi_done, i + 1)
                        pool.tensor_tensor(q_lo[:, c % 2, :], qf[:, :], q_hi[:, c % 2, :].bitcast(F32),
                                           ALU.subtract).then_inc(qlo_done, 1)

                    def unit(p, c, steady):
                        i = p * 4 + c
                        for st in range(TPB):
                            if st == 0 and (steady or i + 1 < UNITS):
                                q_rest(i + 1, c + 1)
                            if (c, st) == (1, 1) and (steady or p + 1 < HP):
                                weights(p + 1)
                            if (c, st) == (3, 0) and (steady or p < HP):
                                ge(pool, bhi_done, p + 1)
                                pool.tensor_tensor(b_lo[:, :], wb_all[:, p, :] if not steady else
                                                   wb_all[:, bass.ds(p, 1), :].rearrange("p a n -> p (a n)"),
                                                   b_hi[:, :].bitcast(F32), ALU.subtract).then_inc(blo_done, 1)
                            if st == POOL_STEP + 1 and (steady or i < UNITS):
                                ge(pool, rinv_done, i * 4 + st)
                                pr_ = prob[:, c % 2, st - 1, :]
                                pool.tensor_tensor(pr_, pr_, bc(rinv[:, c % 2, st - 1:st], [P, S]),
                                                   ALU.mult).then_inc(norm_pool, 1)
                            if st == 3 and (steady or i + 2 < UNITS):
                                q_sum(i + 2)
                            if (o := out_step(p, c, st, steady)) is not None:
                                m, n = o
                                t = c // 2 * TPB + n
                                ge(pool, o_ev, m * 4 + (n + 1))
                                ge(pool, acc_done, m * 4 + n)
                                pool.tensor_tensor(acc[:, t, :], acc[:, t, :], o_tmp[:, n % 2, :], ALU.add).then_inc(acc_done, 1)

                    pool.memset(qu[:, :], 0.0).then_inc(acc_set, 1)
                    pool.memset(acc[:, :, :], 0.0).then_inc(acc_set, 1)
                    weights(0)
                    q_sum(0)
                    q_rest(0, 0)
                    q_sum(1)
                    pool.wait_ge(acc_set, 2)
                    pairs(pool, unit)
                    pool.wait_ge(acc_done, 4 * 2 * HP)
                    for t in range(TILES):
                        pool.tensor_tensor(acc[:, t, :], acc[:, t, :], gate[:, 0, t // TPB, :], ALU.mult).then_inc(acc_set, 1)
                        pool.wait_ge(acc_set, t + 3)
                        pool.tensor_tensor(x[:, t, :], x[:, t, :], acc[:, t, :], ALU.add).then_inc(x3_done, 1)

        if stop_after == 2:
            with nc.Block() as block:
                @block.sync
                def _(sp):
                    sp.dma_start(out_dram, x[:, :, :]).then_inc(stored, 16)
                    sp.wait_ge(stored, 16)
            return

        with ExitStack() as ph:
            stage = sb("stage_d", [P, KC, D], F32, ph)
            fa = sb("fa", [R1, D], F32, ph)
            fb = sb("fb", [R1, D], F32, ph)
            w_eff = sb("w_eff", [P, KC, D], F32, ph)
            w_sq = sb("w_sq", [P, KC, D], F32, ph)
            wh = sb("wl_hi", [P, KC, D], F32R, ph)
            wl = sb("wl_lo", [P, KC, D], F32R, ph)
            mag = sb("mag", [P, D], F32, ph)
            norm = sb("norm", [P, D], F32, ph)
            factor = sb("factor", [P, B, D], F32, ph)
            y_g = sb("y_g", [P, 2, D], F32, ph)
            w_in = sem("w_in")
            ba_ps = sem("ba_ps")
            weff_done = sem("weff_done")
            wsq_done = sem("wsq_done")
            whi2_done = sem("whi2_done")
            wlo2_done = sem("wlo2_done")
            norm_ps = sem("norm_ps")
            norm_done = sem("norm_done")
            chain = sem("factor_chain")
            y_ps = sem("y_ps")
            yg_done = sem("yg_done")
            x4_done = sem("x4_done")
            nrm = Norm("n3", SB, CB, used=y_ps, ctx=ph)
            pT, y_bank, n_bank, w_bank = bank[0], bank[1:3], bank[3], bank[4:8]

            with nc.Block() as block:
                @block.sync
                def _(sp):
                    sp.dma_start(stage[:, :, :], a["wf1"].rearrange("(k p) n -> p k n", p=P)).then_inc(w_in, 16)
                    sp.dma_start(fa[:, :], a["fa1"]).then_inc(w_in, 16)
                    sp.dma_start(fb[:, :], a["fb1"]).then_inc(w_in, 16)
                    sp.dma_start(mag[:, :], bc(a["mag1"], [P, D])).then_inc(w_in, 16)
                    for t in range(TILES):
                        sp.wait_ge(x4_done, t + 1)
                        sp.dma_start(out_dram[:, t, :], x[:, t, :]).then_inc(stored, 16)
                    sp.wait_ge(stored, 16 * TILES)

                @block.gpsimd
                def _(pool):
                    for t in range(TILES):
                        pool.wait_ge(yg_done, t + 1)
                        pool.tensor_tensor(x[:, t, :], x[:, t, :], y_g[:, t % 2, :], ALU.add).then_inc(x4_done, 1)

                @block.scalar
                def _(act):
                    nrm.act_std(act)
                    for k in range(KC):
                        act.wait_ge(weff_done, k + 1)
                        act.activation(w_sq[:, k, :], w_eff[:, k, :], ACT.Square).then_inc(wsq_done, 1)
                        act.activation(wh[:, k, :], w_eff[:, k, :], ACT.Copy).then_inc(whi2_done, 1)
                    act.wait_ge(norm_ps, 1)
                    act.activation(norm[:, :], n_bank[:, :], ACT.Sqrt).then_inc(norm_done, 1)
                    for t in range(TILES):
                        nrm.act_h(act, t, pT)

                @block.vector
                def _(dve):
                    nrm.dve_stats(dve)
                    dve.wait_ge(w_in, 64)
                    for k in range(KC):
                        dve.wait_ge(ba_ps, k + 1)
                        dve.tensor_tensor(w_eff[:, k, :], w_bank[k][:, :], stage[:, k, :], ALU.add).then_inc(weff_done, 1)
                    nrm.dve_xn(dve, 0)
                    for k in range(KC):
                        dve.wait_ge(whi2_done, k + 1)
                        dve.tensor_tensor(wl[:, k, :], w_eff[:, k, :], wh[:, k, :].bitcast(F32),
                                          ALU.subtract).then_inc(wlo2_done, 1)
                    link = Chain(dve, chain)
                    dve.wait_ge(norm_done, 1)
                    link(dve.reciprocal(norm[:, :], norm[:, :]))
                    link(dve.tensor_tensor(norm[:, :], norm[:, :], mag[:, :], ALU.mult))
                    for b in range(B):
                        link(dve.tensor_tensor(factor[:, b, :], norm[:, :], gate[:, 1, b, :], ALU.mult))
                    nrm.dve_lo(dve, 0)
                    for t in range(TILES):
                        if t + 1 < TILES:
                            nrm.dve_xn(dve, t + 1)
                            nrm.dve_lo(dve, t + 1)
                        dve.wait_ge(y_ps, t + 1)
                        if t >= 2:
                            dve.wait_ge(x4_done, t - 1)
                        dve.tensor_tensor(y_g[:, t % 2, :], y_bank[t % 2][:, :], factor[:, t // TPB, :],
                                          ALU.mult).then_inc(yg_done, 1)

                @block.tensor
                def _(pe):
                    pe.wait_ge(w_in, 64)
                    for k in range(KC):
                        pe.matmul(w_bank[k][:, :], fa[:, k * P:(k + 1) * P], fb[:, :],
                                  start=True, stop=True).then_inc(ba_ps, 1)
                    for k in range(KC):
                        pe.wait_ge(wsq_done, k + 1)
                        mm = pe.matmul(n_bank[:, :], ones[:, :], w_sq[:, k, :], start=(k == 0), stop=(k == KC - 1))
                    mm.then_inc(norm_ps, 1)
                    nrm.pe_xT(pe, 0, pT)
                    pe.wait_ge(wlo2_done, KC)
                    for t in range(TILES):
                        if t + 1 < TILES:
                            nrm.pe_xT(pe, t + 1, pT)
                        pe.wait_ge(nrm.lo, t + 1)
                        if t >= 2:
                            pe.wait_ge(yg_done, t - 1)
                        split_matmuls(pe, y_bank[t % 2][:, :], [
                            (nrm.h(t, c), (wh[:, c, :], wl[:, c, :])) for c in range(KC)]).then_inc(y_ps, 1)


def _constants():
    import numpy as np

    inv = (1.0 / 10000.0 ** (np.arange(0, RD, 2, dtype=np.float32) / np.float32(RD))).astype(np.float32)
    ang = np.outer(np.arange(S, dtype=np.float32), inv).astype(np.float32)
    cos, sin = np.cos(ang).astype(np.float32), np.sin(ang).astype(np.float32)
    cosq = np.full((P, S), SCALE1, np.float32)
    sinq = np.zeros((P, S), np.float32)
    cosq[KVR:] = np.concatenate([cos, cos], 1).T * np.float32(SCALE1)
    sinq[KVR:KVR + 32] = sin.T * np.float32(SCALE1)
    sinq[KVR + 32:] = -sin.T * np.float32(SCALE1)
    cosk = np.concatenate([cos, cos], 1).reshape(TPB, P, RD).transpose(1, 0, 2)
    sink = np.concatenate([sin, -sin], 1).reshape(TPB, P, RD).transpose(1, 0, 2)
    return {
        "ident": np.eye(P, dtype=np.float32),
        "iota": np.tile(np.arange(E0, dtype=np.float32), (P, 1)),
        "cosq": cosq, "sinq": sinq,
        "cosk": np.ascontiguousarray(cosk), "sink": np.ascontiguousarray(sink),
    }


def _layout(i):
    import numpy as np

    t = {k: np.asarray(v) for k, v in i.items()}
    wqb = t["L1_attn_w_qb"].reshape(QR, NH, ND + RD)
    wkvb = t["L1_attn_w_kvb"].reshape(KVR, NH, ND + VD)
    nope = wqb[:, :, :ND].transpose(1, 2, 0)
    rope = wqb[:, :, ND:]
    return {
        "x": t["L0_attn_hidden_states"].reshape(TOK, D),
        "c0": t["L0_c"].T, "c1": t["L1_c"].T,
        "wmod0": t["L0_wmod"], "wmod1": t["L1_wmod"],
        "wqkv0": np.concatenate([t["L0_attn_wq"].T, t["L0_attn_wk"].T, t["L0_attn_wv"].T], 1),
        "bqkv0": np.concatenate([t["L0_attn_bq"], t["L0_attn_bk"], t["L0_attn_bv"]])[None],
        "wffn0": np.concatenate([t["L0_ffn_base_w"].T, t["L0_ffn_A"].T, t["L0_ffn_router_w"].T], 1),
        "bffn0": t["L0_ffn_base_b"][None],
        "wexp0": t["L0_ffn_B"].transpose(0, 2, 1).reshape(E0 * R0, D),
        "wc1": np.concatenate([t["L1_attn_w_qa"], t["L1_attn_w_kva"]], 1),
        "gq1": t["L1_attn_g_qa"][None], "gk1": t["L1_attn_g_kva"][None],
        "wqn1": np.concatenate([nope, nope[:, :, P:]], 2),
        "wqr1": np.stack([rope[:P], np.concatenate([rope[P:], rope[P:]], 0)], 1),
        "wkn1": wkvb[:, :, :ND].transpose(2, 1, 0),
        "wvn1": wkvb[:, :, ND:].transpose(2, 1, 0),
        "wo1": t["L1_attn_w_o"],
        "wf1": t["L1_ffn_W"].T, "fa1": t["L1_ffn_lora_A"], "fb1": t["L1_ffn_lora_B"].T,
        "mag1": t["L1_ffn_magnitude"][None],
        **_constants(),
    }


def kernel(**inputs):
    import numpy as _np
    import concourse.bacc as _bacc
    from concourse import mybir as _mybir
    from concourse.bass_utils import run_bass_kernel_spmd as _run

    nc = _bacc.Bacc("TRN2", target_bir_lowering=False, num_devices=1)
    arrays, aps = {}, {}
    for name, v in _layout(inputs).items():
        v = _np.ascontiguousarray(v)
        arrays[f"in_{name}"] = v
        aps[name] = nc.dram_tensor(f"in_{name}", v.shape, _mybir.dt.from_np(v.dtype), kind="ExternalInput").ap()
    out = nc.dram_tensor("out_x", (TOK, D), F32, kind="ExternalOutput").ap()
    megakernel(nc, aps, out)
    r = _run(nc, [arrays], core_ids=[0])
    return r.results[0]["out_x"].reshape(B, S, D)
```

```python
from contextlib import ExitStack

import concourse.bass as bass
from concourse import mybir

P = 128
F32 = mybir.dt.float32
F32R = mybir.dt.float32r
U32 = mybir.dt.uint32
ALU = mybir.AluOpType
ACT = mybir.ActivationFunctionType
AX = mybir.AxisListType

B, S, D = 2, 512, 512
TOK = B * S
TILES = TOK // P
TPB = S // P
KC = D // P
QD = P // 32

H0, HD0 = 32, 16
PAD0 = 32
VW = HD0 + 1

R0, E0 = 64, 16
PROJ0 = D + R0 + E0
EC = E0 * R0 // P
LORA_SCALE = 32.0 / 64.0

NH, QR, KVR, RD, ND, VD = 32, 192, 64, 64, 128, 128
QREST = QR - P
CQ = QR + KVR + RD
HP = NH // 2
SCALE1 = float(ND + RD) ** -0.5
CW = KVR + 1

R1 = 32
LN_EPS = 1e-5
RMS_EPS = 1e-6
SIX = 6 * KC
SA, CA, GA, SB, CB, GB = (j * KC for j in range(6))


def bc(ap, shape):
    return ap.to_broadcast(shape)


class Chain:

    def __init__(self, eng, sem, n=0):
        self.eng, self.sem, self.n = eng, sem, n

    def __call__(self, ins):
        self.n += 1
        ins.then_inc(self.sem, 1)
        self.eng.wait_ge(self.sem, self.n)


def split_matmuls(pe, out, pairs, first=True, last=True):
    n = len(pairs)
    for i, ((xh, xl), (wh, wl)) in enumerate(pairs):
        pe.matmul(out, xh, wh, start=first and i == 0, stop=False)
        pe.matmul(out, xh, wl, start=False, stop=False)
        mm = pe.matmul(out, xl, wh, start=False, stop=last and i == n - 1)
    return mm


def megakernel(nc, a, out):
    x_dram = a["x"].rearrange("(t p) d -> p t d", p=P)
    out_dram = out.rearrange("(t p) d -> p t d", p=P)

    with ExitStack() as whole:
        def sb(name, shape, dt=F32, ctx=whole):
            return ctx.enter_context(nc.sbuf_tensor(name, shape, dt))

        def sem(name):
            return whole.enter_context(nc.semaphore(name))

        bank = [whole.enter_context(nc.psum_tensor(f"bank{i}", [P, 512], F32)) for i in range(8)]

        x = sb("x_res", [P, TILES, D])
        ident = sb("ident", [P, P])
        ones = sb("ones", [P, P])
        eps = sb("eps", [P, 1])
        cs = sb("cs", [P, 2 * KC * B])
        cs_e = sb("cs_e", [P, 2 * KC * B])
        cs_s = sb("cs_s", [P, 2 * KC * B])
        mod = sb("mod", [P, SIX * B])
        gabs = sb("gabs", [P, 4 * KC * B])
        gate = sb("gate", [P, 2, B, D])
        stats = sb("stats", [P, TILES, 6])
        mv = sb("mv", [P, TILES, 2])
        rstd = sb("rstd", [P, TILES])
        mod3 = mod[:, :].rearrange("p (m b) -> p m b", b=B)
        cs4 = cs_s[:, :].rearrange("p (l k b) -> p l k b", l=2, b=B)

        x_in = sem("x_in")
        const_in = sem("const_in")
        wmod_in = [sem(f"wmod_in{j}") for j in range(6)]
        raw_in = [sem("raw_in0"), sem("raw_in1")]
        raw_free = sem("raw_free")
        stored = sem("stored")

        def load_chunks(sp, stage, chunks, base):
            for i, src in enumerate(chunks):
                n = base + i
                if n >= 2:
                    sp.wait_ge(raw_free, n - 1)
                w = 1
                for s in src.shape[1:]:
                    w *= s
                dst = stage[:, n % 2, 0:w]
                if len(src.shape) == 3:
                    dst = dst.rearrange("p (a b) -> p a b", a=src.shape[1])
                sp.dma_start(dst, src).then_inc(raw_in[n % 2], 16)

        split_hi = sem("split_hi")

        def split_act(act, stage, chunks, base):
            for i, (hi, lo) in enumerate(chunks):
                n = base + i
                w = hi.shape[-1]
                act.wait_ge(raw_in[n % 2], 16 * (n // 2 + 1))
                act.activation(hi, stage[:, n % 2, 0:w], ACT.Copy).then_inc(split_hi, 1)

        def split_dve(dve, stage, chunks, base):
            for i, (hi, lo) in enumerate(chunks):
                n = base + i
                w = hi.shape[-1]
                dve.wait_ge(split_hi, n + 1)
                dve.tensor_tensor(lo, stage[:, n % 2, 0:w], hi.bitcast(F32), ALU.subtract).then_inc(raw_free, 1)

        stat_done = sem("stat_done")

        def tile_stats(dve, t):
            dve.bn_stats(stats[:, t, :], x[:, t, :]).then_inc(stat_done, 1)

        class Norm:

            def __init__(self, tag, shift, scale, used, ctx, used_per=1):
                self.x = sb(f"{tag}_x", [P, 2, D], F32, ctx)
                self.f = sb(f"{tag}_f", [P, KC, P], F32, ctx)
                self.h_hi = sb(f"{tag}_h_hi", [P, 2, KC, P], F32R, ctx)
                self.h_lo = sb(f"{tag}_h_lo", [P, 2, KC, P], F32R, ctx)
                self.shift, self.scale = shift, scale
                self.n = int(tag[1:])
                self.var = sem(f"{tag}_var")
                self.std = sem(f"{tag}_std")
                self.rstd = sem(f"{tag}_rstd")
                self.xn = sem(f"{tag}_xn")
                self.xT = sem(f"{tag}_xT")
                self.hf = sem(f"{tag}_hf")
                self.hi = sem(f"{tag}_hi")
                self.lo = sem(f"{tag}_lo")
                self.used = used
                self.used_per = used_per

            def dve_stats(self, dve):
                for t in range(TILES):
                    dve.wait_ge(stat_done, TILES * self.n + t + 1)
                    dve.bn_aggr(mv[:, t, :], stats[:, t, :]).then_inc(self.var, 1)
                dve.wait_ge(self.std, 1)
                dve.reciprocal(rstd[:, :], rstd[:, :]).then_inc(self.rstd, 1)

            def act_std(self, act):
                act.wait_ge(self.var, TILES)
                act.activation(rstd[:, :], mv[:, :, 1], ACT.Sqrt, bias=eps[:, 0:1]).then_inc(self.std, 1)

            def dve_xn(self, dve, t):
                if t == 0:
                    dve.wait_ge(self.rstd, 1)
                if t >= 2:
                    dve.wait_ge(self.xT, t - 1)
                dve.tensor_scalar(self.x[:, t % 2, :], x[:, t, :], mv[:, t, 0:1], rstd[:, t:t + 1],
                                  ALU.subtract, ALU.mult).then_inc(self.xn, 1)

            def pe_xT(self, pe, t, pT):
                pe.wait_ge(self.xn, t + 1)
                if t >= 1:
                    pe.wait_ge(self.hf, t)
                for c in range(KC):
                    mm = pe.transpose(pT[:, c * P:(c + 1) * P], self.x[:, t % 2, c * P:(c + 1) * P], ident[:, :])
                mm.then_inc(self.xT, 1)

            def act_h(self, act, t, pT):
                b = t // TPB
                act.wait_ge(self.xT, t + 1)
                if t >= 1:
                    act.wait_ge(self.lo, t)
                for c in range(KC):
                    a_ = act.activation(self.f[:, c, :], pT[:, c * P:(c + 1) * P], ACT.Identity,
                                        bias=mod3[:, self.shift + c, b:b + 1], scale=mod3[:, self.scale + c, b:b + 1])
                a_.then_inc(self.hf, 1)
                if t >= 2:
                    act.wait_ge(self.used, self.used_per * (t - 1))
                act.wait_ge(self.hf, t + 1)
                act.activation(self.h_hi[:, t % 2, :, :], self.f[:, :, :], ACT.Copy).then_inc(self.hi, 1)

            def dve_lo(self, dve, t):
                dve.wait_ge(self.hi, t + 1)
                dve.tensor_tensor(self.h_lo[:, t % 2, :, :], self.f[:, :, :], self.h_hi[:, t % 2, :, :].bitcast(F32),
                                  ALU.subtract).then_inc(self.lo, 1)

            def h(self, t, c):
                return (self.h_hi[:, t % 2, c, :], self.h_lo[:, t % 2, c, :])

        prefetch = whole.enter_context(ExitStack())
        stage = sb("stage_a", [P, 2, 3 * D], F32, prefetch)
        raw_e = sb("raw_e", [P, EC, D], F32, prefetch)
        raw_f = stage[:, :, :].rearrange("p a b -> p (a b)")[:, 0:KC * PROJ0].rearrange("p (k n) -> p k n", k=KC)
        stage_flat = stage[:, :, :].rearrange("p a b -> p (a b)")
        at = [KC * CQ, QR, KVR, TPB * RD, TPB * RD]
        at = [sum(at[:n]) for n in range(len(at) + 1)]
        raw_c = stage_flat[:, 0:at[1]].rearrange("p (k n) -> p k n", k=KC)
        gq, gk = stage_flat[:, at[1]:at[2]], stage_flat[:, at[2]:at[3]]
        cosk = stage_flat[:, at[3]:at[4]].rearrange("p (t r) -> p t r", t=TPB)
        sink = stage_flat[:, at[4]:at[5]].rearrange("p (t r) -> p t r", t=TPB)
        small_in = sem("small_in")
        split2_hi = sem("split2_hi")
        split2_lo = sem("split2_lo")
        mrow = raw_e[:, :, :].rearrange("p a b -> p (a b)")[0:B, 0:SIX * P]
        exp_c = sem("exp_c")
        silu = sem("silu")
        const_set = sem("const_set")
        row_ps = sem("row_ps")
        row_ev = sem("row_ev")
        mod_ps = sem("mod_ps")
        mod_done = sem("mod_done")
        mod_chain = sem("mod_chain")
        gate_ps = sem("gate_ps")
        gate_done = sem("gate_done")
        mod_steps = [0]

        def load_wmod(sp, layer, wmod):
            src = a[f"wmod{layer}"].rearrange("(k p) n -> p k n", p=P)
            for j in range(6):
                sp.dma_start(wmod[:, :, j * D:(j + 1) * D], src[:, :, j * D:(j + 1) * D]).then_inc(wmod_in[j], 16)

        def pe_rows(pe, layer, j, wmod, ps):
            pe.wait_ge(wmod_in[j], 16 * (layer + 1))
            for k in range(KC):
                mm = pe.matmul(ps[0:B, :], cs4[:, layer, k, :], wmod[:, k, j * D:(j + 1) * D],
                               start=(k == 0), stop=(k == KC - 1))
            mm.then_inc(row_ps, 1)

        def act_rows(act, layer, j, ps):
            act.wait_ge(row_ps, 6 * layer + j + 1)
            act.activation(mrow[:, j * D:(j + 1) * D], ps[0:B, :], ACT.Copy).then_inc(row_ev, 1)

        def modulation(layer, wmod=None, extra_act=None, extra_dve=None, extra_sp=None, extra_pool=None,
                       late_dve=None):
            with nc.Block() as block:
                @block.sync
                def _(sp):
                    if layer == 0:
                        cs_in = cs[:, :].rearrange("p (l k b) -> p l k b", l=2, b=B)
                        sp.dma_start(cs_in[:, 0], a["c0"].rearrange("(k p) b -> p k b", p=P)).then_inc(const_in, 16)
                        sp.dma_start(cs_in[:, 1], a["c1"].rearrange("(k p) b -> p k b", p=P)).then_inc(const_in, 16)
                        sp.dma_start(ident[:, :], a["ident"]).then_inc(const_in, 16)
                        load_wmod(sp, 0, wmod)
                    if extra_sp:
                        extra_sp(sp)

                @block.gpsimd
                def _(pool):
                    if extra_pool:
                        extra_pool(pool)

                @block.scalar
                def _(act):
                    if layer == 0:
                        act.wait_ge(const_in, 48)
                        act.activation(cs_e[:, :], cs[:, :], ACT.Exp, scale=-1.0).then_inc(exp_c, 1)
                        for j in range(6):
                            act_rows(act, 0, j, bank[2 + j])
                    if extra_act:
                        extra_act(act)

                @block.vector
                def _(dve):
                    link = Chain(dve, mod_chain, mod_steps[0])
                    if layer == 0:
                        dve.memset(ones[:, :], 1.0).then_inc(const_set, 1)
                        dve.memset(eps[:, :], LN_EPS).then_inc(const_set, 1)
                        dve.wait_ge(exp_c, 1)
                        link(dve.tensor_scalar_add(cs_e[:, :], cs_e[:, :], 1.0))
                        link(dve.reciprocal(cs_e[:, :], cs_e[:, :]))
                        dve.tensor_tensor(cs_s[:, :], cs[:, :], cs_e[:, :], ALU.mult).then_inc(silu, 1)
                    if extra_dve:
                        extra_dve(dve)
                    dve.wait_ge(mod_ps, layer + 1)
                    link(dve.tensor_copy(mod[:, :], bank[0][:, 0:SIX * B]))
                    w = KC * B
                    for n, g in enumerate((GA, GB)):
                        gg = mod3[:, g:g + KC, :].rearrange("p m b -> p (m b)")
                        t0, t1 = gabs[:, 2 * n * w:(2 * n + 1) * w], gabs[:, (2 * n + 1) * w:(2 * n + 2) * w]
                        link(dve.tensor_scalar(t0, gg, -1.0, None, ALU.mult))
                        link(dve.tensor_tensor(t0, t0, gg, ALU.max))
                        link(dve.tensor_scalar(t0, t0, 0.25, None, ALU.max))
                        link(dve.tensor_scalar(t1, gg, 0.0, 2.0, ALU.is_ge, ALU.mult))
                        link(dve.tensor_scalar(t1, t1, -1.0, None, ALU.add))
                        dve.tensor_tensor(gg, t0, t1, ALU.mult).then_inc(mod_done, 1)
                    link(dve.tensor_scalar_add(mod3[:, CA:CA + KC, :], mod3[:, CA:CA + KC, :], 1.0))
                    link(dve.tensor_scalar_add(mod3[:, CB:CB + KC, :], mod3[:, CB:CB + KC, :], 1.0))
                    mod_steps[0] = link.n
                    if late_dve:
                        late_dve(dve)
                    for n in range(4):
                        dve.wait_ge(gate_ps, 4 * layer + n + 1)
                        dve.tensor_copy(gate[:, n // 2, n % 2, :], bank[1 + n][:, :]).then_inc(gate_done, 1)

                @block.tensor
                def _(pe):
                    if layer == 0:
                        pe.wait_ge(silu, 1)
                        for j in range(6):
                            pe_rows(pe, 0, j, wmod, bank[2 + j])
                    for j in range(6):
                        pe.wait_ge(row_ev, 6 * layer + j + 1)
                        for m in range(j * KC, (j + 1) * KC):
                            mm = pe.transpose(bank[0][:, m * B:(m + 1) * B], mrow[:, m * P:(m + 1) * P], ident[0:B, 0:B])
                    mm.then_inc(mod_ps, 1)
                    for n, (g, b) in enumerate(((GA, 0), (GA, 1), (GB, 0), (GB, 1))):
                        pe.wait_ge(mod_done, 2 * layer + n // 2 + 1)
                        for c in range(KC):
                            mm = pe.matmul(bank[1 + n][:, c * P:(c + 1) * P],
                                           bc(mod3[:, g + c, b:b + 1], [P, P]), ident[:, :], start=True, stop=True)
                        mm.then_inc(gate_ps, 1)

        raw_n = [0]

        fsrc = a["wffn0"].rearrange("(k p) n -> p k n", p=P)
        esrc = a["wexp0"].rearrange("(k p) n -> p k n", p=P)
        ffn_in = sem("ffn_in")
        with ExitStack() as ph:
            wq_hi = sb("wqkv_hi", [P, KC, 3 * D], F32R, ph)
            wq_lo = sb("wqkv_lo", [P, KC, 3 * D], F32R, ph)
            wsrc = a["wqkv0"].rearrange("(k p) n -> p k n", p=P)
            chunks = [wsrc[:, k, :] for k in range(KC)]
            parts = [(wq_hi[:, k, :], wq_lo[:, k, :]) for k in range(KC)]
            base = raw_n[0]
            bias0 = sb("bias0", [P, 3 * D], F32, ph)
            qk = sb("qk", [P, 2, H0, PAD0], F32, ph)
            q_bd = sb("q_bd", [P, 32, P], F32, ph)
            bias_in = sem("bias_in")
            pad_set = sem("pad_set")
            qkv_ready = sem("qkv_ready")
            nrm = Norm("n0", SA, CA, used=qkv_ready, ctx=ph, used_per=3)

            def load_start(sp):
                for t in range(TILES):
                    sp.dma_start(x[:, t, :], x_dram[:, t, :]).then_inc(x_in, 16)
                load_chunks(sp, stage, chunks, base)
                sp.dma_start(bias0[:, :], bc(a["bqkv0"], [P, 3 * D])).then_inc(bias_in, 16)

            def act_start(act):
                nrm.act_std(act)
                split_act(act, stage, parts, base)

            def dve_start(dve):
                dve.wait_ge(x_in, 16 * TILES)
                for t in range(TILES):
                    tile_stats(dve, t)
                nrm.dve_stats(dve)
                for i in range(2):
                    split_dve(dve, stage, parts[i:i + 1], base + i)

            def dve_later(dve):
                for i in range(2, KC):
                    split_dve(dve, stage, parts[i:i + 1], base + i)

            def pad_start(pool):
                pool.memset(qk[:, :, :, :], 0.0).then_inc(pad_set, 1)
                pool.memset(q_bd[:, :, :], 0.0).then_inc(pad_set, 1)

            with ExitStack() as ms:
                wmod0 = sb("wmod0", [P, KC, 6 * D], F32, ms)
                modulation(0, wmod0, extra_sp=load_start, extra_act=act_start, extra_dve=dve_start, late_dve=dve_later,
                           extra_pool=pad_start)
            raw_n[0] += len(chunks)

            v_tok = sb("v_tok", [P, D], F32, ph)
            qT = sb("qT", [P, 32, H0], F32, ph)
            kT = sb("kT", [P, 2, 32, H0], F32, ph)
            e_bd = sb("e_bd", [P, 32, P], F32, ph)
            vT = sb("vT", [P, 3, 32, VW], F32, ph)
            s_max = sb("s_max", [P, 32], F32, ph)
            s_sub = sb("s_sub", [P, 32, H0], F32, ph)
            e_s = sb("e_s", [P, 32, H0], F32, ph)
            eT = sb("eT", [P, 32, H0], F32, ph)
            o_rec = sb("o_rec", [P, 32], F32, ph)
            o_n = sb("o_n", [P, HD0, 32], F32, ph)
            o_tok = sb("o_tok", [P, D], F32, ph)
            o_g = sb("o_g", [P, D], F32, ph)
            qkv_ev = sem("qkv_ev")
            turned = sem("turned")
            qbd_done = sem("qbd_done")
            s_ps = sem("s_ps")
            max_done = sem("max_done")
            sub_done = sem("sub_done")
            exp_done = sem("exp_done")
            eT_done = sem("eT_done")
            ebd_done = sem("ebd_done")
            o_ps = sem("o_ps")
            rec_done = sem("rec_done")
            on_done = sem("on_done")
            otok_done = sem("otok_done")
            og_done = sem("og_done")
            x1_done = sem("x1_done")
            pT, q_ps, k_ps, v_ps = bank[0], bank[1], bank[2], bank[3]
            s_bank, o_bank = bank[4:6], bank[6:8]
            HB = 16
            OW = HB * VW

            def s_view(j):
                return s_bank[j][:, :].rearrange("p (n h) -> p n h", h=H0)

            def o_view(j):
                return o_bank[j][:, 0:OW].rearrange("p (n d) -> p n d", d=VW)

            with nc.Block() as block:
                @block.sync
                def _(sp):
                    sp.dma_start(raw_f, fsrc).then_inc(ffn_in, 16)
                    sp.dma_start(raw_e[:, 0:4, :], esrc[:, 0:4, :]).then_inc(ffn_in, 16)
                    sp.dma_start(raw_e[:, 4:8, :], esrc[:, 4:8, :]).then_inc(ffn_in, 16)

                @block.gpsimd
                def _(pool):
                    pool.memset(vT[:, :, :, :], 1.0).then_inc(pad_set, 1)
                    pool.memset(e_bd[:, :, :], 0.0).then_inc(pad_set, 1)
                    for t in range(TILES):
                        pool.wait_ge(otok_done, t + 1)
                        if t >= 1:
                            pool.wait_ge(x1_done, t)
                        pool.tensor_tensor(o_g[:, :], o_tok[:, :], gate[:, 0, t // TPB, :], ALU.mult).then_inc(og_done, 1)
                        pool.wait_ge(og_done, t + 1)
                        pool.tensor_tensor(x[:, t, :], x[:, t, :], o_g[:, :], ALU.add).then_inc(x1_done, 1)

                @block.scalar
                def _(act):
                    def q_blocks(t):
                        act.wait_ge(turned, 3 * t + 1)
                        if t >= 1:
                            act.wait_ge(s_ps, 2 * t)
                        for g in range(QD):
                            r = slice(32 * g, 32 * g + 32)
                            a_ = act.activation(q_bd[r, :, r], qT[r, :, :], ACT.Copy)
                        a_.then_inc(qbd_done, 1)

                    def exps(t):
                        act.wait_ge(sub_done, 2 * t + 2)
                        if t >= 1:
                            act.wait_ge(eT_done, t)
                        act.activation(e_s[:, :, :], s_sub[:, :, :], ACT.Exp, scale=float(HD0) ** -0.5).then_inc(exp_done, 1)

                    def e_blocks(t):
                        act.wait_ge(eT_done, t + 1)
                        if t >= 1:
                            act.wait_ge(o_ps, 2 * t)
                        else:
                            act.wait_ge(pad_set, 4)
                        for g in range(QD):
                            r = slice(32 * g, 32 * g + 32)
                            a_ = act.activation(e_bd[r, :, r], eT[r, :, :], ACT.Copy)
                        a_.then_inc(ebd_done, 1)

                    nrm.act_h(act, 0, pT)
                    for t in range(TILES + 1):
                        if t >= 2:
                            e_blocks(t - 2)
                        if t + 1 < TILES:
                            nrm.act_h(act, t + 1, pT)
                        if t < TILES:
                            q_blocks(t)
                        if t >= 1:
                            exps(t - 1)
                    e_blocks(TILES - 1)

                @block.vector
                def _(dve):
                    nrm.dve_xn(dve, 0)
                    nrm.dve_lo(dve, 0)
                    dve.wait_ge(bias_in, 16)

                    def q_turn(t):
                        dve.wait_ge(qkv_ready, 3 * t + 1)
                        if t >= 1:
                            dve.wait_ge(turned, 3 * t - 2)
                        dve.tensor_tensor(qk[:, 0, :, 0:HD0], q_ps[:, :].rearrange("p (h d) -> p h d", d=HD0),
                                          bias0[:, 0:D].rearrange("p (h d) -> p h d", d=HD0),
                                          ALU.add).then_inc(qkv_ev, 1)
                        dve.wait_ge(qkv_ev, 3 * t + 1)
                        if t >= 1:
                            dve.wait_ge(qbd_done, t)
                        dve.transpose(qT[:, :, :].rearrange("p n h -> p h n"), qk[:, 0, :, :]).then_inc(turned, 1)

                    def k_turn(t):
                        dve.wait_ge(qkv_ready, 3 * t + 2)
                        if t >= 1:
                            dve.wait_ge(turned, 3 * t - 1)
                        dve.tensor_tensor(qk[:, 1, :, 0:HD0], k_ps[:, :].rearrange("p (h d) -> p h d", d=HD0),
                                          bias0[:, D:2 * D].rearrange("p (h d) -> p h d", d=HD0),
                                          ALU.add).then_inc(qkv_ev, 1)
                        dve.wait_ge(qkv_ev, 3 * t + 2)
                        if t >= 2:
                            dve.wait_ge(s_ps, 2 * (t - 1))
                        dve.transpose(kT[:, t % 2, :, :].rearrange("p n h -> p h n"), qk[:, 1, :, :]).then_inc(turned, 1)

                    def v_turn(t):
                        dve.wait_ge(qkv_ready, 3 * t + 3)
                        if t >= 1:
                            dve.wait_ge(turned, 3 * t)
                        dve.tensor_tensor(v_tok[:, :], v_ps[:, :], bias0[:, 2 * D:3 * D], ALU.add).then_inc(qkv_ev, 1)
                        dve.wait_ge(qkv_ev, 3 * t + 3)
                        if t == 0:
                            dve.wait_ge(pad_set, 3)
                        if t >= 3:
                            dve.wait_ge(o_ps, 2 * (t - 2))
                        dve.transpose(vT[:, t % 3, :, 0:HD0].rearrange("p n d -> p d n"),
                                      v_tok[:, :].rearrange("p (h d) -> p d h", d=HD0)).then_inc(turned, 1)

                    def softmax(t, j):
                        dve.wait_ge(s_ps, 2 * t + j + 1)
                        if t >= 1:
                            dve.wait_ge(sub_done, 2 * t - 1 + j)
                        dve.tensor_reduce(s_max[:, HB * j:HB * (j + 1)], s_view(j), AX.X, ALU.max).then_inc(max_done, 1)
                        if t >= 1:
                            dve.wait_ge(exp_done, t)
                        dve.wait_ge(max_done, 2 * t + j + 1)
                        dve.tensor_tensor(s_sub[:, HB * j:HB * (j + 1), :], s_view(j),
                                          bc(s_max[:, HB * j:HB * (j + 1)].unsqueeze(2), [P, HB, H0]),
                                          ALU.subtract).then_inc(sub_done, 1)

                    def turn(t):
                        dve.wait_ge(exp_done, t + 1)
                        if t >= 1:
                            dve.wait_ge(ebd_done, t)
                        dve.transpose(eT[:, :, :].rearrange("p n h -> p (n h)"),
                                      e_s[:, :, :].rearrange("p n h -> p (n h)")).then_inc(eT_done, 1)

                    def finish(t):
                        for j in range(2):
                            dve.wait_ge(o_ps, 2 * t + j + 1)
                            if t >= 1:
                                dve.wait_ge(on_done, 2 * t - 1 + j)
                            dve.reciprocal(o_rec[:, HB * j:HB * (j + 1)], o_view(j)[:, :, HD0]).then_inc(rec_done, 1)
                        if t >= 1:
                            dve.wait_ge(otok_done, t)
                        for j in range(2):
                            dve.wait_ge(rec_done, 2 * t + j + 1)
                            dve.tensor_tensor(o_n[:, :, HB * j:HB * (j + 1)].rearrange("p d n -> p n d"),
                                              o_view(j)[:, :, 0:HD0],
                                              bc(o_rec[:, HB * j:HB * (j + 1)].unsqueeze(2), [P, HB, HD0]),
                                              ALU.mult).then_inc(on_done, 1)
                        dve.wait_ge(on_done, 2 * t + 2)
                        if t >= 1:
                            dve.wait_ge(og_done, t)
                        dve.transpose(o_tok[:, :].rearrange("p (h d) -> p d h", d=HD0), o_n[:, :, :]).then_inc(otok_done, 1)

                    for t in range(TILES + 3):
                        if 1 <= t <= TILES:
                            v_turn(t - 1)
                        if t >= 3:
                            finish(t - 3)
                        if t >= 4:
                            dve.wait_ge(x1_done, t - 3)
                            tile_stats(dve, t - 4)
                        if t + 1 < TILES:
                            nrm.dve_xn(dve, t + 1)
                        if 1 <= t <= TILES:
                            softmax(t - 1, 0)
                        if t < TILES:
                            q_turn(t)
                        if 1 <= t <= TILES:
                            softmax(t - 1, 1)
                        if t + 1 < TILES:
                            nrm.dve_lo(dve, t + 1)
                        if t < TILES:
                            k_turn(t)
                        if 1 <= t <= TILES:
                            turn(t - 1)
                    dve.wait_ge(x1_done, TILES)
                    tile_stats(dve, TILES - 1)

                @block.tensor
                def _(pe):
                    BIG = 3 * 3 * KC
                    PARTS = 6

                    def project(t, i):
                        j, c, term = i // (3 * KC), i // 3 % KC, i % 3
                        ps = (q_ps, k_ps, v_ps)[j]
                        if i == 0:
                            pe.wait_ge(nrm.lo, t + 1)
                        if i % (3 * KC) == 0 and t >= 1:
                            pe.wait_ge(qkv_ev, 3 * t - 2 + j)
                        (h_hi, h_lo), cols = nrm.h(t, c), slice(j * D, (j + 1) * D)
                        x_, w_ = ((h_hi, wq_hi), (h_hi, wq_lo), (h_lo, wq_hi))[term]
                        mm = pe.matmul(ps[:, :], x_, w_[:, c, cols], start=(i % (3 * KC) == 0),
                                       stop=(i % (3 * KC) == 3 * KC - 1))
                        if i % (3 * KC) == 3 * KC - 1:
                            mm.then_inc(qkv_ready, 1)

                    def scores(t, n):
                        if n == 0:
                            pe.wait_ge(qbd_done, t + 1)
                            pe.wait_ge(turned, 3 * t + 2)
                        if n % HB == 0 and t >= 1:
                            pe.wait_ge(sub_done, 2 * t - 1 + n // HB)
                        mm = pe.matmul(s_view(n // HB)[:, n % HB, :], q_bd[:, n, :], kT[:, t % 2, n, :],
                                       start=True, stop=True)
                        if n % HB == HB - 1:
                            mm.then_inc(s_ps, 1)

                    def context(t, n):
                        if n == 0:
                            pe.wait_ge(ebd_done, t + 1)
                            pe.wait_ge(turned, 3 * t + 3)
                        if n % HB == 0 and t >= 1:
                            pe.wait_ge(on_done, 2 * t - 1 + n // HB)
                        mm = pe.matmul(o_view(n // HB)[:, n % HB, :], e_bd[:, n, :], vT[:, t % 3, n, :],
                                       start=True, stop=True)
                        if n % HB == HB - 1:
                            mm.then_inc(o_ps, 1)

                    nrm.pe_xT(pe, 0, pT)
                    for t in range(TILES + 2):
                        for part in range(PARTS):
                            if t < TILES:
                                for i in range(part * BIG // PARTS, (part + 1) * BIG // PARTS):
                                    project(t, i)
                            for n in range(64 * part // PARTS, 64 * (part + 1) // PARTS):
                                if n < 32 and 1 <= t <= TILES:
                                    scores(t - 1, n)
                                if n >= 32 and t >= 2:
                                    context(t - 2, n - 32)
                            if part == 2 and t + 1 < TILES:
                                nrm.pe_xT(pe, t + 1, pT)

        with ExitStack() as ph:
            wmod1 = sb("wmod1", [P, KC, 6 * D], F32, ph)
            wf_hi = sb("wf_hi", [P, KC, PROJ0], F32R, ph)
            wf_lo = sb("wf_lo", [P, KC, PROJ0], F32R, ph)
            we_hi = sb("we_hi", [P, EC, D], F32R, ph)
            we_lo = sb("we_lo", [P, EC, D], F32R, ph)
            biasf = sb("biasf", [P, D], F32, ph)
            iota = sb("iota", [P, E0], F32, ph)
            top = sb("top", [P, 8], F32, ph)
            topi = sb("topi", [P, 8], U32, ph)
            topf = sb("topf", [P, 2], F32, ph)
            rp = sb("rp", [P, E0], F32, ph)
            rm = sb("rm", [P, 1], F32, ph)
            rsum = sb("rsum", [P, 1], F32, ph)
            den = sb("den", [P, 4], F32, ph)
            c1 = sb("c1", [P, E0], F32, ph)
            comb = sb("comb", [P, E0], F32, ph)
            z = sb("z", [P, 2, E0, R0], F32, ph)
            z_hi = sb("z_hi", [P, 2, 512], F32R, ph)
            z_lo = sb("z_lo", [P, 2, 512], F32R, ph)
            f_sum = sb("f_sum", [P, D], F32, ph)
            f_g = sb("f_g", [P, D], F32, ph)
            bias_in = sem("biasf_in")
            chain = sem("router_chain")
            base_ps = sem("base_ps")
            rexp_done = sem("rexp_done")
            rmax_done = sem("rmax_done")
            z_done = sem("z_done")
            zT_ps = sem("zT_ps")
            zhi_done = sem("zhi_done")
            zlo_done = sem("zlo_done")
            f_ps = sem("f_ps")
            fsum_done = sem("fsum_done")
            fg_done = sem("fg_done")
            x2_done = sem("x2_done")
            nrm = Norm("n1", SB, CB, used=base_ps, ctx=ph, used_per=2)
            pT = bank[0]
            y_bank, r_bank, z_bank, m_bank = bank[1:3], bank[3:5], bank[5:7], bank[7]
            parts = ([(raw_f[:, k, :], wf_hi[:, k, :], wf_lo[:, k, :]) for k in range(KC)]
                     + [(raw_e[:, k, :], we_hi[:, k, :], we_lo[:, k, :]) for k in range(EC)])

            with nc.Block() as block:
                @block.sync
                def _(sp):
                    sp.dma_start(biasf[:, :], bc(a["bffn0"], [P, D])).then_inc(bias_in, 16)
                    sp.dma_start(iota[:, :], a["iota"]).then_inc(bias_in, 16)
                    load_wmod(sp, 1, wmod1)
                    sp.wait_ge(split2_lo, KC)
                    sp.dma_start(raw_c, a["wc1"].rearrange("(k p) n -> p k n", p=P)).then_inc(small_in, 16)
                    sp.dma_start(gq, bc(a["gq1"], [P, QR])).then_inc(small_in, 16)
                    sp.dma_start(gk, bc(a["gk1"], [P, KVR])).then_inc(small_in, 16)
                    sp.dma_start(cosk, a["cosk"]).then_inc(small_in, 16)
                    sp.dma_start(sink, a["sink"]).then_inc(small_in, 16)

                @block.gpsimd
                def _(pool):
                    for t in range(TILES):
                        pool.wait_ge(fsum_done, t + 1)
                        if t >= 1:
                            pool.wait_ge(x2_done, t)
                        pool.tensor_tensor(f_g[:, :], f_sum[:, :], gate[:, 1, t // TPB, :], ALU.mult).then_inc(fg_done, 1)
                        pool.wait_ge(fg_done, t + 1)
                        pool.tensor_tensor(x[:, t, :], x[:, t, :], f_g[:, :], ALU.add).then_inc(x2_done, 1)

                @block.scalar
                def _(act):
                    nrm.act_std(act)
                    act.wait_ge(ffn_in, 48)
                    for raw, hi, lo in parts[:KC]:
                        act.activation(hi, raw, ACT.Copy).then_inc(split2_hi, 1)
                    nrm.act_h(act, 0, pT)
                    for raw, hi, lo in parts[KC:]:
                        act.activation(hi, raw, ACT.Copy).then_inc(split2_hi, 1)
                    for t in range(TILES + 1):
                        if t >= 1:
                            for j in range(2):
                                n = 2 * (t - 1) + j
                                act.wait_ge(zT_ps, n + 1)
                                if n >= 2:
                                    act.wait_ge(f_ps, n - 1)
                                act.activation(z_hi[:, j, :], z_bank[j][:, :], ACT.Copy).then_inc(zhi_done, 1)
                        if t + 1 < TILES:
                            nrm.act_h(act, t + 1, pT)
                        if t < TILES:
                            act.wait_ge(rmax_done, t + 1)
                            if t >= 1:
                                act.wait_ge(z_done, t)
                            act.activation(rp[:, :], r_bank[t % 2][:, R0:R0 + E0], ACT.Exp, bias=rm[:, 0:1],
                                           accum_out=rsum[:, 0:1]).then_inc(rexp_done, 1)
                        if 1 <= t <= 6:
                            act.wait_ge(split2_lo, KC + EC)
                            act_rows(act, 1, t - 1, m_bank)

                @block.vector
                def _(dve):
                    nrm.dve_stats(dve)
                    nrm.dve_xn(dve, 0)
                    nrm.dve_xn(dve, 1)
                    for i, (raw, hi, lo) in enumerate(parts):
                        if i == KC:
                            nrm.dve_lo(dve, 0)
                        dve.wait_ge(split2_hi, i + 1)
                        dve.tensor_tensor(lo, raw, hi.bitcast(F32), ALU.subtract).then_inc(split2_lo, 1)
                    dve.wait_ge(bias_in, 32)
                    link = Chain(dve, chain)

                    def route(t):
                        rb = r_bank[t % 2]
                        dve.wait_ge(base_ps, 2 * t + 1)
                        dve.tensor_reduce(rm[:, :], rb[:, R0:R0 + E0], AX.X, ALU.max, negate=True).then_inc(rmax_done, 1)
                        dve.wait_ge(rexp_done, t + 1)
                        link(dve.max(top[:, :], rp[:, :]))
                        dve.tensor_scalar(den[:, 0:1], rsum[:, :], 1e-6, None, ALU.mult)
                        dve.tensor_tensor(den[:, 1:2], top[:, 0:1], top[:, 1:2], ALU.add)
                        link(dve.max_index(topi[:, :], top[:, :], rp[:, :]))
                        dve.tensor_tensor(den[:, 2:3], den[:, 0:1], den[:, 1:2], ALU.add)
                        link(dve.tensor_copy(topf[:, :], topi[:, 0:2]))
                        link(dve.reciprocal(den[:, 3:4], den[:, 2:3]))
                        link(dve.tensor_scalar(top[:, 0:2], top[:, 0:2], den[:, 3:4], LORA_SCALE, ALU.mult, ALU.mult))
                        dve.tensor_scalar(c1[:, :], iota[:, :], topf[:, 0:1], top[:, 0:1], ALU.is_equal, ALU.mult)
                        link(dve.tensor_scalar(comb[:, :], iota[:, :], topf[:, 1:2], top[:, 1:2], ALU.is_equal, ALU.mult))
                        link(dve.tensor_tensor(comb[:, :], comb[:, :], c1[:, :], ALU.add))
                        if t >= 2:
                            dve.wait_ge(zT_ps, 2 * (t - 1))
                        dve.tensor_tensor(z[:, t % 2, :, :], bc(rb[:, 0:R0].unsqueeze(1), [P, E0, R0]),
                                          bc(comb[:, :].unsqueeze(2), [P, E0, R0]), ALU.mult).then_inc(z_done, 1)

                    for t in range(TILES + 2):
                        if t >= 2:
                            dve.wait_ge(f_ps, 2 * (t - 1))
                            if t >= 3:
                                dve.wait_ge(fg_done, t - 2)
                            dve.tensor_tensor(f_sum[:, :], y_bank[t % 2][:, :], biasf[:, :],
                                              ALU.add).then_inc(fsum_done, 1)
                        if 1 <= t <= TILES:
                            for j in range(2):
                                n = 2 * (t - 1) + j
                                dve.wait_ge(zhi_done, n + 1)
                                if n >= 2:
                                    dve.wait_ge(f_ps, n - 1)
                                dve.tensor_tensor(z_lo[:, j, :], z_bank[j][:, :], z_hi[:, j, :].bitcast(F32),
                                                  ALU.subtract).then_inc(zlo_done, 1)
                        if t + 1 < TILES:
                            nrm.dve_lo(dve, t + 1)
                        if t + 2 < TILES:
                            nrm.dve_xn(dve, t + 2)
                        if t < TILES:
                            route(t)
                        if t >= 3:
                            dve.wait_ge(x2_done, t - 2)
                            tile_stats(dve, t - 3)
                    for t in range(TILES - 1, TILES):
                        dve.wait_ge(x2_done, t + 1)
                        tile_stats(dve, t)

                @block.tensor
                def _(pe):
                    def project(t):
                        pe.wait_ge(nrm.lo, t + 1)
                        if t >= 2:
                            pe.wait_ge(z_done, t - 1)
                        split_matmuls(pe, r_bank[t % 2][:, 0:R0 + E0], [
                            (nrm.h(t, c), (wf_hi[:, c, D:PROJ0], wf_lo[:, c, D:PROJ0]))
                            for c in range(KC)]).then_inc(base_ps, 1)
                        if t >= 2:
                            pe.wait_ge(fsum_done, t - 1)
                        split_matmuls(pe, y_bank[t % 2][:, :], [
                            (nrm.h(t, c), (wf_hi[:, c, 0:D], wf_lo[:, c, 0:D])) for c in range(KC)],
                            last=False).then_inc(base_ps, 1)

                    def turn(t):
                        pe.wait_ge(z_done, t + 1)
                        for j in range(2):
                            if t >= 1:
                                pe.wait_ge(zlo_done, 2 * t - 1 + j)
                            for c in range(4):
                                e = 2 * (4 * j + c)
                                mm = pe.transpose(z_bank[j][:, c * P:(c + 1) * P],
                                                  z[:, t % 2, e:e + 2, :].rearrange("p e r -> p (e r)"), ident[:, :])
                            mm.then_inc(zT_ps, 1)

                    def experts(t):
                        if t == 0:
                            pe.wait_ge(split2_lo, KC + EC)
                        for j in range(2):
                            pe.wait_ge(zlo_done, 2 * t + j + 1)
                            mm = split_matmuls(pe, y_bank[t % 2][:, :], [
                                ((z_hi[:, j, c * P:(c + 1) * P], z_lo[:, j, c * P:(c + 1) * P]),
                                 (we_hi[:, 4 * j + c, :], we_lo[:, 4 * j + c, :])) for c in range(4)],
                                first=False, last=(j == 1))
                            mm.then_inc(f_ps, 1)

                    nrm.pe_xT(pe, 0, pT)
                    pe.wait_ge(split2_lo, KC)
                    for t in range(TILES + 1):
                        if t >= 1:
                            turn(t - 1)
                        if t + 1 < TILES:
                            nrm.pe_xT(pe, t + 1, pT)
                        if t < TILES:
                            project(t)
                        if t >= 1:
                            experts(t - 1)
                        if 1 <= t <= 6:
                            if t >= 2:
                                pe.wait_ge(row_ev, 6 + t - 1)
                            pe_rows(pe, 1, t - 1, wmod1, m_bank)


        with ExitStack() as ph:
            wq_all = sb("wq_all", [P, NH, 2, P], F32, ph)
            wb_all = sb("wb_all", [P, HP, D], F32, ph)
            xk_hi = sb("xk_hi", [P, 3, TOK], F32R, ph)
            xk_lo = sb("xk_lo", [P, 2, TOK], F32R, ph)
            c_hi = sb("c_hi", [P, TILES, 3 * KVR], F32R, ph)
            c_mix = sb("c_mix", [P, TILES, 3 * KVR], F32R, ph)
            cosq, sinq = stage_flat[:, 2 * D + 2 * S:2 * D + 3 * S], stage_flat[:, 2 * D + 3 * S:2 * D + 4 * S]
            rot_in = sem("rot_in")

            with ExitStack() as pr:
                HPC = 4
                wc_hi = sb("wc_hi", [P, KC, CQ], F32R, pr)
                wc_lo = sb("wc_lo", [P, KC, CQ], F32R, pr)
                wqn = sb("wqn", [P, 2, HPC, 2 * P], F32, pr)
                wkn = sb("wkn", [P, NH, KVR], F32, pr)
                wvn = sb("wvn", [P, NH, KVR], F32, pr)
                wo = raw_e[:, :, :].rearrange("p (s h) n -> p s h n", s=2)
                sq = sb("sq", [P, QR], F32, pr)
                ssq = sb("ssq", [P, 2, 2], F32, pr)
                rms = sb("rms", [P, 2, 2], F32, pr)
                qn = sb("qn", [P, 2, 2 * P], F32, pr)
                kk = sb("kk", [P, 2, P], F32, pr)
                ra = sb("ra", [P, RD], F32, pr)
                rb = sb("rb", [P, RD], F32, pr)
                heads_in = sem("heads_in")
                wqn_in = [sem("wqn_in0"), sem("wqn_in1")]
                wo_in = [sem("wo_in0"), sem("wo_in1")]
                ab_ps = sem("ab_ps")
                ab_ev = sem("ab_ev")
                c_ps = sem("c_ps")
                sq_done = sem("sq_done")
                ssq_done = sem("ssq_done")
                rms_done = sem("rms_done")
                c_set = sem("c_set")
                chain = sem("rms_chain")
                kk_done = sem("kk_done")
                xkT_ps = sem("xkT_ps")
                xkhi_done = sem("xkhi_done")
                xklo_done = sem("xklo_done")
                nrm = Norm("n2", SA, CA, used=c_ps, ctx=pr)
                pT, c_bank, k_bank = bank[0], bank[1:3], bank[3:5]
                a_bank, b_bank = bank[5], bank[6:8]
                wc_base = KC + EC
                GROUPS = NH // HPC
                STEPS = 1 + HPC // 2

                def act_start(act):
                    nrm.act_std(act)
                    act.wait_ge(small_in, 80)
                    for k in range(KC):
                        act.activation(wc_hi[:, k, :], raw_c[:, k, :], ACT.Copy).then_inc(split2_hi, 1)

                def dve_start(dve):
                    nrm.dve_stats(dve)
                    nrm.dve_xn(dve, 0)
                    nrm.dve_xn(dve, 1)

                def dve_later(dve):
                    for k in range(KC):
                        dve.wait_ge(split2_hi, wc_base + k + 1)
                        dve.tensor_tensor(wc_lo[:, k, :], raw_c[:, k, :], wc_hi[:, k, :].bitcast(F32),
                                          ALU.subtract).then_inc(split2_lo, 1)

                def load_heads(sp):
                    sp.dma_start(wkn[:, :, :], a["wkn1"]).then_inc(heads_in, 16)
                    sp.dma_start(wvn[:, :, :], a["wvn1"]).then_inc(heads_in, 16)

                modulation(1, extra_sp=load_heads, extra_act=act_start, extra_dve=dve_start, late_dve=dve_later)

                with nc.Block() as block:
                    @block.sync
                    def _(sp):
                        for g in range(GROUPS):
                            if g >= 2:
                                sp.wait_ge(ab_ps, STEPS * (g - 1))
                            hs = slice(g * HPC, (g + 1) * HPC)
                            sp.dma_start(wqn[:, g % 2, :, :], a["wqn1"][hs].rearrange("h n m -> n h m")).then_inc(wqn_in[g % 2], 16)
                            sp.dma_start(wo[:, g % 2, :, :],
                                         a["wo1"].rearrange("(h v) n -> v h n", v=VD)[:, hs, :]).then_inc(wo_in[g % 2], 16)
                        for c in range(2):
                            sp.dma_start(wq_all[:, :, c, KVR:P], a["wqr1"][:, c]).then_inc(rot_in, 16)
                        sp.dma_start(cosq, a["cosq"]).then_inc(rot_in, 16)
                        sp.dma_start(sinq, a["sinq"]).then_inc(rot_in, 16)
                        sp.wait_ge(rot_in, 64)

                    @block.scalar
                    def _(act):
                        def heads(g):
                            act.wait_ge(ab_ps, STEPS * g + 1)
                            act.activation(wq_all[:, g * HPC:(g + 1) * HPC, :, 0:KVR],
                                           a_bank[:, :].rearrange("p (h c n) -> p h c n", h=HPC, c=2),
                                           ACT.Copy).then_inc(ab_ev, 1)
                            for q in range(HPC // 2):
                                act.wait_ge(ab_ps, STEPS * g + q + 2)
                                act.activation(wb_all[:, g * HPC // 2 + q, :], b_bank[q % 2][:, :],
                                               ACT.Copy).then_inc(ab_ev, 1)

                        nrm.act_h(act, 0, pT)
                        for t in range(TILES + 2):
                            if t >= 2:
                                heads(t - 2)
                            if t + 1 < TILES:
                                nrm.act_h(act, t + 1, pT)
                            if t < TILES:
                                act.wait_ge(c_ps, t + 1)
                                if t >= 1:
                                    act.wait_ge(sq_done, 2 * t)
                                if t >= 2:
                                    act.wait_ge(rms_done, t - 1)
                                cb = c_bank[t % 2]
                                act.activation(sq[:, 0:QR], cb[:, 0:QR], ACT.Square,
                                               accum_out=ssq[:, t % 2, 0:1]).then_inc(sq_done, 1)
                                act.wait_ge(sq_done, 2 * t + 1)
                                act.activation(sq[:, 0:KVR], cb[:, QR:QR + KVR], ACT.Square,
                                               accum_out=ssq[:, t % 2, 1:2]).then_inc(sq_done, 1)
                                act.wait_ge(sq_done, 2 * t + 2)
                                act.activation(rms[:, t % 2, 0:1], ssq[:, t % 2, 0:1], ACT.Sqrt,
                                               scale=1.0 / QR).then_inc(ssq_done, 1)
                                act.activation(rms[:, t % 2, 1:2], ssq[:, t % 2, 1:2], ACT.Sqrt,
                                               scale=1.0 / KVR).then_inc(ssq_done, 1)
                            if 1 <= t <= TILES:
                                act.wait_ge(xkT_ps, t)
                                ts = slice((t - 1) * P, t * P)
                                act.activation(xk_hi[:, :, ts],
                                               k_bank[(t - 1) % 2][:, 0:3 * P].rearrange("p (c n) -> p c n", c=3),
                                               ACT.Copy).then_inc(xkhi_done, 1)
                    @block.vector
                    def _(dve):
                        dve.memset(c_hi[:, :, :].bitcast(F32), 0.0).then_inc(c_set, 1)
                        dve.wait_ge(c_set, 1)
                        nrm.dve_lo(dve, 0)
                        link = Chain(dve, chain)
                        for t in range(TILES + 1):
                            if t + 1 < TILES:
                                nrm.dve_lo(dve, t + 1)
                            if t + 2 < TILES:
                                nrm.dve_xn(dve, t + 2)
                            if t < TILES:
                                cb, s2 = c_bank[t % 2], t % 2
                                r0, r1 = rms[:, s2, 0:1], rms[:, s2, 1:2]
                                dve.wait_ge(ssq_done, 2 * t + 2)
                                link(dve.tensor_scalar_add(rms[:, s2, :], rms[:, s2, :], RMS_EPS))
                                link(dve.reciprocal(rms[:, s2, :], rms[:, s2, :]))
                                dve.tensor_tensor(ra[:, :], cb[:, QR + KVR:CQ], cosk[:, t % TPB, :], ALU.mult)
                                dve.tensor_tensor(rb[:, 0:32], cb[:, CQ - 32:CQ], sink[:, t % TPB, 32:RD], ALU.mult)
                                link(dve.tensor_tensor(rb[:, 32:RD], cb[:, QR + KVR:CQ - 32], sink[:, t % TPB, 0:32], ALU.mult))
                                if t >= 2:
                                    dve.wait_ge(xkT_ps, t - 1)
                                dve.scalar_tensor_tensor(qn[:, s2, 0:QR], cb[:, 0:QR], r0, gq[:, :], ALU.mult, ALU.mult)
                                dve.scalar_tensor_tensor(qn[:, s2, QR:2 * P], cb[:, P:QR], r0, gq[:, P:QR], ALU.mult, ALU.mult)
                                link(dve.scalar_tensor_tensor(kk[:, s2, 0:KVR], cb[:, QR:QR + KVR], r1, gk[:, :],
                                                              ALU.mult, ALU.mult))
                                link(dve.tensor_copy(c_hi[:, t, KVR:2 * KVR], kk[:, s2, 0:KVR]))
                                dve.tensor_copy(c_mix[:, t, KVR:2 * KVR], kk[:, s2, 0:KVR])
                                for w in (slice(0, KVR), slice(2 * KVR, 3 * KVR)):
                                    dve.tensor_tensor(c_mix[:, t, w], kk[:, s2, 0:KVR],
                                                      c_hi[:, t, KVR:2 * KVR].bitcast(F32), ALU.subtract)
                                dve.tensor_tensor(kk[:, s2, KVR:P], ra[:, :], rb[:, :], ALU.add).then_inc(kk_done, 1)
                                dve.wait_ge(kk_done, t + 1)
                                dve.tensor_scalar_add(ssq[:, s2, :], ssq[:, s2, :], 0.0).then_inc(rms_done, 1)
                            if t >= 1:
                                kb = k_bank[(t - 1) % 2]
                                ts = slice((t - 1) * P, t * P)
                                dve.wait_ge(xkhi_done, t)
                                dve.tensor_tensor(xk_lo[:, :, ts],
                                                  kb[:, 0:3 * P].rearrange("p (c n) -> p c n", c=3)[:, 0:3:2, :],
                                                  xk_hi[:, 0:3:2, ts].bitcast(F32), ALU.subtract)
                                dve.tensor_tensor(xk_hi[QREST:P, 1, ts], kb[QREST:P, P:2 * P],
                                                  xk_hi[QREST:P, 1, ts].bitcast(F32), ALU.subtract).then_inc(xklo_done, 1)

                    @block.tensor
                    def _(pe):
                        def turn(t):
                            pe.wait_ge(kk_done, t + 1)
                            if t >= 2:
                                pe.wait_ge(xklo_done, t - 1)
                            kb = k_bank[t % 2]
                            pe.transpose(kb[:, 0:P], qn[:, t % 2, 0:P], ident[:, :])
                            pe.transpose(kb[:, P:2 * P], qn[:, t % 2, P:2 * P], ident[:, :])
                            pe.transpose(kb[:, 2 * P:3 * P], kk[:, t % 2, :], ident[:, :]).then_inc(xkT_ps, 1)

                        def heads(g):
                            pe.wait_ge(wqn_in[g % 2], 16 * (g // 2 + 1))
                            if g >= 1:
                                pe.wait_ge(ab_ev, STEPS * (g - 1) + 1)
                            for q in range(HPC):
                                for c in range(2):
                                    mm = pe.matmul(a_bank[:, (2 * q + c) * KVR:(2 * q + c + 1) * KVR],
                                                   wqn[:, g % 2, q, c * P:(c + 1) * P], wkn[:, g * HPC + q, :],
                                                   start=True, stop=True)
                            mm.then_inc(ab_ps, 1)
                            pe.wait_ge(wo_in[g % 2], 16 * (g // 2 + 1))
                            for q in range(HPC // 2):
                                if g >= 1:
                                    pe.wait_ge(ab_ev, STEPS * (g - 1) + q + 2)
                                for e in range(2):
                                    mm = pe.matmul(b_bank[q % 2][e * KVR:(e + 1) * KVR, :], wvn[:, g * HPC + 2 * q + e, :],
                                                   wo[:, g % 2, 2 * q + e, :], start=True, stop=True)
                                mm.then_inc(ab_ps, 1)

                        nrm.pe_xT(pe, 0, pT)
                        pe.wait_ge(split2_lo, wc_base + KC)
                        for t in range(TILES + 1):
                            if t + 1 < TILES:
                                nrm.pe_xT(pe, t + 1, pT)
                            if t < TILES:
                                pe.wait_ge(nrm.lo, t + 1)
                                if t >= 2:
                                    pe.wait_ge(rms_done, t - 1)
                                split_matmuls(pe, c_bank[t % 2][:, 0:CQ], [
                                    (nrm.h(t, c), (wc_hi[:, c, :], wc_lo[:, c, :])) for c in range(KC)]).then_inc(c_ps, 1)
                            if t == 1:
                                pe.wait_ge(heads_in, 32)
                            if t >= 1:
                                heads(t - 1)
                                turn(t - 1)

            w_hi = sb("w_hi", [P, 2, 2, P], F32R, ph)
            w_lo = sb("w_lo", [P, 2, 2, P], F32R, ph)
            b_hi = sb("b_hi", [P, D], F32R, ph)
            b_lo = sb("b_lo", [P, D], F32R, ph)
            o_tmp = stage_flat[:, 0:2 * D].rearrange("p (s n) -> p s n", s=2)
            qf, qu = stage_flat[:, 2 * D:2 * D + S], stage_flat[:, 2 * D + S:2 * D + 2 * S]
            q_hi = sb("q_hi", [P, 2, S], F32R, ph)
            q_lo = sb("q_lo", [P, 2, S], F32R, ph)
            nmax = sb("nmax", [P, 2, TPB], F32, ph)
            rsum = sb("rsum1", [P, 2, TPB], F32, ph)
            rinv = sb("rinv", [P, 2, TPB], F32, ph)
            prob = sb("prob", [P, 2, TPB, S], F32, ph)
            pT_hi = sb("pT_hi", [P, TPB, S], F32R, ph)
            pT_lo = sb("pT_lo", [P, TPB, S], F32R, ph)
            ct_r = sb("ct_r", [P, S], F32, ph)
            ct_f = sb("ct_f", [P, S], F32, ph)
            cT_hi = sb("cT_hi", [P, S], F32R, ph)
            cT_lo = sb("cT_lo", [P, S], F32R, ph)
            acc = raw_e
            whi_done = sem("whi_done")
            wlo_done = sem("wlo_done")
            bhi_done = sem("bhi_done")
            blo_done = sem("blo_done")
            q_ps = sem("q1_ps")
            qrot = sem("qrot")
            qsum = sem("qsum")
            qhi_done = sem("qhi_done")
            qlo_done = sem("qlo_done")
            s_ps = sem("s1_ps")
            max_done = sem("max1_done")
            exp_done = sem("exp1_done")
            rinv_done = sem("rinv_done")
            norm_dve = sem("norm_dve")
            norm_pool = sem("norm_pool")
            norm_act = sem("norm_act")
            pT_ps = sem("pT_ps")
            phi_done = sem("phi_done")
            plo_done = sem("plo_done")
            pv_ps = sem("pv_ps")
            chi_done = sem("chi_done")
            crest_done = sem("crest_done")
            csum_done = sem("csum_done")
            clo_done = sem("clo_done")
            o_ps = sem("o1_ps")
            o_ev = sem("o1_ev")
            acc_done = sem("acc_done")
            acc_set = sem("acc_set")
            s_bank, t_bank = bank[0:2], bank[2:4]
            q_bank, ct_bank, o_bank = bank[4], bank[5:7], bank[7]
            UNITS = 4 * HP
            OUT_STEPS = ((0, 2), (0, 3), (1, 1), (1, 3))
            ACT_STEP = 1
            POOL_STEP = 2

            def ge(eng, s_, v):
                if not (isinstance(v, int) and v <= 0):
                    eng.wait_ge(s_, v)

            def pairs(eng, unit):
                for p in (0, 1):
                    for c in range(4):
                        unit(p, c, False)
                with eng.Fori(2, HP - 1) as p:
                    for c in range(4):
                        unit(p, c, True)
                for p in (HP - 1, HP):
                    for c in range(4):
                        unit(p, c, False)

            def out_step(p, c, st, steady):
                if (c % 2, st) not in OUT_STEPS:
                    return None
                n, m = OUT_STEPS.index((c % 2, st)), p * 2 + (c // 2 - 2)
                if not steady and not 0 <= m < 2 * HP:
                    return None
                return m, n

            with nc.Block() as block:
                @block.tensor
                def _(pe):
                    def project(i, c, pair):
                        b, e = (c // 2) % 2, c % 2
                        ts = slice(b * S, (b + 1) * S)
                        if c == 0:
                            pe.wait_ge(wlo_done, pair + 1)
                        ge(pe, qrot, 3 * i)
                        pe.matmul(q_bank[:, :], w_hi[:, e, 0, :], xk_hi[:, 0, ts], start=True, stop=False)
                        pe.matmul(q_bank[:, :], w_hi[:, e, 0, :], xk_lo[:, 0, ts], start=False, stop=False)
                        pe.matmul(q_bank[:, :], w_lo[:, e, 0, :], xk_hi[:, 0, ts], start=False, stop=False)
                        pe.matmul(q_bank[:, :], w_hi[:, e, 1, :], xk_hi[:, 1, ts], start=False, stop=False)
                        pe.matmul(q_bank[:, :], w_lo[:, e, 1, :], xk_hi[:, 1, ts], start=False, stop=True).then_inc(q_ps, 1)

                    def context(g, c, tt):
                        e, b = c % 2, c // 2
                        w = slice(KVR, 3 * KVR) if e == 0 else slice(0, 2 * KVR)
                        ct = ct_bank[e][:, :]
                        ge(pe, plo_done, g + 1)
                        k = b * TPB + tt
                        pe.matmul(ct, c_mix[:, k, w], pT_hi[:, tt, :], start=(tt == 0), stop=False)
                        pe.matmul(ct, c_hi[:, k, w], pT_lo[:, tt, :], start=False,
                                  stop=(tt == TPB - 1)).then_inc(pv_ps, 1)

                    def unit(p, c, steady):
                        i = p * 4 + c
                        b = c // 2
                        for st in range(TPB):
                            if steady or i < UNITS:
                                if st == 0:
                                    ge(pe, qlo_done, i + 1)
                                ge(pe, exp_done, i * 4 + (st - 1))
                                q = slice(st * P, (st + 1) * P)
                                sbk, ks = s_bank[st % 2][:, :], slice(b * S, (b + 1) * S)
                                pe.matmul(sbk, q_hi[:, c % 2, q], xk_hi[:, 2, ks], start=True, stop=False)
                                pe.matmul(sbk, q_hi[:, c % 2, q], xk_lo[:, 1, ks], start=False, stop=False)
                                pe.matmul(sbk, q_lo[:, c % 2, q], xk_hi[:, 2, ks], start=False, stop=True).then_inc(s_ps, 1)
                            if steady or 5 <= 4 * i + st < 4 * UNITS + 5:
                                ts, slot = (st - 1) % TPB, (c - 1) % 2 if st else c % 2
                                if ts == 0:
                                    ge(pe, norm_dve, i * 2)
                                    ge(pe, norm_act, i)
                                    ge(pe, norm_pool, i)
                                ge(pe, plo_done, i * 4 + (st - 6))
                                for n in range(TPB):
                                    mm = pe.transpose(t_bank[ts % 2][:, n * P:(n + 1) * P],
                                                      prob[:, slot, n, ts * P:(ts + 1) * P], ident[:, :])
                                mm.then_inc(pT_ps, 1)
                            if st == 0 and (steady or i + 2 < UNITS):
                                project(i + 2, (c + 2) % 4, p + (c + 2) // 4)
                            if steady or 7 <= 4 * i + st < 4 * UNITS + 7:
                                cc = (c - 1) % 4 if st >= 3 else (c - 2) % 4
                                if st == 3:
                                    ge(pe, csum_done, i - 2)
                                context(i * 4 + (st - 7), cc, (st - 3) % TPB)
                            if (o := out_step(p, c, st, steady)) is not None:
                                m, n = o
                                if n == 0:
                                    ge(pe, clo_done, m + 1)
                                    if c == 0:
                                        ge(pe, blo_done, p)
                                ge(pe, o_ev, m * 4 + n)
                                ts = slice(n * P, (n + 1) * P)
                                pe.matmul(o_bank[:, :], cT_hi[:, ts], b_hi[:, :], start=True, stop=False)
                                pe.matmul(o_bank[:, :], cT_hi[:, ts], b_lo[:, :], start=False, stop=False)
                                pe.matmul(o_bank[:, :], cT_lo[:, ts], b_hi[:, :], start=False, stop=True).then_inc(o_ps, 1)

                    project(0, 0, 0)
                    project(1, 1, 0)
                    pairs(pe, unit)

                @block.vector
                def _(dve):
                    def rotate(i, part):
                        lo, hi = slice(KVR, KVR + 32), slice(KVR + 32, P)
                        if part == 0:
                            ge(dve, q_ps, i + 1)
                            ge(dve, qsum, i)
                            dve.tensor_tensor(qu[lo, :], q_bank[hi, :], sinq[hi, :], ALU.mult).then_inc(qrot, 1)
                        elif part == 1:
                            dve.tensor_tensor(qu[hi, :], q_bank[lo, :], sinq[lo, :], ALU.mult).then_inc(qrot, 1)
                        else:
                            ge(dve, qlo_done, i)
                            dve.tensor_tensor(qf[:, :], q_bank[:, :], cosq[:, :], ALU.mult).then_inc(qrot, 1)

                    def normalize(p, i, c, st):
                        ge(dve, exp_done, i * 4 + (st + 1))
                        if st == POOL_STEP:
                            ge(dve, norm_pool, i - 1)
                        if st == ACT_STEP:
                            ge(dve, norm_act, i - 1)
                        r = rinv[:, c % 2, st:st + 1]
                        dve.reciprocal(r, rsum[:, c % 2, st:st + 1]).then_inc(rinv_done, 1)
                        if st not in (ACT_STEP, POOL_STEP):
                            ge(dve, rinv_done, i * 4 + (st + 1))
                            dve.tensor_scalar(prob[:, c % 2, st, :], prob[:, c % 2, st, :], r, None,
                                              ALU.mult).then_inc(norm_dve, 1)

                    def unit(p, c, steady):
                        i = p * 4 + c
                        for st in range(TPB):
                            g = i * 4 + st
                            if steady or i < UNITS:
                                ge(dve, s_ps, i * 4 + (st + 1))
                                if st == 0:
                                    ge(dve, exp_done, (i - 1) * 4)
                                dve.tensor_reduce(nmax[:, c % 2, st:st + 1], s_bank[st % 2][:, :], AX.X, ALU.max,
                                                  negate=True).then_inc(max_done, 1)
                            if steady or 6 <= g < 4 * UNITS + 6:
                                ts = (st - 2) % TPB
                                ge(dve, phi_done, i * 4 + (st - 5))
                                ge(dve, pv_ps, i * 4 + (st - 9))
                                dve.tensor_tensor(pT_lo[:, ts, :], t_bank[ts % 2][:, :],
                                                  pT_hi[:, ts, :].bitcast(F32), ALU.subtract).then_inc(plo_done, 1)
                            if st and (steady or i < UNITS):
                                normalize(p, i, c, st - 1)
                            if not st and (steady or 1 <= i <= UNITS):
                                normalize(p, i - 1, (c - 1) % 4, TPB - 1)
                            if st and (steady or i + 2 < UNITS):
                                rotate(i + 2, st - 1)
                            if st == 0 and (steady or 3 <= i < UNITS + 3):
                                e = (c + 1) % 2
                                main = slice(e * KVR, (e + 1) * KVR)
                                ge(dve, crest_done, i - 2)
                                ge(dve, clo_done, p * 2 + (c // 2 - 2 + c % 2))
                                dve.tensor_tensor(ct_f[main, :], ct_bank[e][main, :], ct_r[main, :],
                                                  ALU.add).then_inc(csum_done, 1)
                            if (c % 2, st) == (0, 1) and (steady or 0 <= 2 * p + c // 2 - 2 < 2 * HP):
                                m = p * 2 + (c // 2 - 2)
                                ge(dve, chi_done, m + 1)
                                dve.tensor_tensor(cT_lo[:, :], ct_f[:, :], cT_hi[:, :].bitcast(F32),
                                                  ALU.subtract).then_inc(clo_done, 1)

                    dve.wait_ge(acc_set, 1)
                    for i in (0, 1):
                        for part in range(3):
                            rotate(i, part)
                    pairs(dve, unit)

                @block.scalar
                def _(act):
                    def weights(p):
                        ge(act, q_ps, p * 4)
                        act.activation(w_hi[:, :, :, :], wq_all[:, bass.ds(p * 2, 2), :, :], ACT.Copy).then_inc(whi_done, 1)

                    def p_round(i, st, steady):
                        if steady or 5 <= 4 * i + st < 4 * UNITS + 5:
                            ts = (st - 1) % TPB
                            ge(act, pT_ps, i * 4 + (st - 4))
                            ge(act, pv_ps, i * 4 + (st - 8))
                            act.activation(pT_hi[:, ts, :], t_bank[ts % 2][:, :], ACT.Copy).then_inc(phi_done, 1)

                    def q_round(i, c):
                        ge(act, qsum, i + 1)
                        ge(act, s_ps, (i - 1) * 4)
                        act.activation(q_hi[:, c % 2, :], qf[:, :], ACT.Copy).then_inc(qhi_done, 1)

                    def unit(p, c, steady):
                        i = p * 4 + c
                        for st in range(TPB):
                            if st:
                                p_round(i, st, steady)
                            if steady or i < UNITS:
                                ge(act, max_done, i * 4 + (st + 1))
                                if st == 0:
                                    ge(act, pT_ps, (i - 1) * 4)
                                    ge(act, rinv_done, (i - 1) * 4)
                                act.activation(prob[:, c % 2, st, :], s_bank[st % 2][:, :], ACT.Exp,
                                               bias=nmax[:, c % 2, st:st + 1],
                                               accum_out=rsum[:, c % 2, st:st + 1]).then_inc(exp_done, 1)
                            if not st:
                                p_round(i, st, steady)
                            if st == 3 and (steady or 0 <= i - 2 < UNITS):
                                main, rest = (slice(0, KVR), slice(KVR, P))[::1 - c % 2 * 2]
                                ge(act, pv_ps, i * 4 - 4)
                                ge(act, csum_done, i - 2)
                                act.activation(ct_r[main, :], ct_bank[c % 2][rest, :], ACT.Copy).then_inc(crest_done, 1)
                            if (c % 2, st) == (0, 1) and (steady or 0 <= 2 * p + c // 2 - 2 < 2 * HP):
                                m = p * 2 + (c // 2 - 2)
                                ge(act, csum_done, m * 2 + 2)
                                ge(act, o_ps, m * 4)
                                act.activation(cT_hi[:, :], ct_f[:, :], ACT.Copy).then_inc(chi_done, 1)
                            if (o := out_step(p, c, st, steady)) is not None:
                                m, n = o
                                ge(act, o_ps, m * 4 + (n + 1))
                                ge(act, acc_done, m * 4 + (n - 1))
                                act.activation(o_tmp[:, n % 2, :], o_bank[:, :], ACT.Copy).then_inc(o_ev, 1)
                            if st == ACT_STEP + 1 and (steady or i < UNITS):
                                ge(act, rinv_done, i * 4 + st)
                                pr_ = prob[:, c % 2, st - 1, :]
                                act.activation(pr_, pr_, ACT.Copy, scale=rinv[:, c % 2, st - 1:st]).then_inc(norm_act, 1)
                            if st == 0 and (steady or i + 1 < UNITS):
                                q_round(i + 1, c + 1)
                            if (c, st) == (1, 1) and (steady or p + 1 < HP):
                                weights(p + 1)
                            if (c, st) == (0, 0) and (steady or 1 <= p <= HP):
                                ge(act, o_ps, p * 8 - 8)
                                act.activation(b_hi[:, :], wb_all[:, p - 1, :] if not steady else
                                               wb_all[:, bass.ds(p - 1, 1), :].rearrange("p a n -> p (a n)"),
                                               ACT.Copy).then_inc(bhi_done, 1)

                    weights(0)
                    q_round(0, 0)
                    pairs(act, unit)

                @block.gpsimd
                def _(pool):
                    def weights(p):
                        ge(pool, whi_done, p + 1)
                        pool.tensor_tensor(w_lo[:, :, :, :], wq_all[:, bass.ds(p * 2, 2), :, :],
                                           w_hi[:, :, :, :].bitcast(F32), ALU.subtract).then_inc(wlo_done, 1)

                    def q_sum(i):
                        ge(pool, qrot, i * 3 + 3)
                        pool.tensor_tensor(qf[:, :], qf[:, :], qu[:, :], ALU.add).then_inc(qsum, 1)

                    def q_rest(i, c):
                        ge(pool, qhi_done, i + 1)
                        pool.tensor_tensor(q_lo[:, c % 2, :], qf[:, :], q_hi[:, c % 2, :].bitcast(F32),
                                           ALU.subtract).then_inc(qlo_done, 1)

                    def unit(p, c, steady):
                        i = p * 4 + c
                        for st in range(TPB):
                            if st == 0 and (steady or i + 1 < UNITS):
                                q_rest(i + 1, c + 1)
                            if (c, st) == (1, 1) and (steady or p + 1 < HP):
                                weights(p + 1)
                            if (c, st) == (0, 0) and (steady or 1 <= p <= HP):
                                ge(pool, bhi_done, p)
                                pool.tensor_tensor(b_lo[:, :], wb_all[:, p - 1, :] if not steady else
                                                   wb_all[:, bass.ds(p - 1, 1), :].rearrange("p a n -> p (a n)"),
                                                   b_hi[:, :].bitcast(F32), ALU.subtract).then_inc(blo_done, 1)
                            if st == POOL_STEP + 1 and (steady or i < UNITS):
                                ge(pool, rinv_done, i * 4 + st)
                                pr_ = prob[:, c % 2, st - 1, :]
                                pool.tensor_tensor(pr_, pr_, bc(rinv[:, c % 2, st - 1:st], [P, S]),
                                                   ALU.mult).then_inc(norm_pool, 1)
                            if st == 3 and (steady or i + 2 < UNITS):
                                q_sum(i + 2)
                            if (o := out_step(p, c, st, steady)) is not None:
                                m, n = o
                                t = c // 2 * TPB + n
                                ge(pool, o_ev, m * 4 + (n + 1))
                                ge(pool, acc_done, m * 4 + n)
                                pool.tensor_tensor(acc[:, t, :], acc[:, t, :], o_tmp[:, n % 2, :], ALU.add).then_inc(acc_done, 1)

                    pool.memset(qu[:, :], 0.0).then_inc(acc_set, 1)
                    pool.memset(acc[:, :, :], 0.0).then_inc(acc_set, 1)
                    weights(0)
                    q_sum(0)
                    q_rest(0, 0)
                    q_sum(1)
                    pool.wait_ge(acc_set, 2)
                    pairs(pool, unit)


        with ExitStack() as ph:
            DVE_TILES = 5
            w_raw = sb("w_raw", [P, KC, D], F32, ph)
            fa = sb("fa", [R1, D], F32, ph)
            fb = sb("fb", [R1, D], F32, ph)
            w_eff = sb("w_eff", [P, KC, D], F32, ph)
            w_sq = sb("w_sq", [P, KC, D], F32, ph)
            wh = sb("wl_hi", [P, KC, D], F32R, ph)
            wl = sb("wl_lo", [P, KC, D], F32R, ph)
            mag = sb("mag", [P, D], F32, ph)
            norm = sb("norm", [P, D], F32, ph)
            factor = sb("factor", [P, B, D], F32, ph)
            y_g = sb("y_g", [P, 2, D], F32, ph)
            w_in = sem("w_in")
            ba_ps = sem("ba_ps")
            weff_done = sem("weff_done")
            wsq_done = sem("wsq_done")
            whi2_done = sem("whi2_done")
            wlo2_done = sem("wlo2_done")
            norm_ps = sem("norm_ps")
            norm_done = sem("norm_done")
            chain = sem("factor_chain")
            gated = sem("gated")
            x3_done = sem("x3_done")
            y_ps = sem("y_ps")
            yg_done = sem("yg_done")
            x4_done = sem("x4_done")
            nrm = Norm("n3", SB, CB, used=y_ps, ctx=ph)
            pT, y_bank, n_bank, w_bank = bank[0], bank[1:3], bank[3], bank[4:8]

            with nc.Block() as block:
                @block.sync
                def _(sp):
                    sp.dma_start(w_raw[:, :, :], a["wf1"].rearrange("(k p) n -> p k n", p=P)).then_inc(w_in, 16)
                    sp.dma_start(fa[:, :], a["fa1"]).then_inc(w_in, 16)
                    sp.dma_start(fb[:, :], a["fb1"]).then_inc(w_in, 16)
                    sp.dma_start(mag[:, :], bc(a["mag1"], [P, D])).then_inc(w_in, 16)
                    for t in range(TILES):
                        sp.wait_ge(x4_done, t + 1)
                        sp.dma_start(out_dram[:, t, :], x[:, t, :]).then_inc(stored, 16)
                    sp.wait_ge(stored, 16 * TILES)

                @block.gpsimd
                def _(pool):
                    for i, t in enumerate(range(DVE_TILES, TILES)):
                        pool.tensor_tensor(acc[:, t, :], acc[:, t, :], gate[:, 0, t // TPB, :], ALU.mult).then_inc(gated, 1)
                        pool.wait_ge(gated, i + 1)
                        pool.tensor_tensor(x[:, t, :], x[:, t, :], acc[:, t, :], ALU.add).then_inc(x3_done, 1)
                    for t in range(TILES):
                        pool.wait_ge(yg_done, t + 1)
                        pool.tensor_tensor(x[:, t, :], x[:, t, :], y_g[:, t % 2, :], ALU.add).then_inc(x4_done, 1)

                @block.scalar
                def _(act):
                    for k in range(KC):
                        act.wait_ge(weff_done, k + 1)
                        act.activation(w_sq[:, k, :], w_eff[:, k, :], ACT.Square).then_inc(wsq_done, 1)
                        act.activation(wh[:, k, :], w_eff[:, k, :], ACT.Copy).then_inc(whi2_done, 1)
                    nrm.act_std(act)
                    nrm.act_h(act, 0, pT)
                    act.wait_ge(norm_ps, 1)
                    act.activation(norm[:, :], n_bank[:, :], ACT.Sqrt).then_inc(norm_done, 1)
                    for t in range(1, TILES):
                        nrm.act_h(act, t, pT)

                @block.vector
                def _(dve):
                    link = Chain(dve, chain)
                    for t in range(DVE_TILES):
                        link(dve.tensor_tensor(acc[:, t, :], acc[:, t, :], gate[:, 0, t // TPB, :], ALU.mult))
                        link(dve.tensor_tensor(x[:, t, :], x[:, t, :], acc[:, t, :], ALU.add))
                        tile_stats(dve, t)
                    dve.wait_ge(w_in, 64)
                    for k in range(KC):
                        dve.wait_ge(ba_ps, k + 1)
                        dve.tensor_tensor(w_eff[:, k, :], w_bank[k][:, :], w_raw[:, k, :], ALU.add).then_inc(weff_done, 1)
                    for t in range(DVE_TILES, TILES):
                        dve.wait_ge(x3_done, t - DVE_TILES + 1)
                        tile_stats(dve, t)
                    nrm.dve_stats(dve)
                    nrm.dve_xn(dve, 0)
                    nrm.dve_xn(dve, 1)
                    for k in range(KC):
                        dve.wait_ge(whi2_done, k + 1)
                        dve.tensor_tensor(wl[:, k, :], w_eff[:, k, :], wh[:, k, :].bitcast(F32),
                                          ALU.subtract).then_inc(wlo2_done, 1)
                    nrm.dve_lo(dve, 0)
                    dve.wait_ge(norm_done, 1)
                    link(dve.reciprocal(norm[:, :], norm[:, :]))
                    link(dve.tensor_tensor(norm[:, :], norm[:, :], mag[:, :], ALU.mult))
                    for b in range(B):
                        link(dve.tensor_tensor(factor[:, b, :], norm[:, :], gate[:, 1, b, :], ALU.mult))
                    for t in range(TILES):
                        if t + 1 < TILES:
                            nrm.dve_lo(dve, t + 1)
                        if t + 2 < TILES:
                            nrm.dve_xn(dve, t + 2)
                        dve.wait_ge(y_ps, t + 1)
                        if t >= 2:
                            dve.wait_ge(x4_done, t - 1)
                        dve.tensor_tensor(y_g[:, t % 2, :], y_bank[t % 2][:, :], factor[:, t // TPB, :],
                                          ALU.mult).then_inc(yg_done, 1)

                @block.tensor
                def _(pe):
                    pe.wait_ge(w_in, 64)
                    for k in range(KC):
                        pe.matmul(w_bank[k][:, :], fa[:, k * P:(k + 1) * P], fb[:, :],
                                  start=True, stop=True).then_inc(ba_ps, 1)
                    for k in range(KC):
                        pe.wait_ge(wsq_done, k + 1)
                        mm = pe.matmul(n_bank[:, :], ones[:, :], w_sq[:, k, :], start=(k == 0), stop=(k == KC - 1))
                    mm.then_inc(norm_ps, 1)
                    nrm.pe_xT(pe, 0, pT)
                    pe.wait_ge(wlo2_done, KC)
                    for t in range(TILES):
                        if t + 1 < TILES:
                            nrm.pe_xT(pe, t + 1, pT)
                        pe.wait_ge(nrm.lo, t + 1)
                        if t >= 2:
                            pe.wait_ge(yg_done, t - 1)
                        split_matmuls(pe, y_bank[t % 2][:, :], [
                            (nrm.h(t, c), (wh[:, c, :], wl[:, c, :])) for c in range(KC)]).then_inc(y_ps, 1)


def _constants():
    import numpy as np

    inv = (1.0 / 10000.0 ** (np.arange(0, RD, 2, dtype=np.float32) / np.float32(RD))).astype(np.float32)
    ang = np.outer(np.arange(S, dtype=np.float32), inv).astype(np.float32)
    cos, sin = np.cos(ang).astype(np.float32), np.sin(ang).astype(np.float32)
    cosq = np.full((P, S), SCALE1, np.float32)
    sinq = np.zeros((P, S), np.float32)
    cosq[KVR:] = np.concatenate([cos, cos], 1).T * np.float32(SCALE1)
    sinq[KVR:KVR + 32] = sin.T * np.float32(SCALE1)
    sinq[KVR + 32:] = -sin.T * np.float32(SCALE1)
    cosk = np.concatenate([cos, cos], 1).reshape(TPB, P, RD).transpose(1, 0, 2)
    sink = np.concatenate([sin, -sin], 1).reshape(TPB, P, RD).transpose(1, 0, 2)
    return {
        "ident": np.eye(P, dtype=np.float32),
        "iota": np.tile(np.arange(E0, dtype=np.float32), (P, 1)),
        "cosq": cosq, "sinq": sinq,
        "cosk": np.ascontiguousarray(cosk), "sink": np.ascontiguousarray(sink),
    }


def _layout(i):
    import numpy as np

    t = {k: np.asarray(v) for k, v in i.items()}
    wqb = t["L1_attn_w_qb"].reshape(QR, NH, ND + RD)
    wkvb = t["L1_attn_w_kvb"].reshape(KVR, NH, ND + VD)
    nope = wqb[:, :, :ND].transpose(1, 2, 0)
    rope = wqb[:, :, ND:]
    return {
        "x": t["L0_attn_hidden_states"].reshape(TOK, D),
        "c0": t["L0_c"].T, "c1": t["L1_c"].T,
        "wmod0": t["L0_wmod"], "wmod1": t["L1_wmod"],
        "wqkv0": np.concatenate([t["L0_attn_wq"].T, t["L0_attn_wk"].T, t["L0_attn_wv"].T], 1),
        "bqkv0": np.concatenate([t["L0_attn_bq"], t["L0_attn_bk"], t["L0_attn_bv"]])[None],
        "wffn0": np.concatenate([t["L0_ffn_base_w"].T, t["L0_ffn_A"].T, t["L0_ffn_router_w"].T], 1),
        "bffn0": t["L0_ffn_base_b"][None],
        "wexp0": t["L0_ffn_B"].transpose(0, 2, 1).reshape(E0 * R0, D),
        "wc1": np.concatenate([t["L1_attn_w_qa"], t["L1_attn_w_kva"]], 1),
        "gq1": t["L1_attn_g_qa"][None], "gk1": t["L1_attn_g_kva"][None],
        "wqn1": np.concatenate([nope, nope[:, :, P:]], 2),
        "wqr1": np.stack([rope[:P], np.concatenate([rope[P:], rope[P:]], 0)], 1),
        "wkn1": wkvb[:, :, :ND].transpose(2, 1, 0),
        "wvn1": wkvb[:, :, ND:].transpose(2, 1, 0),
        "wo1": t["L1_attn_w_o"],
        "wf1": t["L1_ffn_W"].T, "fa1": t["L1_ffn_lora_A"], "fb1": t["L1_ffn_lora_B"].T,
        "mag1": t["L1_ffn_magnitude"][None],
        **_constants(),
    }


def kernel(**inputs):
    import numpy as _np
    import concourse.bacc as _bacc
    from concourse import mybir as _mybir
    from concourse.bass_utils import run_bass_kernel_spmd as _run

    nc = _bacc.Bacc("TRN2", target_bir_lowering=False, num_devices=1)
    arrays, aps = {}, {}
    for name, v in _layout(inputs).items():
        v = _np.ascontiguousarray(v)
        arrays[f"in_{name}"] = v
        aps[name] = nc.dram_tensor(f"in_{name}", v.shape, _mybir.dt.from_np(v.dtype), kind="ExternalInput").ap()
    out = nc.dram_tensor("out_x", (TOK, D), F32, kind="ExternalOutput").ap()
    megakernel(nc, aps, out)
    r = _run(nc, [arrays], core_ids=[0])
    return r.results[0]["out_x"].reshape(B, S, D)
```
